# Optimizing a Trainium2 kernel written in Bass

```python
import numpy as np
import jax
import jax.numpy as jnp

def _softmax(x, axis=-1):
    return jax.nn.softmax(x, axis=axis)

def _gelu(x):
    return jax.nn.gelu(x, approximate=True)

def _silu(x):
    return jax.nn.silu(x)

def _sigmoid(x):
    return jax.nn.sigmoid(x)

def _layernorm(x, axis=-1, eps=1e-05):
    m = jnp.mean(x, axis=axis, keepdims=True)
    v = jnp.var(x, axis=axis, keepdims=True)
    return (x - m) / jnp.sqrt(v + eps)

def _scatter_add(tgt, idx, src, axis=0):
    return tgt.at[idx].add(src)

def _segment_sum(src, seg, n):
    return jax.ops.segment_sum(src, seg, n)
kernel_name = 'mk_gnn_resnorm_d2_gnn_r32_3607ff'

def setup_inputs(seed: int=0):
    np.random.seed(seed)
    _w = jnp.asarray

    def _rec_inputs():
        import jax
        import jax.numpy as jnp
        _gk = jax.random.key(seed)
        x = -0.000202 + 1 * jax.random.normal(jax.random.fold_in(_gk, 1), (3125, 128), jnp.float32)
        _s = jax.random.randint(jax.random.fold_in(_gk, 2), (50000,), 0, 3125, jnp.int32)
        _d = jax.random.randint(jax.random.fold_in(_gk, 3), (50000,), 0, 3125, jnp.int32)
        _loop = jnp.arange(3125, dtype=jnp.int32)
        src = jnp.concatenate([_s, _d, _loop])
        dst = jnp.concatenate([_d, _s, _loop])
        _o = jnp.argsort(dst, stable=True)
        src = src[_o]
        dst = dst[_o]
        edge_type_8 = jax.random.randint(jax.random.fold_in(_gk, 13), (103125,), 0, 8, jnp.int32)
        edge_weight = jax.random.uniform(jax.random.fold_in(_gk, 14), (103125,), jnp.float32, 0.0, 0.999998)
        return (x, src, dst, edge_type_8, edge_weight)
    x, src, dst, edge_type_8, edge_weight = _rec_inputs()

    def _L0_gnn_setup():
        import jax, jax.numpy as jnp
        import numpy as np
        N = 50000
        E = 12500
        D = 128
        R = 8
        NB = 4
        EPS = 1e-08
        key = jax.random.key(seed)
        ks = jax.random.split(key, 10)
        s = 1.0 / np.sqrt(D).astype(np.float32)
        h = jax.random.normal(ks[0], (N, D), jnp.float32)
        V = jax.random.normal(ks[1], (NB, D, D), jnp.float32) * s
        w_comp = jax.random.normal(ks[2], (R, NB), jnp.float32)
        loop_w = jax.random.normal(ks[3], (D, D), jnp.float32) * s
        bias = jnp.zeros((D,), jnp.float32)
        ffn_w = jax.random.normal(ks[4], (D, D), jnp.float32) * s
        ffn_b = jnp.zeros((D,), jnp.float32)
        ln_g = jnp.ones((D,), jnp.float32)
        ln_b = jnp.zeros((D,), jnp.float32)
        src = jax.random.randint(ks[5], (E,), 0, N, dtype=jnp.int32)
        dst = jax.random.randint(ks[6], (E,), 0, N, dtype=jnp.int32)
        etype = jax.random.randint(ks[7], (E,), 0, R, dtype=jnp.int32)
        norm = jax.random.uniform(ks[8], (E,), jnp.float32)
        return {'h': h, 'V': V, 'w_comp': w_comp, 'loop_w': loop_w, 'bias': bias, 'ffn_w': ffn_w, 'ffn_b': ffn_b, 'ln_g': ln_g, 'ln_b': ln_b, 'norm': norm, 'src': src, 'dst': dst, 'etype': etype}
    _L0_gnn_all = _L0_gnn_setup()
    _L0_gnn_in = {k: v for k, v in _L0_gnn_all.items() if k in ('V', 'w_comp', 'loop_w', 'bias', 'ffn_w', 'ffn_b', 'ln_g', 'ln_b')}
    del _L0_gnn_all

    def _L1_gnn_setup():
        import jax, jax.numpy as jnp
        import numpy as np
        N, E = (50000, 20000)
        D_IN, D_HID, D_OUT, HEADS = (128, 128, 128, 2)

        def _lin_init(k, fan_in, fan_out):
            return jax.random.normal(k, (fan_in, fan_out), jnp.float32) / np.sqrt(fan_in)

        def _transformer_conv(x, src, dst, Wq, bq, Wk, bk, Wv, bv, Ws, bs, heads):
            n = x.shape[0]
            C = Wq.shape[1] // heads
            q = (x @ Wq + bq).reshape(n, heads, C)
            k = (x @ Wk + bk).reshape(n, heads, C)
            v = (x @ Wv + bv).reshape(n, heads, C)
            qi = q[dst]
            kj = k[src]
            vj = v[src]
            alpha = jnp.sum(qi * kj, axis=-1) / np.sqrt(C)
            amax = jax.ops.segment_max(alpha, dst, num_segments=n)
            ex = jnp.exp(alpha - amax[dst])
            denom = jax.ops.segment_sum(ex, dst, num_segments=n)
            a = ex / denom[dst]
            msg = vj * a[..., None]
            out = jax.ops.segment_sum(msg, dst, num_segments=n).reshape(n, heads * C)
            return out + x @ Ws + bs
        key = jax.random.key(seed)
        ks = jax.random.split(key, 20)
        inp = {'x': jax.random.normal(ks[0], (N, D_IN), jnp.float32), 'edge_index': jax.random.randint(ks[1], (2, E), 0, N, dtype=jnp.int32)}
        inp['Wq1'] = _lin_init(ks[2], D_IN, D_HID)
        inp['bq1'] = jnp.zeros((D_HID,), jnp.float32)
        inp['Wk1'] = _lin_init(ks[3], D_IN, D_HID)
        inp['bk1'] = jnp.zeros((D_HID,), jnp.float32)
        inp['Wv1'] = _lin_init(ks[4], D_IN, D_HID)
        inp['bv1'] = jnp.zeros((D_HID,), jnp.float32)
        inp['Ws1'] = _lin_init(ks[5], D_IN, D_HID)
        inp['bs1'] = jnp.zeros((D_HID,), jnp.float32)
        inp['Wq2'] = _lin_init(ks[6], D_HID, D_OUT)
        inp['bq2'] = jnp.zeros((D_OUT,), jnp.float32)
        inp['Wk2'] = _lin_init(ks[7], D_HID, D_OUT)
        inp['bk2'] = jnp.zeros((D_OUT,), jnp.float32)
        inp['Wv2'] = _lin_init(ks[8], D_HID, D_OUT)
        inp['bv2'] = jnp.zeros((D_OUT,), jnp.float32)
        inp['Ws2'] = _lin_init(ks[9], D_HID, D_OUT)
        inp['bs2'] = jnp.zeros((D_OUT,), jnp.float32)
        return inp
    _L1_gnn_all = _L1_gnn_setup()
    _L1_gnn_in = {k: v for k, v in _L1_gnn_all.items() if k in ('Wq1', 'bq1', 'Wk1', 'bk1', 'Wv1', 'bv1', 'Ws1', 'bs1', 'Wq2', 'bq2', 'Wk2', 'bk2', 'Wv2', 'bv2', 'Ws2', 'bs2')}
    del _L1_gnn_all
    return {'x': x, 'src': src, 'dst': dst, 'edge_type_8': edge_type_8, 'edge_weight': edge_weight, 'L0_gnn_V': _L0_gnn_in['V'], 'L0_gnn_w_comp': _L0_gnn_in['w_comp'], 'L0_gnn_loop_w': _L0_gnn_in['loop_w'], 'L0_gnn_bias': _L0_gnn_in['bias'], 'L0_gnn_ffn_w': _L0_gnn_in['ffn_w'], 'L0_gnn_ffn_b': _L0_gnn_in['ffn_b'], 'L0_gnn_ln_g': _L0_gnn_in['ln_g'], 'L0_gnn_ln_b': _L0_gnn_in['ln_b'], 'L1_gnn_Wq1': _L1_gnn_in['Wq1'], 'L1_gnn_bq1': _L1_gnn_in['bq1'], 'L1_gnn_Wk1': _L1_gnn_in['Wk1'], 'L1_gnn_bk1': _L1_gnn_in['bk1'], 'L1_gnn_Wv1': _L1_gnn_in['Wv1'], 'L1_gnn_bv1': _L1_gnn_in['bv1'], 'L1_gnn_Ws1': _L1_gnn_in['Ws1'], 'L1_gnn_bs1': _L1_gnn_in['bs1'], 'L1_gnn_Wq2': _L1_gnn_in['Wq2'], 'L1_gnn_bq2': _L1_gnn_in['bq2'], 'L1_gnn_Wk2': _L1_gnn_in['Wk2'], 'L1_gnn_bk2': _L1_gnn_in['bk2'], 'L1_gnn_Wv2': _L1_gnn_in['Wv2'], 'L1_gnn_bv2': _L1_gnn_in['bv2'], 'L1_gnn_Ws2': _L1_gnn_in['Ws2'], 'L1_gnn_bs2': _L1_gnn_in['bs2']}

def reference(x, src, dst, edge_type_8, edge_weight, L0_gnn_V, L0_gnn_w_comp, L0_gnn_loop_w, L0_gnn_bias, L0_gnn_ffn_w, L0_gnn_ffn_b, L0_gnn_ln_g, L0_gnn_ln_b, L1_gnn_Wq1, L1_gnn_bq1, L1_gnn_Wk1, L1_gnn_bk1, L1_gnn_Wv1, L1_gnn_bv1, L1_gnn_Ws1, L1_gnn_bs1, L1_gnn_Wq2, L1_gnn_bq2, L1_gnn_Wk2, L1_gnn_bk2, L1_gnn_Wv2, L1_gnn_bv2, L1_gnn_Ws2, L1_gnn_bs2):
    import jax
    import jax.numpy as jnp

    def _L0_gnn_ref(h, V, w_comp, loop_w, bias, ffn_w, ffn_b, ln_g, ln_b, norm, src, dst, etype):
        import jax, jax.numpy as jnp
        import numpy as np
        N = 50000
        E = 12500
        D = 128
        R = 8
        NB = 4
        EPS = 1e-08
        n_nodes, d = h.shape
        nb = V.shape[0]
        Hb = jnp.einsum('ni,bio->bno', h, V)
        coef = w_comp[etype]
        m = coef[:, 0][:, None] * Hb[0][src]
        for b in range(1, nb):
            m = m + coef[:, b][:, None] * Hb[b][src]
        m = m * norm[:, None]
        agg = jax.ops.segment_sum(m, dst, num_segments=n_nodes)
        hn = jax.nn.relu(agg + h @ loop_w + bias)
        y = hn @ ffn_w.T + ffn_b + h
        mu = jnp.mean(y, axis=-1, keepdims=True)
        var = jnp.var(y, axis=-1, keepdims=True)
        return (y - mu) / jnp.sqrt(var + EPS) * ln_g + ln_b

    def _L1_gnn_ref(x, edge_index, Wq1, bq1, Wk1, bk1, Wv1, bv1, Ws1, bs1, Wq2, bq2, Wk2, bk2, Wv2, bv2, Ws2, bs2):
        import jax, jax.numpy as jnp
        import numpy as np
        N, E = (50000, 20000)
        D_IN, D_HID, D_OUT, HEADS = (128, 128, 128, 2)

        def _lin_init(k, fan_in, fan_out):
            return jax.random.normal(k, (fan_in, fan_out), jnp.float32) / np.sqrt(fan_in)

        def _transformer_conv(x, src, dst, Wq, bq, Wk, bk, Wv, bv, Ws, bs, heads):
            n = x.shape[0]
            C = Wq.shape[1] // heads
            q = (x @ Wq + bq).reshape(n, heads, C)
            k = (x @ Wk + bk).reshape(n, heads, C)
            v = (x @ Wv + bv).reshape(n, heads, C)
            qi = q[dst]
            kj = k[src]
            vj = v[src]
            alpha = jnp.sum(qi * kj, axis=-1) / np.sqrt(C)
            amax = jax.ops.segment_max(alpha, dst, num_segments=n)
            ex = jnp.exp(alpha - amax[dst])
            denom = jax.ops.segment_sum(ex, dst, num_segments=n)
            a = ex / denom[dst]
            msg = vj * a[..., None]
            out = jax.ops.segment_sum(msg, dst, num_segments=n).reshape(n, heads * C)
            return out + x @ Ws + bs
        src, dst = (edge_index[0], edge_index[1])
        h = _transformer_conv(x, src, dst, Wq1, bq1, Wk1, bk1, Wv1, bv1, Ws1, bs1, HEADS)
        h = jax.nn.relu(h)
        return _transformer_conv(h, src, dst, Wq2, bq2, Wk2, bk2, Wv2, bv2, Ws2, bs2, HEADS)
    edge_index = jnp.stack([src, dst])
    x = _layernorm(x + _L0_gnn_ref(x, L0_gnn_V, L0_gnn_w_comp, L0_gnn_loop_w, L0_gnn_bias, L0_gnn_ffn_w, L0_gnn_ffn_b, L0_gnn_ln_g, L0_gnn_ln_b, edge_weight, src, dst, edge_type_8), axis=-1)
    x = _layernorm(x + _L1_gnn_ref(x, edge_index, L1_gnn_Wq1, L1_gnn_bq1, L1_gnn_Wk1, L1_gnn_bk1, L1_gnn_Wv1, L1_gnn_bv1, L1_gnn_Ws1, L1_gnn_bs1, L1_gnn_Wq2, L1_gnn_bq2, L1_gnn_Wk2, L1_gnn_bk2, L1_gnn_Wv2, L1_gnn_bv2, L1_gnn_Ws2, L1_gnn_bs2), axis=-1)
    return x

_drawn_inputs = setup_inputs


def setup_inputs(seed=0):
    import zlib

    import numpy as np

    out = dict(_drawn_inputs(seed))
    spreads = {'L0_gnn_bias': (0.0, 0.767),
     'L0_gnn_ffn_b': (0.0, 0.56),
     'L0_gnn_ln_g': (1.0, 0.2),
     'L0_gnn_ln_b': (0.0, 0.1),
     'L1_gnn_bq1': (0.0, 0.661),
     'L1_gnn_bk1': (0.0, 0.8),
     'L1_gnn_bv1': (0.0, 0.1),
     'L1_gnn_bs1': (0.0, 0.1),
     'L1_gnn_bq2': (0.0, 0.8),
     'L1_gnn_bk2': (0.0, 0.8),
     'L1_gnn_bv2': (0.0, 0.1),
     'L1_gnn_bs2': (0.0, 0.1)}
    factors = {}
    for name, (base, spread) in spreads.items():
        noise = np.random.default_rng([zlib.crc32(name.encode()), seed]).standard_normal(out[name].shape)
        drawn = base * np.exp(spread * noise) if base else spread * noise
        out[name] = jnp.asarray(drawn.astype(out[name].dtype))
    for name, factor in factors.items():
        out[name] = (out[name] * factor).astype(out[name].dtype)
    return out
```

```python
from contextlib import ExitStack

import concourse.bass as bass
from concourse import mybir

F32 = mybir.dt.float32
BF16 = mybir.dt.bfloat16
I32 = mybir.dt.int32
U32 = mybir.dt.uint32
ALU = mybir.AluOpType
ACT = mybir.ActivationFunctionType
AX = mybir.AxisListType

NODES, EDGES, D = 3125, 103125, 128
RELS, BASES = 8, 4
HEADS, HD = 2, 64
T = 25
R = NODES // T
EC = EDGES // R
SLOTS = 64
COLS = 35
PAD = COLS * 128
PAIRS = 63
CW = 500
CH = 7
FIRST = 5
NEG = -1.0e30
FLOOR = -1.0e29
MAGIC = 12582912.0


def widths():
    return [min(CW, NODES - CW * j) for j in range(CH)]


class Steps:

    def __init__(self, eng, sem, done=0):
        self.eng, self.sem, self.done = eng, sem, done

    def __call__(self, ins):
        ins.then_inc(self.sem, 1)
        self.done = self.done + 1
        self.eng.wait_ge(self.sem, self.done)


def is_int(t):
    return isinstance(t, int)


def inside(t):
    return not is_int(t) or 0 <= t < T


def half(t, par):
    if is_int(t):
        return t // 2
    return (t - par) // 2


def wait(eng, sem, value):
    if not is_int(value) or value > 0:
        eng.wait_ge(sem, value)


def build(nc, a, out, stop_after=None):
    ctx = ExitStack()
    with ctx:
        ctx.enter_context(nc.allow_non_contiguous_dma(reason="small transposed rows"))

        def dram(name, shape, dt):
            return nc.dram_tensor(name, shape, dt, kind="Internal").ap()

        m = {
            "rel_table": dram("rel_table", (RELS * NODES, D), F32),
            "records": dram("records", (EDGES + PAD, 3), F32),
            "sources": dram("sources", (EDGES + PAD, 2), F32),
            "bias": dram("bias", (T, 128, NODES), F32),
        }
        kept = ExitStack()
        with kept:
            def sb(name, shape, dt):
                return kept.enter_context(nc.sbuf_tensor(name, shape, dt))
            m["x"] = sb("x_rows", [R, T, D], F32)
            m["xT"] = sb("xT", [128, NODES], F32)
            m["h"] = sb("h_rows", [R, T, D], F32)
            m["hT"] = sb("hT", [128, NODES], F32)
            m["eye"] = sb("eye", [128, 128], F32)
            m["ones"] = sb("ones", [128, 128], F32)
            m["starts"] = sb("starts", [128, T + 2], F32)
            m["flag"] = sb("flag", [1, 1], I32)
            m["iota"] = sb("iota", [128, 128], F32)
            m["ps"] = [kept.enter_context(nc.psum_tensor(f"ps{i}", [128, 512], F32)) for i in range(8)]
            prepare(nc, a, m)
            message(nc, a, m)
            first_norms(nc, a, m)
            if stop_after == "x1":
                dump(nc, m["x"], out)
                return
            conv(nc, a, m, 1, None)
            if stop_after == "h":
                dump(nc, m["h"], out)
                return
            conv(nc, a, m, 2, out)


def dump(nc, rows, out):
    with nc.semaphore("dumped") as s, nc.Block() as block:
        @block.sync
        def _(sp):
            sp.dma_start(out.rearrange("(t p) f -> p t f", p=R), rows[:, :, :]).then_inc(s, 16)
            sp.wait_ge(s, 16)


def prepare(nc, a, m):
    ctx = ExitStack()
    with ctx:
        def sb(name, shape, dt):
            return ctx.enter_context(nc.sbuf_tensor(name, shape, dt))

        def sem(name):
            return ctx.enter_context(nc.semaphore(name))

        x, xT, eye, ones, ps = m["x"], m["xT"], m["eye"], m["ones"], m["ps"]
        V = sb("V", [128, BASES, D], F32)
        comp = sb("comp", [128, RELS * BASES], F32)
        W = sb("W", [128, RELS, D], F32)
        rows = sb("rel_rows", [R, 2, RELS, D], F32)
        si = sb("src_int", [R, EC], I32)
        di = sb("dst_int", [R, EC], I32)
        dn = sb("dst_next", [R, SLOTS], I32)
        ti = sb("type_int", [R, EC], I32)
        wf = sb("weight", [R, EC], F32)
        sf = sb("src_f", [R, EC], F32)
        df = sb("dst_f", [R, EC + SLOTS], F32)
        tf = sb("type_f", [R, EC], F32)
        cf = sb("chunk_f", [R, EC], F32)
        rec = sb("rec", [R, EC, 3], F32)
        srcs = sb("srcs", [R, EC, 2], F32)
        junk = sb("junk", [R, EC], F32)
        count = sb("count", [R, T + 4], F32)
        sizes = sb("sizes", [1, T], F32)
        large = sb("large", [1, 1], F32)
        bad = sb("bad", [1, 2], F32)
        pad_rec = sb("pad_rec", [128, COLS, 3], F32)
        pad_src = sb("pad_src", [128, COLS, 2], F32)

        x_in, w_in, e_in, n_in = sem("x_in"), sem("w_in"), sem("e_in"), sem("n_in")
        const, dve, sent = sem("const"), sem("dve_p"), sem("sent")
        xt_ps, xt_ok, w_ok = sem("xt_ps"), sem("xt_ok"), sem("w_ok")
        rel_ps, rel_a, rel_v = sem("rel_ps"), sem("rel_a"), sem("rel_v")
        rel_out = [sem("rel_out0"), sem("rel_out1")]
        rec_ok, src_ok, pad_ok, cnt_ok, cnt_ps = sem("rec_ok"), sem("src_ok"), sem("pad_ok"), sem("cnt_ok"), sem("cnt_ps")
        block = ctx.enter_context(nc.Block())
        groups = [(g, min(4, T - g)) for g in range(0, T, 4)]

        @block.sync
        def _(sp):
            sp.dma_start(x[:, :, :], a["x"].rearrange("(t p) f -> p t f", p=R)).then_inc(x_in, 16)
            sp.dma_start(di[:, :], a["dst"].rearrange("(p n) -> p n", n=EC)).then_inc(e_in, 16)
            sp.dma_start(dn[0:R - 1, :], a["dst"].rearrange("(p n) -> p n", n=EC)[1:R, 0:SLOTS]).then_inc(e_in, 16)
            sp.dma_start(V[:, :, :], a["L0_gnn_V"].rearrange("b i o -> i b o")).then_inc(w_in, 16)
            sp.dma_start(comp[:, :], a["L0_gnn_w_comp"].rearrange("r b -> (r b)").partition_broadcast(128)).then_inc(w_in, 16)
            sp.dma_start(si[:, :], a["src"].rearrange("(p n) -> p n", n=EC)).then_inc(n_in, 16)
            sp.dma_start(ti[:, :], a["edge_type_8"].rearrange("(p n) -> p n", n=EC)).then_inc(n_in, 16)
            sp.dma_start(wf[:, :], a["edge_weight"].rearrange("(p n) -> p n", n=EC)).then_inc(n_in, 16)
            sp.wait_ge(pad_ok, 1)
            sp.dma_start(m["records"][EDGES:EDGES + PAD, :].rearrange("(p n) c -> p n c", p=128), pad_rec[:, :, :]).then_inc(sent, 16)
            sp.dma_start(m["sources"][EDGES:EDGES + PAD, :].rearrange("(p n) c -> p n c", p=128), pad_src[:, :, :]).then_inc(sent, 16)
            sp.wait_ge(rec_ok, 1)
            sp.dma_start(m["records"][0:EDGES, :].rearrange("(p n) c -> p n c", n=EC), rec[:, :, :]).then_inc(sent, 16)
            sp.wait_ge(src_ok, 1)
            sp.dma_start(m["sources"][0:EDGES, :].rearrange("(p n) c -> p n c", n=EC), srcs[:, :, :]).then_inc(sent, 16)
            table = m["rel_table"].rearrange("(r t p) f -> p t r f", t=T, p=R)
            for t in range(T):
                sp.wait_ge(rel_a, t + 1)
                sp.wait_ge(rel_v, t + 1)
                sp.dma_start(table[:, t], rows[:, t % 2]).then_inc(rel_out[t % 2], 16)
            sp.wait_ge(sent, 64)
            sp.wait_ge(rel_out[0], 16 * ((T + 1) // 2))
            sp.wait_ge(rel_out[1], 16 * (T // 2))

        @block.gpsimd
        def _(pool):
            nc.gpsimd.iota(m["iota"][:, :], pattern=[[1, 128]], base=0, channel_multiplier=0,
                           allow_small_or_imprecise_dtypes=True).then_inc(const, 1)
            nc.gpsimd.memset(ones[:, :], 1.0).then_inc(const, 1)
            pool.wait_ge(const, 2)
            nc.gpsimd.affine_select(out=eye[:, :], in_=ones[:, :], compare_op=ALU.is_equal, fill=0.0, base=0,
                                    pattern=[[-1, 128]], channel_multiplier=1).then_inc(const, 1)

        @block.tensor
        def _(pe):
            pe.wait_ge(x_in, 16)
            pe.wait_ge(const, 3)
            for n, (g, k) in enumerate(groups):
                if n >= 2:
                    pe.wait_ge(xt_ok, n - 1)
                for i in range(k):
                    last = nc.tensor.transpose(ps[n % 2][0:128, i * R:(i + 1) * R], x[:, g + i, :], eye[0:R, 0:R])
                last.then_inc(xt_ps, 1)
            pe.wait_ge(cnt_ok, 1)
            nc.tensor.matmul(ps[2][:, 0:T + 4], ones[0:R, 0:128], count[:, :], start=True, stop=True).then_inc(cnt_ps, 1)
            pe.wait_ge(w_ok, 1)
            pe.wait_ge(xt_ok, len(groups))
            for t in range(T):
                if t >= 2:
                    pe.wait_ge(rel_a, t - 1)
                    pe.wait_ge(rel_v, t - 1)
                for h in range(2):
                    last = nc.tensor.matmul(ps[4 + 2 * (t % 2) + h][0:R, :], xT[:, t * R:(t + 1) * R],
                                            W[:, 4 * h:4 * h + 4, :], start=True, stop=True)
                last.then_inc(rel_ps, 1)

        @block.scalar
        def _(act):
            for n, (g, k) in enumerate(groups):
                act.wait_ge(xt_ps, n + 1)
                nc.scalar.copy(xT[:, g * R:(g + k) * R], ps[n % 2][:, 0:k * R]).then_inc(xt_ok, 1)
            for t in range(T):
                act.wait_ge(rel_ps, t + 1)
                if t >= 2:
                    act.wait_ge(rel_out[t % 2], 16 * (t // 2))
                nc.scalar.copy(rows[:, t % 2, 0:4, :], ps[4 + 2 * (t % 2)][0:R, :].rearrange("p (r f) -> p r f", f=D)).then_inc(rel_a, 1)

        @block.vector
        def _(v):
            then = Steps(v, dve)
            V_ = nc.vector
            V_.memset(pad_rec[:, :, :], 0.0)
            V_.memset(count[:, :], 0.0)
            V_.memset(df[:, EC:EC + SLOTS], 1.0e6)
            then(V_.memset(pad_src[:, :, :], -512.0))
            V_.memset(pad_rec[:, :, 1:2], -1000.0).then_inc(pad_ok, 1)
            v.wait_ge(e_in, 32)
            V_.tensor_copy(df[:, 0:EC], di[:, :])
            then(V_.tensor_copy(df[0:R - 1, EC:EC + SLOTS], dn[0:R - 1, :]))
            for t in range(1, T + 1):
                then(V_.tensor_scalar(junk[:, :], df[:, 0:EC], float(R * t), None, ALU.is_lt, ALU.add, accum_out=count[:, t:t + 1]))
            then(V_.tensor_tensor(junk[:, :], df[:, 0:EC], df[:, 1:EC + 1], ALU.is_gt))
            then(V_.tensor_reduce(count[:, T + 2:T + 3], junk[:, :], AX.X, ALU.add))
            then(V_.tensor_tensor(junk[:, :], df[:, 0:EC], df[:, SLOTS:EC + SLOTS], ALU.is_equal))
            V_.tensor_reduce(count[:, T + 3:T + 4], junk[:, :], AX.X, ALU.add).then_inc(cnt_ok, 1)
            v.wait_ge(w_in, 32)
            for r in range(RELS):
                V_.tensor_scalar(W[:, r, :], V[:, 0, :], comp[:, BASES * r:BASES * r + 1], None, ALU.mult)
            then(V_.memset(bad[:, :], 0.0))
            for b in range(1, BASES):
                for r in range(RELS):
                    last = V_.scalar_tensor_tensor(W[:, r, :], V[:, b, :], comp[:, BASES * r + b:BASES * r + b + 1],
                                                   W[:, r, :], ALU.mult, ALU.add)
                    if r == RELS - 1 and b < BASES - 1:
                        then(last)
            last.then_inc(w_ok, 1)
            v.wait_ge(n_in, 48)
            V_.tensor_copy(sf[:, :], si[:, :])
            then(V_.tensor_copy(tf[:, :], ti[:, :]))
            V_.scalar_tensor_tensor(rec[:, :, 0], tf[:, :], float(NODES), sf[:, :], ALU.mult, ALU.add)
            V_.tensor_copy(rec[:, :, 1], df[:, 0:EC])
            V_.tensor_copy(rec[:, :, 2], wf[:, :]).then_inc(rec_ok, 1)
            then(V_.tensor_scalar(cf[:, :], sf[:, :], 1.0 / R, -0.496, ALU.mult, ALU.add))
            then(V_.tensor_scalar_add(cf[:, :], cf[:, :], MAGIC))
            then(V_.tensor_scalar_add(cf[:, :], cf[:, :], -MAGIC))
            V_.tensor_copy(srcs[:, :, 1], cf[:, :])
            V_.scalar_tensor_tensor(srcs[:, :, 0], cf[:, :], -float(R), sf[:, :], ALU.mult, ALU.add).then_inc(src_ok, 1)
            v.wait_ge(cnt_ps, 1)
            V_.tensor_copy(m["starts"][:, :], ps[2][:, 0:T + 2])
            then(V_.tensor_copy(bad[:, :], ps[2][0:1, T + 2:T + 4]))
            then(V_.tensor_tensor(sizes[:, :], m["starts"][0:1, 1:T + 1], m["starts"][0:1, 0:T], ALU.subtract))
            then(V_.tensor_scalar(sizes[:, :], sizes[:, :], float(PAD), None, ALU.is_gt))
            then(V_.tensor_reduce(large[:, :], sizes[:, :], AX.X, ALU.add))
            then(V_.tensor_tensor(bad[:, 0:1], bad[:, 0:1], bad[:, 1:2], ALU.add))
            then(V_.tensor_tensor(bad[:, 0:1], bad[:, 0:1], large[:, :], ALU.add))
            then(V_.tensor_scalar(m["flag"][:, :], bad[:, 0:1], 0.0, None, ALU.is_gt))
            for t in range(T):
                v.wait_ge(rel_ps, t + 1)
                if t >= 2:
                    v.wait_ge(rel_out[t % 2], 16 * (t // 2))
                V_.tensor_copy(rows[:, t % 2, 4:8, :], ps[5 + 2 * (t % 2)][0:R, :].rearrange("p (r f) -> p r f", f=D)).then_inc(rel_v, 1)


def message(nc, a, m):
    ctx = ExitStack()
    with ctx:
        def sb(name, shape, dt):
            return ctx.enter_context(nc.sbuf_tensor(name, shape, dt))

        def sem(name):
            return ctx.enter_context(nc.semaphore(name))

        h, xT, eye, ones, iota, starts, ps = (m[k] for k in ("h", "xT", "eye", "ones", "iota", "starts", "ps"))
        G = sb("gathered", [128, 2, COLS, D + 1], F32)
        A = sb("dst_onehot", [128, 2, COLS, R], F32)
        win = [sb(f"window{i}", [128, COLS * 3], F32) for i in range(2)]
        widx = [sb(f"window_at{i}", [128, 1], U32) for i in range(2)]
        rel = [sb(f"rel_at{i}", [128, COLS], U32) for i in range(2)]
        ell = [sb(f"slots{i}", [64, 2, SLOTS * 2], F32) for i in range(2)]
        eidx = [sb(f"slots_at{i}", [64, 2], U32) for i in range(2)]
        deg = [sb(f"degree{i}", [R, 1], F32) for i in range(2)]
        xt = [sb(f"xT_tile{i}", [128, R], F32) for i in range(2)]
        dab = [sb(f"degree_ab{i}", [64, 2], F32) for i in range(2)]
        start = sb("tile_start", [64, 1], F32)
        lane = sb("lane", [128, 1], F32)
        nodes = sb("tile_nodes", [128, R], F32)
        tri = sb("tri", [128, 4, 64], F32)
        loopw = sb("loop_w", [128, D + 1], F32)
        lbias = sb("loop_bias", [1, D + 1], F32)
        off = sb("unused", [64, 2, SLOTS], F32)
        codes = sb("codes", [128, 2, 2, SLOTS], F32)
        codesT = sb("codesT", [128, 2, 64], BF16)
        iob = sb("iota_b", [128, 128], BF16)
        L = sb("low_onehot", [128, PAIRS, R], BF16)
        H = sb("high_onehot", [128, PAIRS, 2 * T], BF16)
        CT = sb("countsT", [R, T, 2 * PAIRS], F32)
        bias = [sb(f"bias{i}", [128, NODES], F32) for i in range(2)]
        lns = [sb(f"ln{i}", [R, CW], F32) for i in range(2)]
        tiny = sb("tiny", [128, 1], F32)
        spare = sb("spare", [128, 1], F32)

        psA, psS, psC, psT, psK = ps[0:2], ps[2], ps[3:5], ps[5:7], ps[7]
        const, w_in, dve, gps = sem("m_const"), sem("m_w_in"), sem("dve_m"), sem("pool_m")
        at_ok, rel_ok, hot_ok, scaled = sem("at_ok"), sem("rel_ok"), sem("hot_ok"), sem("scaled")
        win_in = [sem("win_in0"), sem("win_in1")]
        g_in = [sem("g_in0"), sem("g_in1")]
        ell_in = [sem("ell_in0"), sem("ell_in1")]
        out_ok = [sem("bias_out0"), sem("bias_out1")]
        xt_ok, agg, deg_ok, st_ok, eidx_ok = sem("xt_ok_m"), sem("agg"), sem("deg_ok"), sem("st_ok"), sem("eidx_ok")
        codes_ok, codes_ps, lh_ok = sem("codes_ok"), sem("codes_ps"), sem("lh_ok")
        c_ps, c_ok, t_ps, ln_ok, masked, bias_ok = (sem("c_ps"), sem("c_ok"), sem("t_ps"), sem("ln_ok"), sem("masked"),
                                                    sem("bias_ok"))
        WINDOW_AFTER, SLOTS_AFTER = COLS // 2, COLS - 6
        pairs = [min(10, PAIRS - 10 * j) for j in range(CH)]
        cw = widths()
        block = ctx.enter_context(nc.Block())

        @block.gpsimd
        def _(pool):
            nc.gpsimd.iota(lane[:, :], pattern=[[0, 1]], base=0, channel_multiplier=COLS,
                           allow_small_or_imprecise_dtypes=True).then_inc(gps, 1)
            nc.gpsimd.memset(tri[:, :, :], 1.0).then_inc(gps, 1)
            pool.wait_ge(gps, 2)
            for q in range(2):
                nc.gpsimd.affine_select(out=tri[:, q, :], in_=tri[:, q, :], compare_op=ALU.is_gt, fill=0.0,
                                        base=PAIRS * q, pattern=[[1, 64]], channel_multiplier=-1)
                nc.gpsimd.affine_select(out=tri[:, 2 + q, :], in_=tri[:, 2 + q, :], compare_op=ALU.is_equal, fill=0.0,
                                        base=PAIRS * q, pattern=[[1, 64]], channel_multiplier=-1).then_inc(gps, 1)
            pool.wait_ge(gps, 4)
            nc.gpsimd.memset(tri[:, 2, PAIRS:64], 0.0).then_inc(const, 1)

            settled = Steps(pool, gps, 4)

            def settle():
                pool.wait_ge(gps, settled.done)
                nc.gpsimd.tensor_tensor(spare[:, :], lane[:, :], lane[:, :], ALU.add).then_inc(gps, 1)
                settled.done = settled.done + 1

            def window(t, par):
                pool.wait_ge(at_ok, t + 1)
                if not is_int(t) or t >= 2:
                    pool.wait_ge(hot_ok, t - 1)
                    pool.wait_ge(scaled, t - 1)
                settle()
                nc.gpsimd.indirect_dma_start(out=win[par][:, :], out_offset=None, in_=m["records"],
                                             in_offset=bass.IndirectOffsetOnAxis(ap=widx[par][:, :], axis=0)).then_inc(win_in[par], 16)

            def slots(u, par):
                pool.wait_ge(eidx_ok, u + 1)
                if not is_int(u) or u >= 2:
                    pool.wait_ge(codes_ok, u - 1)
                settle()
                for q in range(2):
                    nc.gpsimd.indirect_dma_start(out=ell[par][:, q, :], out_offset=None, in_=m["sources"],
                                                 in_offset=bass.IndirectOffsetOnAxis(ap=eidx[par][:, q:q + 1], axis=0)).then_inc(ell_in[par], 16)

            def step(t, par):
                settled.done = 4 + (1 + 2 * min(t, T) + max(0, t - 1) if is_int(t) else t * 3)
                if inside(t):
                    pool.wait_ge(rel_ok, t + 1)
                    if not is_int(t) or t >= 2:
                        pool.wait_ge(agg, t - 1)
                    settle()
                    for j in range(COLS):
                        nc.gpsimd.indirect_dma_start(out=G[:, par, j, 0:D], out_offset=None, in_=m["rel_table"],
                                                     in_offset=bass.IndirectOffsetOnAxis(ap=rel[par][:, j:j + 1], axis=0)).then_inc(g_in[par], 16)
                        if j == WINDOW_AFTER and (not is_int(t) or t + 1 < T):
                            window(t + 1, 1 - par)
                        if j == SLOTS_AFTER and inside(t - 1):
                            slots(t - 1, 1 - par)
                elif inside(t - 1):
                    slots(t - 1, 1 - par)

            pool.wait_ge(const, 2)
            window(0, 0)
            pipeline_loop(pool, step)
            pool.wait_ge(win_in[T % 2], 16 * ((T + 1) // 2))

        @block.sync
        def _(sp):
            sp.dma_start(loopw[:, 0:D], a["L0_gnn_loop_w"]).then_inc(w_in, 16)
            sp.dma_start(lbias[:, 0:D], a["L0_gnn_bias"].rearrange("(a n) -> a n", a=1)).then_inc(w_in, 16)
            sp.wait_ge(const, 2)

            def step(t, par):
                v = t - 2
                if inside(v):
                    sp.wait_ge(bias_ok, (v + 1) * CH)
                    sp.dma_start(m["bias"][bass.ds(v, 1), :, :].rearrange("a p n -> (a p) n"), bias[par][:, :]).then_inc(out_ok[par], 16)
            pipeline_loop(sp, step)
            sp.wait_ge(out_ok[0], 16 * ((T + 1) // 2))
            sp.wait_ge(out_ok[1], 16 * (T // 2))

        @block.vector
        def _(v_):
            V = nc.vector
            V.memset(G[:, :, :, D:D + 1], 1.0)
            V.memset(loopw[:, D:D + 1], 0.0)
            V.memset(lbias[:, D:D + 1], 0.0)
            V.memset(tiny[:, :], 1.0e-37)
            V.memset(bias[0][96:128, :], 0.0)
            V.memset(bias[1][96:128, :], 0.0)
            V.memset(codes[64:128, :, :, :], 0.0)
            V.tensor_copy(iob[:, :], iota[:, :])
            V.engine_nop().then_inc(const, 1)
            V.tensor_copy(nodes[:, :], iota[:, 0:R]).then_inc(dve, 1)
            v_.wait_ge(dve, 1)
            v_.wait_ge(const, 2)

            def window_at(t, par):
                V.tensor_tensor(widx[par][:, :], starts[:, bass.ds(t, 1)], lane[:, :], ALU.add).then_inc(at_ok, 1)

            def rows_at(t, par):
                v_.wait_ge(win_in[par], (half(t, par) + 1) * 16)
                if not is_int(t) or t >= 2:
                    v_.wait_ge(g_in[par], half(t, par) * (16 * COLS))
                V.tensor_copy(rel[par][:, :], win[par].rearrange("p (j c) -> p j c", c=3)[:, :, 0]).then_inc(rel_ok, 1)

            def main(t, par, then):
                v_.wait_ge(win_in[par], (half(t, par) + 1) * 16)
                if not is_int(t) or t + 2 < T:
                    window_at(t + 2, par)
                w3 = win[par].rearrange("p (j c) -> p j c", c=3)
                if not is_int(t) or t >= 2:
                    v_.wait_ge(agg, t - 1)
                V.tensor_tensor(A[:, par, :, :], nodes[:, :].unsqueeze(1).to_broadcast([128, COLS, R]),
                                w3[:, :, 1:2].to_broadcast([128, COLS, R]), ALU.is_equal).then_inc(hot_ok, 1)
                v_.wait_ge(hot_ok, t + 1)
                then(V.tensor_scalar_add(nodes[:, :], nodes[:, :], float(R)))

            def onehots(v, par, then):
                v_.wait_ge(ell_in[par], (half(v, par) + 1) * 32)
                wait(v_, codes_ok, v)
                for q in range(2):
                    last = V.tensor_scalar(off[:, q, :], iota[0:64, 0:SLOTS], dab[par][:, q:q + 1], -512.0, ALU.is_ge, ALU.mult)
                then(last)
                slot = ell[par].rearrange("p q (s c) -> p q s c", c=2)
                V.tensor_tensor(codes[0:64, 0, :, :], slot[:, :, :, 0], off[:, :, :], ALU.add)
                V.tensor_tensor(codes[0:64, 1, 0, :], slot[:, 0, :, 1], off[:, 0, :], ALU.add)
                V.scalar_tensor_tensor(codes[0:64, 1, 1, :], slot[:, 1, :, 1], float(T), off[:, 1, :], ALU.add, ALU.add).then_inc(codes_ok, 1)
                v_.wait_ge(codes_ps, v + 1)
                wait(v_, lh_ok, v)
                then(V.tensor_copy(codesT[:, :, :], psK[:, 0:256].rearrange("p (k n) -> p k n", k=2)[:, :, 0:64]))
                if not is_int(v) or v >= 1:
                    v_.wait_ge(c_ps, v * CH)
                V.tensor_tensor(L[:, :, :], iob[:, 0:R].unsqueeze(1).to_broadcast([128, PAIRS, R]),
                                codesT[:, 0, 0:PAIRS].unsqueeze(2).to_broadcast([128, PAIRS, R]), ALU.is_equal)
                V.tensor_tensor(H[:, :, :], iob[:, 0:2 * T].unsqueeze(1).to_broadcast([128, PAIRS, 2 * T]),
                                codesT[:, 1, 0:PAIRS].unsqueeze(2).to_broadcast([128, PAIRS, 2 * T]), ALU.is_equal).then_inc(lh_ok, 1)

            def sums(u, par, then):
                v_.wait_ge(agg, u + 1)
                V.tensor_scalar_max(h[:, bass.ds(u, 1), :].rearrange("p a f -> p (a f)"), psA[par][0:R, 0:D], 0.0)
                wait(v_, eidx_ok, u)
                V.tensor_copy(start[:, :], starts[0:64, bass.ds(u, 1)])
                V.tensor_copy(deg[par][:, :], psA[par][0:R, D:D + 1]).then_inc(deg_ok, 1)
                v_.wait_ge(deg_ok, u + 1)
                v_.wait_ge(st_ok, u + 1)
                if not is_int(u) or u >= 2:
                    v_.wait_ge(ell_in[par], half(u, par) * 32)
                V.tensor_copy(dab[par][:, :], psS[0:64, 2:4])
                V.tensor_scalar(eidx[par][:, :], psS[0:64, 0:2], start[:, :], None, ALU.add).then_inc(eidx_ok, 1)

            def bias_rows(v, par, then):
                if not is_int(v) or v >= 2:
                    v_.wait_ge(out_ok[par], half(v, par) * 16)
                for j in range(CH):
                    n = v * CH + j
                    row = bias[par][0:R, CW * j:CW * j + cw[j]]
                    v_.wait_ge(ln_ok, n + 1)
                    V.tensor_scalar(row, psT[(par + j) % 2][0:R, 0:cw[j]], 0.0, NEG, ALU.is_equal, ALU.mult).then_inc(masked, 1)
                    v_.wait_ge(masked, n + 1)
                    V.tensor_tensor(row, row, lns[(par + j) % 2][:, 0:cw[j]], ALU.add).then_inc(bias_ok, 1)

            def step(t, par):
                base = 1 + min(t, T) + 2 * max(0, t - 2) if is_int(t) else 3 * t - 3
                then = Steps(v_, dve, base)
                if inside(t - 2):
                    onehots(t - 2, par, then)
                if inside(t):
                    main(t, par, then)
                if inside(t - 1):
                    sums(t - 1, 1 - par, then)
                if inside(t + 1):
                    rows_at(t + 1, 1 - par)
                if inside(t - 2):
                    bias_rows(t - 2, par, then)

            window_at(0, 0)
            window_at(1, 1)
            rows_at(0, 0)
            pipeline_loop(v_, step)

        @block.tensor
        def _(pe):
            pe.wait_ge(w_in, 32)
            pe.wait_ge(const, 2)

            def step(t, par):
                v, u = t - 2, t - 1
                if inside(v):
                    pe.wait_ge(codes_ok, v + 1)
                    for k in range(2):
                        last = nc.tensor.transpose(psK[:, 128 * k:128 * (k + 1)], codes[:, k].rearrange("p q s -> p (q s)"),
                                                   eye[:, :])
                    last.then_inc(codes_ps, 1)
                if inside(u):
                    pe.wait_ge(xt_ok, u + 1)
                    if not is_int(u) or u >= 2:
                        pe.wait_ge(deg_ok, u - 1)
                    acc = psA[1 - par][0:R, 0:D + 1]
                    nc.tensor.matmul(acc, xt[1 - par][:, :], loopw[:, :], start=True, stop=False)
                    nc.tensor.matmul(acc, ones[0:1, 0:R], lbias[:, :], start=False, stop=False)
                    pe.wait_ge(hot_ok, u + 1)
                    pe.wait_ge(scaled, u + 1)
                    for j in range(COLS):
                        last = nc.tensor.matmul(acc, A[:, 1 - par, j, :], G[:, 1 - par, j, :], start=False, stop=(j == COLS - 1))
                    last.then_inc(agg, 1)
                if inside(u):
                    pe.wait_ge(deg_ok, u + 1)
                    for q in range(4):
                        last = nc.tensor.matmul(psS[0:64, q:q + 1], tri[0:R, q, :], deg[1 - par][:, :], start=True, stop=True)
                    last.then_inc(st_ok, 1)
                if inside(v):
                    pe.wait_ge(lh_ok, v + 1)
                    for j in range(CH):
                        if not is_int(v) or v * CH + j >= 2:
                            pe.wait_ge(c_ok, v * CH + j - 1)
                        for i in range(pairs[j]):
                            p = 10 * j + i
                            last = nc.tensor.matmul(psC[(par + j) % 2][0:R, 2 * T * i:2 * T * (i + 1)], L[:, p, :], H[:, p, :],
                                                    start=True, stop=True)
                        last.then_inc(c_ps, 1)
                if inside(v):
                    pe.wait_ge(c_ok, v * CH + CH)
                    for j in range(CH):
                        if not is_int(v) or v * CH + j >= 2:
                            pe.wait_ge(ln_ok, v * CH + j - 1)
                            pe.wait_ge(masked, v * CH + j - 1)
                        for i in range(cw[j] // R):
                            last = nc.tensor.transpose(psT[(par + j) % 2][0:R, R * i:R * (i + 1)], CT[:, 4 * j + i, 0:R], eye[0:R, 0:R])
                        last.then_inc(t_ps, 1)
            pipeline_loop(pe, step)

        @block.scalar
        def _(act):
            def step(t, par):
                v, u, up = t - 2, t - 1, 1 - par
                if inside(u):
                    if not is_int(u) or u >= 2:
                        act.wait_ge(agg, u - 1)
                    nc.scalar.copy(xt[up][:, :], xT[:, bass.ds(u * R, R)]).then_inc(xt_ok, 1)
                    act.wait_ge(g_in[up], (half(u, up) + 1) * (16 * COLS))
                    for j in range(COLS):
                        last = nc.scalar.mul(G[:, up, j, 0:D], G[:, up, j, 0:D], win[up][:, 3 * j + 2:3 * j + 3])
                    last.then_inc(scaled, 1)
                if inside(v):
                    if not is_int(v) or v >= 1:
                        act.wait_ge(t_ps, v * CH)
                    for j in range(CH):
                        act.wait_ge(c_ps, v * CH + j + 1)
                        k = pairs[j]
                        for q in range(2):
                            src = psC[(par + j) % 2][0:R, 0:2 * T * k].rearrange("p (i q c) -> p i q c", i=k, q=2)[:, :, q, :]
                            dst = CT[:, :, PAIRS * q + 10 * j:PAIRS * q + 10 * j + k].rearrange("p c i -> p i c")
                            last = nc.scalar.copy(dst, src)
                        last.then_inc(c_ok, 1)
                    for j in range(CH):
                        n = v * CH + j
                        act.wait_ge(t_ps, n + 1)
                        if not is_int(v) or n >= 2:
                            act.wait_ge(bias_ok, n - 1)
                        nc.scalar.activation(lns[(par + j) % 2][:, 0:cw[j]], psT[(par + j) % 2][0:R, 0:cw[j]], ACT.Ln,
                                             bias=tiny[0:R, :]).then_inc(ln_ok, 1)
            act.wait_ge(const, 2)
            pipeline_loop(act, step)


def pipeline_loop(eng, step):
    for t in range(FIRST):
        step(t, t % 2)
    with eng.Fori(0, (T - FIRST) // 2) as k:
        step(k * 2 + FIRST, FIRST % 2)
        step(k * 2 + FIRST + 1, (FIRST + 1) % 2)
    for t in range(T, T + 2):
        step(t, t % 2)


def first_norms(nc, a, m):
    ctx = ExitStack()
    with ctx:
        def sb(name, shape, dt):
            return ctx.enter_context(nc.sbuf_tensor(name, shape, dt))

        def sem(name):
            return ctx.enter_context(nc.semaphore(name))

        x, xT, h, eye, ones, ps = m["x"], m["xT"], m["h"], m["eye"], m["ones"], m["ps"]
        ffn = sb("ffn", [D, D], F32)
        ffnT = sb("ffnT", [D, D], F32)
        ffnb = sb("ffn_b", [1, D], F32)
        gain = sb("ln_g", [R, D], F32)
        shift = sb("ln_b", [R, D], F32)
        hT = [sb(f"hT{i}", [D, 4 * R], F32) for i in range(2)]
        y = [sb(f"y{i}", [R, 4, D], F32) for i in range(2)]
        stats = sb("stats", [R, 4, 6], F32)
        mean = sb("mean", [R, 4, 2], F32)
        rstd = sb("rstd", [R, 4, 1], F32)
        half_power = sb("minus_half", [R, 4, 1], F32)
        w_in, dve, f_ps, f_ok, h_ps, h_ok, y_ps, y_ok, x_ok, t_ps, t_ok, asked, rooted = (
            sem("f_" + n) for n in ("w_in", "dve", "ffn_ps", "ffn_ok", "h_ps", "h_ok", "y_ps", "y_ok", "x_ok", "t_ps", "t_ok",
                                    "asked", "rooted"))
        groups = [(g, min(4, T - g)) for g in range(0, T, 4)]
        block = ctx.enter_context(nc.Block())

        @block.sync
        def _(sp):
            sp.dma_start(ffn[:, :], a["L0_gnn_ffn_w"]).then_inc(w_in, 16)
            sp.dma_start(ffnb[:, :], a["L0_gnn_ffn_b"].rearrange("(a n) -> a n", a=1)).then_inc(w_in, 16)
            sp.dma_start(gain[:, :], a["L0_gnn_ln_g"].partition_broadcast(R)).then_inc(w_in, 16)
            sp.dma_start(shift[:, :], a["L0_gnn_ln_b"].partition_broadcast(R)).then_inc(w_in, 16)

        @block.gpsimd
        def _(pool):
            nc.gpsimd.memset(half_power[:, :, :], -0.5).then_inc(rooted, 1)
            for n in range(2 * len(groups)):
                k = groups[n // 2][1]
                pool.wait_ge(asked, n + 1)
                pool.wait_ge(rooted, 1)
                nc.gpsimd.tensor_tensor(rstd[:, 0:k, :], rstd[:, 0:k, :], half_power[:, 0:k, :], ALU.pow).then_inc(rooted, 1)

        @block.tensor
        def _(pe):
            def turn_h(n):
                g, k = groups[n]
                if n >= 2:
                    pe.wait_ge(h_ok, n - 1)
                for i in range(k):
                    last = nc.tensor.transpose(ps[n % 2][:, i * R:(i + 1) * R], h[:, g + i, :], eye[0:R, 0:R])
                last.then_inc(h_ps, 1)

            def turn_x(n):
                g, k = groups[n]
                pe.wait_ge(x_ok, n + 1)
                if n >= 2:
                    pe.wait_ge(t_ok, n - 1)
                for i in range(k):
                    last = nc.tensor.transpose(ps[4 + n % 2][:, i * R:(i + 1) * R], x[:, g + i, :], eye[0:R, 0:R])
                last.then_inc(t_ps, 1)

            turn_h(0)
            pe.wait_ge(w_in, 64)
            nc.tensor.transpose(ps[6][:, 0:D], ffn[:, :], eye[:, :]).then_inc(f_ps, 1)
            pe.wait_ge(f_ok, 1)
            for n, (g, k) in enumerate(groups):
                if n + 1 < len(groups):
                    turn_h(n + 1)
                pe.wait_ge(h_ok, n + 1)
                if n >= 2:
                    pe.wait_ge(y_ok, n - 1)
                for i in range(k):
                    to = ps[2 + n % 2][0:R, i * D:(i + 1) * D]
                    nc.tensor.matmul(to, ones[0:1, 0:R], ffnb[:, :], start=True, stop=False)
                    last = nc.tensor.matmul(to, hT[n % 2][:, i * R:(i + 1) * R], ffnT[:, :], start=False, stop=True)
                last.then_inc(y_ps, 1)
                if n >= 1:
                    turn_x(n - 1)
            turn_x(len(groups) - 1)

        @block.scalar
        def _(act):
            def turn(n):
                g, k = groups[n]
                act.wait_ge(t_ps, n + 1)
                nc.scalar.copy(xT[:, g * R:(g + k) * R], ps[4 + n % 2][:, 0:k * R]).then_inc(t_ok, 1)

            act.wait_ge(f_ps, 1)
            nc.scalar.copy(ffnT[:, :], ps[6][:, 0:D]).then_inc(f_ok, 1)
            for n, (g, k) in enumerate(groups):
                act.wait_ge(h_ps, n + 1)
                if n >= 2:
                    act.wait_ge(y_ps, n - 1)
                nc.scalar.copy(hT[n % 2][:, 0:k * R], ps[n % 2][:, 0:k * R]).then_inc(h_ok, 1)
                if n >= 2:
                    turn(n - 2)
            for n in range(len(groups) - 2, len(groups)):
                turn(n)

        @block.vector
        def _(v):
            then = Steps(v, dve)
            V = nc.vector
            v.wait_ge(w_in, 64)
            for n, (g, k) in enumerate(groups):
                b = y[n % 2][:, 0:k, :]
                xs = x[:, g:g + k, :]
                v.wait_ge(y_ps, n + 1)
                V.tensor_tensor(b, ps[2 + n % 2][0:R, 0:k * D].rearrange("p (t f) -> p t f", f=D), xs, ALU.add).then_inc(y_ok, 1)
                v.wait_ge(y_ok, n + 1)
                then(norm_rows(V, then, b, b, stats, mean, rstd, k, 1.0e-8, asked, lambda: v.wait_ge(rooted, 2 * n + 2)))
                then(V.tensor_tensor(b, b, gain[:, :].unsqueeze(1).to_broadcast([R, k, D]), ALU.mult))
                then(V.tensor_tensor(b, b, shift[:, :].unsqueeze(1).to_broadcast([R, k, D]), ALU.add))
                then(V.tensor_tensor(b, b, xs, ALU.add))
                norm_rows(V, then, xs, b, stats, mean, rstd, k, 1.0e-5, asked,
                          lambda: v.wait_ge(rooted, 2 * n + 3)).then_inc(x_ok, 1)
                v.wait_ge(x_ok, n + 1)


def norm_rows(V, then, to, rows, stats, mean, rstd, k, eps, asked, root, spare=None):
    for i in range(k):
        last = V.bn_stats(stats[:, i, :], rows[:, i, :])
    then(last)
    if spare is not None:
        V.memset(spare, 0.0).then_inc(then.sem, 1)
        then.done = then.done + 1
    for i in range(k):
        last = V.bn_aggr(mean[:, i, :], stats[:, i, :])
    then(last)
    V.tensor_scalar_add(rstd[:, 0:k, :], mean[:, 0:k, 1:2], eps).then_inc(asked, 1)
    root()
    for i in range(k):
        last = V.tensor_scalar(to[:, i, :], rows[:, i, :], mean[:, i, 0:1], rstd[:, i, :], ALU.subtract, ALU.mult)
    return last


def conv(nc, a, m, layer, out):
    ctx = ExitStack()
    with ctx:
        def sb(name, shape, dt):
            return ctx.enter_context(nc.sbuf_tensor(f"{name}_l{layer}", shape, dt))

        def sem(name):
            return ctx.enter_context(nc.semaphore(f"{name}_l{layer}"))

        x, eye, ones, ps = m["x"], m["eye"], m["ones"], m["ps"]
        inT = m["xT"] if layer == 1 else m["hT"]
        W = {c: sb("W" + c, [D, D], F32) for c in "qkvs"}
        bq, bk = sb("bq", [D, 1], F32), sb("bk", [D, 1], F32)
        bv, bs = sb("bv", [1, D], F32), sb("bs", [1, D], F32)
        qT = sb("qT", [128, NODES], F32)
        kT = sb("kT", [128, NODES], F32)
        vals = sb("values", [R, T, HEADS, HD + 1], F32)
        q_now = [sb(f"q_tile{i}", [128, R], F32) for i in range(2)]
        x_now = [sb(f"in_tile{i}", [128, R], F32) for i in range(2)]
        bias = [sb(f"bias_rows{i}", [128, NODES], F32) for i in range(2)]
        S = [sb(f"scores{i}", [R, HEADS, NODES], F32) for i in range(2)]
        PT = [sb(f"weightsT{i}", [R, CW], F32) for i in range(4)]
        mx = [sb(f"chunk_max{i}", [R, HEADS, CH], F32) for i in range(2)]
        top = sb("top", [R, HEADS], F32)
        neg = [sb(f"neg_max{i}", [R, HEADS], F32) for i in range(2)]
        den = sb("sum", [R, HEADS, 1], F32)
        rows = [sb(f"rows{i}", [R, 1, D], F32) for i in range(2)]
        skip = sb("skip", [R, D], F32)
        OT = [sb(f"sumsT{i}", [HD + 1, HEADS, R], F32) for i in range(2)]
        stats, mean, rstd = sb("stats", [R, 1, 6], F32), sb("mean", [R, 1, 2], F32), sb("rstd", [R, 1, 1], F32)
        half_power = sb("minus_half", [R, 1, 1], F32)
        spare, spare2 = sb("spare", [R, 1], F32), sb("spare2", [R, 1], F32)

        names = ("w_in", "dve", "q_ps", "q_ok", "k_ok", "v_ps", "v_ok", "cur", "qk", "masked", "neg_ok", "exp_ok", "t_ps", "pa_ok",
                 "pv_ok", "pt", "skip_ok", "rows_ok", "r_ps", "r_ok", "one", "fin_ok", "dve2", "asked",
                 "rooted", "carried", "ot_ok", "o_ps", "x_cur")
        z = {n: sem(n) for n in names}
        b_in = [sem("b_in0"), sem("b_in1")]
        out_ok = [sem("rows_out0"), sem("rows_out1")]
        groups = [(g, min(4, T - g)) for g in range(0, T, 4)]
        cw = widths()
        psS, psT, psO = ps[0:4], ps[4:6], ps[6:8]
        ON_V = (1, 4, 7, 10, 13)
        NT = HEADS * CH
        TURN = [((), ()), ((0,), (1,)), ((2,), (3,)), ((4,), (5,)), ((6,), (7, 8)), ((9,), (10, 11)), ((12,), (13,))]
        EXP_BEFORE = {3: 2, 6: 3}
        EXP_AT = 3
        on_v = [sum(c < i for c in ON_V) for i in range(NT + 1)]
        block = ctx.enter_context(nc.Block())

        def chunk_out(eng, u, i):
            if i in ON_V:
                wait(eng, z["pt"], u * len(ON_V) + (on_v[i] + 1))
            else:
                wait(eng, z["pa_ok"], u * (NT - len(ON_V)) + (i - on_v[i] + 1))

        @block.sync
        def _(sp):
            for c in "qkvs":
                sp.dma_start(W[c][:, :], a[f"L1_gnn_W{c}{layer}"]).then_inc(z["w_in"], 16)
            for b, c in ((bq, "q"), (bk, "k")):
                sp.dma_start(b[:, :], a[f"L1_gnn_b{c}{layer}"].rearrange("(n a) -> n a", a=1)).then_inc(z["w_in"], 16)
            for b, c in ((bv, "v"), (bs, "s")):
                sp.dma_start(b[:, :], a[f"L1_gnn_b{c}{layer}"].rearrange("(a n) -> a n", a=1)).then_inc(z["w_in"], 16)

            def step(t, par):
                if inside(t):
                    if not is_int(t) or t >= 2:
                        sp.wait_ge(z["masked"], (t - 1) * NT)
                    sp.dma_start(bias[par][:, :], m["bias"][bass.ds(t, 1), :, :].rearrange("a p n -> (a p) n")).then_inc(b_in[par], 16)
                if layer == 2 and inside(t - 2):
                    sp.wait_ge(z["rows_ok"], t - 1)
                    sp.dma_start(out[bass.ds((t - 2) * R, R), :], rows[par][:, 0, :]).then_inc(out_ok[par], 16)
            pipeline_loop(sp, step)
            if layer == 2:
                sp.wait_ge(out_ok[0], 16 * ((T + 1) // 2))
                sp.wait_ge(out_ok[1], 16 * (T // 2))

        @block.gpsimd
        def _(pool):
            nc.gpsimd.memset(half_power[:, :, :], -0.5)
            nc.gpsimd.memset(vals[:, :, :, HD:HD + 1], 1.0).then_inc(z["one"], 1)
            pool.wait_ge(z["one"], 1)
            pool.wait_ge(z["q_ok"], CH)

            def step(t, par):
                if inside(t):
                    if not is_int(t) or t >= 2:
                        pool.wait_ge(z["qk"], (t - 1) * NT)
                    nc.gpsimd.tensor_copy(q_now[par][:, :], qT[:, bass.ds(t * R, R)]).then_inc(z["cur"], 1)
                if inside(t - 2):
                    if not is_int(t) or t >= 4:
                        pool.wait_ge(z["o_ps"], t - 3)
                    nc.gpsimd.tensor_copy(x_now[par][:, :], inT[:, bass.ds((t - 2) * R, R)]).then_inc(z["x_cur"], 1)
                if layer == 2 and inside(t - 2):
                    pool.wait_ge(z["asked"], t - 1)
                    nc.gpsimd.tensor_tensor(rstd[:, :, :], rstd[:, :, :], half_power[:, :, :], ALU.pow).then_inc(z["rooted"], 1)
            pipeline_loop(pool, step)

        @block.tensor
        def _(pe):
            pe.wait_ge(z["w_in"], 128)
            for j in range(CH):
                if j >= 2:
                    pe.wait_ge(z["q_ok"], j - 1)
                    pe.wait_ge(z["k_ok"], j - 1)
                for c, b in (("q", 0), ("k", 2)):
                    last = nc.tensor.matmul(ps[b + j % 2][:, 0:cw[j]], W[c][:, :], inT[:, CW * j:CW * j + cw[j]], start=True, stop=True)
                last.then_inc(z["q_ps"], 1)
            for n, (g, k) in enumerate(groups):
                if n >= 2:
                    pe.wait_ge(z["v_ok"], n - 1)
                for i in range(k):
                    to = ps[4 + n % 2][0:R, i * D:(i + 1) * D]
                    nc.tensor.matmul(to, ones[0:1, 0:R], bv[:, :], start=True, stop=False)
                    last = nc.tensor.matmul(to, inT[:, (g + i) * R:(g + i + 1) * R], W["v"][:, :], start=False, stop=True)
                last.then_inc(z["v_ps"], 1)
            pe.wait_ge(z["q_ok"], CH)
            pe.wait_ge(z["k_ok"], CH)
            pe.wait_ge(z["v_ok"], len(groups))
            pe.wait_ge(z["one"], 1)

            def product(u, up, i):
                hd, c = i // CH, i % CH
                chunk_out(pe, u, i)
                to = psO[up][0:HD + 1, R * hd:R * (hd + 1)]
                for b in range(cw[c] // R):
                    last = nc.tensor.matmul(to, vals[:, 4 * c + b, hd, :], PT[(2 * up + i) % 4][:, b * R:(b + 1) * R],
                                            start=(c == 0 and b == 0), stop=(c == CH - 1 and b == 0))
                last.then_inc(z["pv_ok"], 1)

            def scores(t, par, j, hd):
                if j == 0 and hd == 0:
                    pe.wait_ge(z["cur"], t + 1)
                if not is_int(t) or t * CH + j >= 2:
                    pe.wait_ge(z["masked"], (t * CH + (j - 2)) * 2 + (hd + 1))
                lo, hi = HD * hd, HD * (hd + 1)
                nc.tensor.matmul(psS[2 * ((par + j) % 2) + hd][0:R, 0:cw[j]], q_now[par][lo:hi, :],
                                 kT[lo:hi, CW * j:CW * j + cw[j]], start=True, stop=True).then_inc(z["qk"], 1)

            def step(t, par):
                u, up, w = t - 1, 1 - par, t - 2
                for j in range(CH):
                    for hd_s in range(HEADS):
                        if inside(t):
                            scores(t, par, j, hd_s)
                        if j == 0 and inside(w):
                            product(w, par, NT - 2 + hd_s)
                        if not inside(u):
                            continue
                        for i in TURN[j][hd_s]:
                            hd, c = i // CH, i % CH
                            if c in (0, EXP_AT):
                                pe.wait_ge(z["exp_ok"], u * 4 + (2 * hd + 1 + (c > 0)))
                            if i >= 2:
                                chunk_out(pe, u, i - 2)
                            elif not is_int(u) or u >= 1:
                                chunk_out(pe, u - 1, i - 2 + NT)
                            for b in range(cw[c] // R):
                                n = 4 * c + b
                                last = nc.tensor.transpose(psT[i % 2][0:R, b * R:(b + 1) * R], S[up][:, hd, n * R:(n + 1) * R],
                                                           eye[0:R, 0:R])
                            last.then_inc(z["t_ps"], 1)
                            if i == 2 and (not is_int(u) or u >= 2):
                                pe.wait_ge(z["fin_ok"], u - 1)
                            if i >= 2:
                                product(u, up, i - 2)
                    if j == 2 and inside(w):
                        pe.wait_ge(z["ot_ok"], w + 1)
                        pe.wait_ge(z["x_cur"], w + 1)
                        for hd in range(HEADS):
                            nc.tensor.transpose(psO[par][0:R, 256 + 128 * hd:256 + 128 * hd + HD + 1], OT[par][:, hd, :],
                                                       eye[0:HD + 1, 0:HD + 1])
                        to = psO[par][0:R, 0:D]
                        nc.tensor.matmul(to, ones[0:1, 0:R], bs[:, :], start=True, stop=False)
                        nc.tensor.matmul(to, x_now[par][:, :], W["s"][:, :], start=False, stop=True).then_inc(z["o_ps"], 1)
                    if layer == 1 and j == 5 and inside(w):
                        pe.wait_ge(z["rows_ok"], w + 1)
                        nc.tensor.transpose(psO[par][:, 128:128 + R], rows[par][:, 0, :], eye[0:R, 0:R]).then_inc(z["r_ps"], 1)
            pipeline_loop(pe, step)

        @block.scalar
        def _(act):
            act.wait_ge(z["w_in"], 128)
            for j in range(CH):
                act.wait_ge(z["q_ps"], j + 1)
                nc.scalar.activation(kT[:, CW * j:CW * j + cw[j]], ps[2 + j % 2][:, 0:cw[j]], ACT.Identity, bias=bk[:, :]).then_inc(z["k_ok"], 1)

            def sums_out(w, par):
                act.wait_ge(z["pv_ok"], (w + 1) * NT)
                if not is_int(w) or w >= 2:
                    act.wait_ge(z["o_ps"], w - 1)
                nc.scalar.copy(OT[par][:, :, :], psO[par][0:HD + 1, 0:2 * R].rearrange("p (h n) -> p h n", h=HEADS)).then_inc(z["ot_ok"], 1)

            def step(t, par):
                u, up, w = t - 1, 1 - par, t - 2
                def exps(n):
                    hd, (lo, hi) = n // 2, ((0, CW * EXP_AT), (CW * EXP_AT, NODES))[n % 2]
                    part = S[up][:, hd, lo:hi]
                    nc.scalar.activation(part, part, ACT.Exp, bias=neg[up][:, hd:hd + 1]).then_inc(z["exp_ok"], 1)

                if inside(u):
                    act.wait_ge(z["neg_ok"], u + 1)
                    exps(0)
                    exps(1)
                if inside(w):
                    sums_out(w, par)
                if inside(u):
                    for i in range(NT):
                        if i in EXP_BEFORE:
                            exps(EXP_BEFORE[i])
                        if i in ON_V:
                            continue
                        c = i % CH
                        act.wait_ge(z["t_ps"], u * NT + (i + 1))
                        if i >= 4 or not is_int(u) or u >= 1:
                            act.wait_ge(z["pv_ok"], u * NT + (i - 3))
                        nc.scalar.copy(PT[(2 * up + i) % 4][:, 0:cw[c]], psT[i % 2][0:R, 0:cw[c]]).then_inc(z["pa_ok"], 1)
                        if layer == 1 and i == 12 and inside(w):
                            turned(w, par)
                elif layer == 1 and inside(w):
                    turned(w, par)

            def turned(w, par):
                act.wait_ge(z["r_ps"], w + 1)
                nc.scalar.copy(m["hT"][:, bass.ds(w * R, R)], psO[par][:, 128:128 + R]).then_inc(z["r_ok"], 1)
            pipeline_loop(act, step)

        @block.vector
        def _(v):
            V = nc.vector
            v.wait_ge(z["w_in"], 128)
            for j in range(CH):
                v.wait_ge(z["q_ps"], j + 1)
                V.tensor_scalar(qT[:, CW * j:CW * j + cw[j]], ps[j % 2][:, 0:cw[j]], bq[:, :], float(HD) ** -0.5, ALU.add, ALU.mult).then_inc(z["q_ok"], 1)
            for n, (g, k) in enumerate(groups):
                v.wait_ge(z["v_ps"], n + 1)
                V.tensor_copy(vals[:, g:g + k, :, 0:HD], ps[4 + n % 2][0:R, 0:k * D].rearrange("p (t h f) -> p t h f", h=HEADS, f=HD)).then_inc(z["v_ok"], 1)

            def finish(w, par, then):
                v.wait_ge(z["o_ps"], w + 1)
                O = psO[par][0:R, 256:512].rearrange("p (h f) -> p h f", h=HEADS)
                then(V.tensor_scalar_max(den[:, :, :], O[:, :, HD:HD + 1], 1.0e-30))
                V.tensor_copy(skip[:, :], psO[par][0:R, 0:D])
                then(V.reciprocal(den[:, :, :], den[:, :, :]))
                if layer == 2 and (not is_int(w) or w >= 2):
                    v.wait_ge(out_ok[par], half(w, par) * 16)
                for hd in range(HEADS):
                    last = V.scalar_tensor_tensor(rows[par][:, 0, HD * hd:HD * (hd + 1)], O[:, hd, 0:HD], den[:, hd, :],
                                                  skip[:, HD * hd:HD * (hd + 1)], ALU.mult, ALU.add)
                last.then_inc(z["fin_ok"], 1)
                v.wait_ge(z["fin_ok"], w + 1)
                r = rows[par]
                if layer == 1:
                    V.tensor_scalar_max(r[:, :, :], r[:, :, :], 0.0).then_inc(z["rows_ok"], 1)
                else:
                    then(V.tensor_tensor(r[:, :, :], r[:, :, :], x[:, bass.ds(w, 1), :], ALU.add))
                    norm_rows(V, then, r, r, stats, mean, rstd, 1, 1.0e-5, z["asked"],
                              lambda: v.wait_ge(z["rooted"], w + 1), spare2[:, :]).then_inc(z["rows_ok"], 1)
                v.wait_ge(z["rows_ok"], w + 1)

            CHAIN = 2 if layer == 1 else 6

            def step(t, par):
                u, up, w = t - 1, 1 - par, t - 2
                then = Steps(v, z["dve"], w * CHAIN if not is_int(w) else CHAIN * max(0, w))
                if inside(t):
                    v.wait_ge(b_in[par], (half(t, par) + 1) * 16)
                    if not is_int(t) or t >= 2:
                        v.wait_ge(z["t_ps"], (t - 1) * NT)
                        v.wait_ge(z["neg_ok"], t - 1)
                for j in range(CH):
                    if inside(t):
                        v.wait_ge(z["carried"], t * CH + j) if not is_int(t) or t * CH + j > 0 else None
                        v.wait_ge(z["qk"], (t * CH + (j + 1)) * 2)
                        V.memset(spare[:, :], 0.0).then_inc(z["carried"], 1)
                        for hd in range(HEADS):
                            lo, hi = CW * j, CW * j + cw[j]
                            V.tensor_tensor_reduce(S[par][:, hd, lo:hi], psS[2 * ((par + j) % 2) + hd][0:R, 0:cw[j]],
                                                   bias[par][0:R, lo:hi], 1.0, FLOOR, ALU.add, ALU.max,
                                                   mx[par][:, hd, j:j + 1]).then_inc(z["masked"], 1)
                    if inside(u):
                        for i in TURN[j][0] + TURN[j][1]:
                            if i in ON_V:
                                c = i % CH
                                v.wait_ge(z["t_ps"], u * NT + (i + 1))
                                if i >= 4 or not is_int(u) or u >= 1:
                                    v.wait_ge(z["pv_ok"], u * NT + (i - 3))
                                V.tensor_copy(PT[(2 * up + i) % 4][:, 0:cw[c]], psT[i % 2][0:R, 0:cw[c]]).then_inc(z["pt"], 1)
                    if j == 3 and inside(w):
                        finish(w, par, then)
                if inside(t):
                    v.wait_ge(z["masked"], (t + 1) * NT)
                    wait(v, z["neg_ok"], t)
                    V.tensor_reduce(top[:, :], mx[par][:, :, :], AX.X, ALU.max).then_inc(z["dve2"], 1)
                    v.wait_ge(z["dve2"], t + 1)
                    if not is_int(t) or t >= 2:
                        v.wait_ge(z["exp_ok"], (t - 1) * 4)
                    V.tensor_scalar_mul(neg[par][:, :], top[:, :], -1.0).then_inc(z["neg_ok"], 1)
            pipeline_loop(v, step)


INPUTS = ['x', 'src', 'dst', 'edge_type_8', 'edge_weight', 'L0_gnn_V', 'L0_gnn_w_comp', 'L0_gnn_loop_w', 'L0_gnn_bias',
          'L0_gnn_ffn_w', 'L0_gnn_ffn_b', 'L0_gnn_ln_g', 'L0_gnn_ln_b'] + [
              f'L1_gnn_{w}{k}{l}' for l in (1, 2) for k in 'qkvs' for w in 'Wb']


def kernel(**inputs):
    import numpy as np
    import concourse.bacc as bacc
    from concourse.bass_utils import run_bass_kernel_spmd

    nc = bacc.Bacc("TRN2", target_bir_lowering=False, num_devices=1)
    arrays, args = {}, {}
    for name in INPUTS:
        value = np.ascontiguousarray(inputs[name])
        arrays[f"in_{name}"] = value
        args[name] = nc.dram_tensor(f"in_{name}", value.shape, mybir.dt.from_np(value.dtype), kind="ExternalInput").ap()
    out = nc.dram_tensor("out", (NODES, D), F32, kind="ExternalOutput").ap()
    build(nc, args, out)
    return run_bass_kernel_spmd(nc, [arrays], core_ids=[0]).results[0]["out"]
```

```python
from contextlib import ExitStack

import concourse.bass as bass
from concourse import mybir

F32 = mybir.dt.float32
BF16 = mybir.dt.bfloat16
I32 = mybir.dt.int32
U32 = mybir.dt.uint32
ALU = mybir.AluOpType
ACT = mybir.ActivationFunctionType
AX = mybir.AxisListType

NODES, EDGES, D = 3125, 103125, 128
RELS, BASES = 8, 4
HEADS, HD = 2, 64
T = 25
R = NODES // T
EC = EDGES // R
SLOTS = 64
COLS = 34
PAD = COLS * 128
BLOCKS = -(-EDGES // 128)
PAIRS = 63
CW = 500
CH = 7
FIRST = 5
NEG = -1.0e30
FLOOR = -1.0e29
MAGIC = 12582912.0


def widths():
    return [min(CW, NODES - CW * j) for j in range(CH)]


class Steps:

    def __init__(self, eng, sem, done=0):
        self.eng, self.sem, self.done = eng, sem, done

    def __call__(self, ins):
        ins.then_inc(self.sem, 1)
        self.done = self.done + 1
        self.eng.wait_ge(self.sem, self.done)


def is_int(t):
    return isinstance(t, int)


def inside(t):
    return not is_int(t) or 0 <= t < T


def half(t, par):
    if is_int(t):
        return t // 2
    return (t - par) // 2


def wait(eng, sem, value):
    if not is_int(value) or value > 0:
        eng.wait_ge(sem, value)


def build(nc, a, out):
    ctx = ExitStack()
    with ctx:
        ctx.enter_context(nc.allow_non_contiguous_dma(reason="small transposed rows"))

        def dram(name, shape, dt):
            return nc.dram_tensor(name, shape, dt, kind="Internal").ap()

        m = {
            "rel_table": dram("rel_table", (RELS * NODES, D), F32),
            "records": dram("records", (EDGES + PAD, 3), F32),
            "sources": dram("sources", (EDGES + PAD, 2), F32),
            "messages": dram("messages", (BLOCKS, 128, D), F32),
            "x1": dram("x1", (NODES, D), F32),
            "bias": dram("bias", (T, 128, NODES), F32),
        }
        kept = ExitStack()
        with kept:
            def sb(name, shape, dt):
                return kept.enter_context(nc.sbuf_tensor(name, shape, dt))
            m["eye"] = sb("eye", [128, 128], F32)
            m["ones"] = sb("ones", [128, 128], F32)
            m["xT"] = sb("xT", [128, NODES], F32)
            m["ps"] = [kept.enter_context(nc.psum_tensor(f"ps{i}", [128, 512], F32)) for i in range(8)]
            m["loop_w"], m["loop_bias"] = sb("loop_w", [128, D + 1], F32), sb("loop_bias", [1, D + 1], F32)
            m["ffnT"], m["ffn_b"] = sb("ffnT", [D, D], F32), sb("ffn_b", [1, D], F32)
            m["ln_g"], m["ln_b"] = sb("ln_g", [R, D], F32), sb("ln_b", [R, D], F32)
            for layer in (1, 2):
                for c in "qvs":
                    m[f"W{c}{layer}"] = sb(f"W{c}{layer}", [D, D], F32)
                m[f"Wk{layer}"] = sb(f"Wk{layer}", [D, HEADS, 2, HD], F32)
                m[f"bq{layer}"], m[f"bk{layer}"] = sb(f"bq{layer}", [D, 1], F32), sb(f"bk{layer}", [D, HEADS], F32)
                m[f"bv{layer}"], m[f"bs{layer}"] = sb(f"bv{layer}", [1, D], F32), sb(f"bs{layer}", [1, D], F32)
            with ExitStack() as first:
                def sb1(name, shape, dt):
                    return first.enter_context(nc.sbuf_tensor(name, shape, dt))
                m["x"] = sb1("x_rows", [R, T, D], F32)
                m["h"] = sb1("h_rows", [R, T, D], F32)
                m["starts"] = sb1("starts", [128, T + 2], F32)
                m["flag"] = sb1("flag", [1, 1], I32)
                m["iota"] = sb1("iota", [128, 128], F32)
                prepare(nc, a, m)
                irregular = nc.values_load(m["flag"][0:1, 0:1], min_val=0, max_val=1)
                with nc.If(irregular):
                    message_any(nc, a, m)
                with nc.Else():
                    message(nc, a, m)
                first_norms(nc, a, m)
            m["hT"] = sb("hT", [128, NODES], F32)
            conv(nc, a, m, 1, None)
            conv(nc, a, m, 2, out)


def prepare(nc, a, m):
    ctx = ExitStack()
    with ctx:
        def sb(name, shape, dt):
            return ctx.enter_context(nc.sbuf_tensor(name, shape, dt))

        def sem(name):
            return ctx.enter_context(nc.semaphore(name))

        x, xT, eye, ones, ps = m["x"], m["xT"], m["eye"], m["ones"], m["ps"]
        V = sb("V", [128, BASES, D], F32)
        comp = sb("comp", [128, RELS * BASES], F32)
        W = sb("W", [128, RELS, D], F32)
        rows = sb("rel_rows", [128, 2, RELS, D], F32)
        si = sb("src_int", [R, EC], I32)
        di = sb("dst_int", [R, EC], I32)
        dn = sb("dst_next", [R, SLOTS], I32)
        ti = sb("type_int", [R, EC], I32)
        wf = sb("weight", [R, EC], F32)
        sf = sb("src_f", [R, EC], F32)
        df = sb("dst_f", [R, EC + SLOTS], F32)
        tf = sb("type_f", [R, EC], F32)
        cf = sb("chunk_f", [R, EC], F32)
        rec = sb("rec", [R, EC, 3], F32)
        srcs = sb("srcs", [R, EC, 2], F32)
        junk = sb("junk", [R, EC], F32)
        ffn = sb("ffn", [D, D], F32)
        f_in, f_ps, f_ok = sem("f_in"), sem("f_ps"), sem("f_ok")
        count = sb("count", [R, T + 4], F32)
        sizes = sb("sizes", [1, T], F32)
        large = sb("large", [1, 1], F32)
        bad = sb("bad", [1, 2], F32)
        pad_rec = sb("pad_rec", [128, COLS, 3], F32)
        pad_src = sb("pad_src", [128, COLS, 2], F32)

        x_in, v_in, w_in, e_in, n_in = sem("x_in"), sem("v_in"), sem("w_in"), sem("e_in"), sem("n_in")
        const, dve, sent = sem("const"), sem("dve_p"), sem("sent")
        xt_ps, xt_ok, w_ok = sem("xt_ps"), sem("xt_ok"), sem("w_ok")
        rel_ps, rel_a = sem("rel_ps"), sem("rel_a")
        rel_out = [sem("rel_out0"), sem("rel_out1")]
        rec_ok, src_ok, pad_ok, cnt_ok, cnt_ps = sem("rec_ok"), sem("src_ok"), sem("pad_ok"), sem("cnt_ok"), sem("cnt_ps")
        block = ctx.enter_context(nc.Block())
        groups = [(g, min(4, T - g)) for g in range(0, T, 4)]

        def load_constants(sp):
            def load(to, src):
                sp.dma_start(to, src).then_inc(w_in, 16)

            load(m["loop_w"][:, 0:D], a["L0_gnn_loop_w"])
            load(m["loop_bias"][:, 0:D], a["L0_gnn_bias"].rearrange("(a n) -> a n", a=1))
            sp.dma_start(ffn[:, :], a["L0_gnn_ffn_w"]).then_inc(f_in, 16)
            load(m["ffn_b"][:, :], a["L0_gnn_ffn_b"].rearrange("(a n) -> a n", a=1))
            load(m["ln_g"][:, :], a["L0_gnn_ln_g"].partition_broadcast(R))
            load(m["ln_b"][:, :], a["L0_gnn_ln_b"].partition_broadcast(R))
            for layer in (1, 2):
                for c in "qvs":
                    load(m[f"W{c}{layer}"][:, :], a[f"L1_gnn_W{c}{layer}"])
                for i in range(2):
                    load(m[f"Wk{layer}"][:, :, i, :], a[f"L1_gnn_Wk{layer}"].rearrange("f (h c) -> f h c", h=HEADS))
                    load(m[f"bk{layer}"][HD * i:HD * (i + 1), :], a[f"L1_gnn_bk{layer}"].rearrange("(h c) -> c h", h=HEADS))
                load(m[f"bq{layer}"][:, :], a[f"L1_gnn_bq{layer}"].rearrange("(n a) -> n a", a=1))
                for c in "vs":
                    load(m[f"b{c}{layer}"][:, :], a[f"L1_gnn_b{c}{layer}"].rearrange("(a n) -> a n", a=1))

        W_IN = 16 * (5 + 2 * 10)

        @block.sync
        def _(sp):
            sp.dma_start(x[:, :, :], a["x"].rearrange("(t p) f -> p t f", p=R)).then_inc(x_in, 16)
            sp.dma_start(V[:, :, :], a["L0_gnn_V"].rearrange("b i o -> i b o")).then_inc(v_in, 16)
            sp.dma_start(comp[:, :], a["L0_gnn_w_comp"].rearrange("r b -> (r b)").partition_broadcast(128)).then_inc(v_in, 16)
            sp.dma_start(di[:, :], a["dst"].rearrange("(p n) -> p n", n=EC)).then_inc(e_in, 16)
            sp.dma_start(dn[0:R - 1, :], a["dst"].rearrange("(p n) -> p n", n=EC)[1:R, 0:SLOTS]).then_inc(e_in, 16)
            sp.dma_start(si[:, :], a["src"].rearrange("(p n) -> p n", n=EC)).then_inc(n_in, 16)
            sp.dma_start(ti[:, :], a["edge_type_8"].rearrange("(p n) -> p n", n=EC)).then_inc(n_in, 16)
            sp.dma_start(wf[:, :], a["edge_weight"].rearrange("(p n) -> p n", n=EC)).then_inc(n_in, 16)
            load_constants(sp)
            table = m["rel_table"].rearrange("(r n) f -> n r f", r=RELS)
            for t in range(T):
                n = min(128, NODES - 128 * t)
                sp.wait_ge(rel_a, t + 1)
                sp.dma_start(table[128 * t:128 * t + n], rows[0:n, t % 2]).then_inc(rel_out[t % 2], 16)
            sp.wait_ge(w_in, W_IN)
            sp.wait_ge(rel_out[0], 16 * ((T + 1) // 2))
            sp.wait_ge(rel_out[1], 16 * (T // 2))

        @block.gpsimd
        def _(pool):
            nc.gpsimd.iota(m["iota"][:, :], pattern=[[1, 128]], base=0, channel_multiplier=0,
                           allow_small_or_imprecise_dtypes=True).then_inc(const, 1)
            nc.gpsimd.memset(ones[:, :], 1.0).then_inc(const, 1)
            pool.wait_ge(const, 2)
            nc.gpsimd.affine_select(out=eye[:, :], in_=ones[:, :], compare_op=ALU.is_equal, fill=0.0, base=0,
                                    pattern=[[-1, 128]], channel_multiplier=1).then_inc(const, 1)
            pool.wait_ge(pad_ok, 1)
            pool.dma_start(m["records"][EDGES:EDGES + PAD, :].rearrange("(p n) c -> p n c", p=128), pad_rec[:, :, :]).then_inc(sent, 16)
            pool.dma_start(m["sources"][EDGES:EDGES + PAD, :].rearrange("(p n) c -> p n c", p=128), pad_src[:, :, :]).then_inc(sent, 16)
            pool.wait_ge(rec_ok, 1)
            pool.dma_start(m["records"][0:EDGES, :].rearrange("(p n) c -> p n c", n=EC), rec[:, :, :]).then_inc(sent, 16)
            pool.wait_ge(src_ok, 1)
            pool.dma_start(m["sources"][0:EDGES, :].rearrange("(p n) c -> p n c", n=EC), srcs[:, :, :]).then_inc(sent, 16)
            pool.wait_ge(sent, 64)

        @block.tensor
        def _(pe):
            pe.wait_ge(x_in, 16)
            pe.wait_ge(const, 3)
            for n, (g, k) in enumerate(groups):
                if n >= 2:
                    pe.wait_ge(xt_ok, n - 1)
                for i in range(k):
                    last = nc.tensor.transpose(ps[n % 2][0:128, i * R:(i + 1) * R], x[:, g + i, :], eye[0:R, 0:R])
                last.then_inc(xt_ps, 1)
            pe.wait_ge(w_ok, 1)
            pe.wait_ge(xt_ok, len(groups))
            for t in range(T):
                n = min(128, NODES - 128 * t)
                if t >= 2:
                    pe.wait_ge(rel_a, t - 1)
                for h in range(2):
                    last = nc.tensor.matmul(ps[4 + 2 * (t % 2) + h][0:n, :], xT[:, 128 * t:128 * t + n],
                                            W[:, 4 * h:4 * h + 4, :], start=True, stop=True)
                last.then_inc(rel_ps, 1)
            pe.wait_ge(f_in, 16)
            nc.tensor.transpose(ps[3][:, 0:D], ffn[:, :], eye[:, :]).then_inc(f_ps, 1)
            pe.wait_ge(cnt_ok, 1)
            nc.tensor.matmul(ps[2][:, 0:T + 4], ones[0:R, 0:128], count[:, :], start=True, stop=True).then_inc(cnt_ps, 1)

        @block.scalar
        def _(act):
            for n, (g, k) in enumerate(groups):
                act.wait_ge(xt_ps, n + 1)
                nc.scalar.copy(xT[:, g * R:(g + k) * R], ps[n % 2][:, 0:k * R]).then_inc(xt_ok, 1)
            for t in range(T):
                act.wait_ge(rel_ps, t + 1)
                if t >= 2:
                    act.wait_ge(rel_out[t % 2], 16 * (t // 2))
                n = min(128, NODES - 128 * t)
                for h in range(2):
                    last = nc.scalar.copy(rows[0:n, t % 2, 4 * h:4 * h + 4, :],
                                          ps[4 + 2 * (t % 2) + h][0:n, :].rearrange("p (r f) -> p r f", f=D))
                last.then_inc(rel_a, 1)
            act.wait_ge(f_ps, 1)
            nc.scalar.copy(m["ffnT"][:, :], ps[3][:, 0:D]).then_inc(f_ok, 1)

        @block.vector
        def _(v):
            then = Steps(v, dve)
            V_ = nc.vector
            V_.memset(pad_rec[:, :, :], 0.0)
            V_.memset(count[:, :], 0.0)
            V_.memset(df[:, EC:EC + SLOTS], 1.0e6)
            then(V_.memset(pad_src[:, :, :], -512.0))
            V_.memset(pad_rec[:, :, 1:2], -1000.0).then_inc(pad_ok, 1)
            v.wait_ge(v_in, 32)
            for r in range(RELS):
                V_.tensor_scalar(W[:, r, :], V[:, 0, :], comp[:, BASES * r:BASES * r + 1], None, ALU.mult)
            then(V_.memset(bad[:, :], 0.0))
            for b in range(1, BASES):
                for r in range(RELS):
                    last = V_.scalar_tensor_tensor(W[:, r, :], V[:, b, :], comp[:, BASES * r + b:BASES * r + b + 1],
                                                   W[:, r, :], ALU.mult, ALU.add)
                    if r == RELS - 1 and b < BASES - 1:
                        then(last)
            last.then_inc(w_ok, 1)
            v.wait_ge(e_in, 32)
            V_.tensor_copy(df[:, 0:EC], di[:, :])
            then(V_.tensor_copy(df[0:R - 1, EC:EC + SLOTS], dn[0:R - 1, :]))
            for t in range(1, T + 1):
                then(V_.tensor_scalar(junk[:, :], df[:, 0:EC], float(R * t), None, ALU.is_lt, ALU.add, accum_out=count[:, t:t + 1]))
            then(V_.tensor_tensor(junk[:, :], df[:, 0:EC], df[:, 1:EC + 1], ALU.is_gt))
            then(V_.tensor_reduce(count[:, T + 2:T + 3], junk[:, :], AX.X, ALU.add))
            then(V_.tensor_tensor(junk[:, :], df[:, 0:EC], df[:, SLOTS:EC + SLOTS], ALU.is_equal))
            V_.tensor_reduce(count[:, T + 3:T + 4], junk[:, :], AX.X, ALU.add).then_inc(cnt_ok, 1)
            v.wait_ge(n_in, 48)
            V_.tensor_copy(sf[:, :], si[:, :])
            then(V_.tensor_copy(tf[:, :], ti[:, :]))
            V_.scalar_tensor_tensor(rec[:, :, 0], tf[:, :], float(NODES), sf[:, :], ALU.mult, ALU.add)
            V_.tensor_copy(rec[:, :, 1], df[:, 0:EC])
            V_.tensor_copy(rec[:, :, 2], wf[:, :]).then_inc(rec_ok, 1)
            then(V_.tensor_scalar(cf[:, :], sf[:, :], 1.0 / R, -0.496, ALU.mult, ALU.add))
            then(V_.tensor_scalar_add(cf[:, :], cf[:, :], MAGIC))
            then(V_.tensor_scalar_add(cf[:, :], cf[:, :], -MAGIC))
            V_.tensor_copy(srcs[:, :, 1], cf[:, :])
            V_.scalar_tensor_tensor(srcs[:, :, 0], cf[:, :], -float(R), sf[:, :], ALU.mult, ALU.add).then_inc(src_ok, 1)
            v.wait_ge(cnt_ps, 1)
            V_.tensor_copy(m["starts"][:, :], ps[2][:, 0:T + 2])
            then(V_.tensor_copy(bad[:, :], ps[2][0:1, T + 2:T + 4]))
            then(V_.tensor_tensor(sizes[:, :], m["starts"][0:1, 1:T + 1], m["starts"][0:1, 0:T], ALU.subtract))
            then(V_.tensor_scalar(sizes[:, :], sizes[:, :], float(PAD), None, ALU.is_gt))
            then(V_.tensor_reduce(large[:, :], sizes[:, :], AX.X, ALU.add))
            then(V_.tensor_tensor(bad[:, 0:1], bad[:, 0:1], bad[:, 1:2], ALU.add))
            then(V_.tensor_tensor(bad[:, 0:1], bad[:, 0:1], large[:, :], ALU.add))
            then(V_.tensor_scalar(m["flag"][:, :], bad[:, 0:1], 0.0, None, ALU.is_gt))


def message(nc, a, m):
    ctx = ExitStack()
    with ctx:
        def sb(name, shape, dt):
            return ctx.enter_context(nc.sbuf_tensor(name, shape, dt))

        def sem(name):
            return ctx.enter_context(nc.semaphore(name))

        h, xT, eye, ones, iota, starts, ps = (m[k] for k in ("h", "xT", "eye", "ones", "iota", "starts", "ps"))
        G = sb("gathered", [128, 2, COLS, D + 1], F32)
        A = sb("dst_onehot", [128, 2, COLS, R], F32)
        win = [sb(f"window{i}", [128, COLS * 3], F32) for i in range(2)]
        widx = [sb(f"window_at{i}", [128, 1], U32) for i in range(2)]
        rel = [sb(f"rel_at{i}", [128, COLS], U32) for i in range(2)]
        ell = [sb(f"slots{i}", [64, 2, SLOTS * 2], F32) for i in range(2)]
        eidx = [sb(f"slots_at{i}", [64, 2], U32) for i in range(2)]
        deg = [sb(f"degree{i}", [R, 1], F32) for i in range(2)]
        xt = [sb(f"xT_tile{i}", [128, R], F32) for i in range(2)]
        dab = [sb(f"degree_ab{i}", [64, 2], F32) for i in range(2)]
        start = sb("tile_start", [64, 1], F32)
        lane = sb("lane", [128, 1], F32)
        nodes = sb("tile_nodes", [128, R], F32)
        tri = sb("tri", [128, 4, 64], F32)
        loopw, lbias = m["loop_w"], m["loop_bias"]
        off = sb("unused", [64, 2, SLOTS], F32)
        codes = sb("codes", [128, 2, 2, SLOTS], F32)
        codesT = sb("codesT", [128, 2, 64], BF16)
        iob = sb("iota_b", [128, 128], BF16)
        L = sb("low_onehot", [128, PAIRS, R], BF16)
        H = sb("high_onehot", [128, PAIRS, 2 * T], BF16)
        CT = sb("countsT", [R, T, 2 * PAIRS], F32)
        bias = [sb(f"bias{i}", [128, NODES], F32) for i in range(2)]
        lns = [sb(f"ln{i}", [R, CW], F32) for i in range(2)]
        tiny = sb("tiny", [128, 1], F32)
        spare = sb("spare", [128, 1], F32)

        psA, psS, psC, psT, psK = ps[0:2], ps[2], ps[3:5], ps[5:7], ps[7]
        const, dve, gps = sem("m_const"), sem("dve_m"), sem("pool_m")
        at_ok, rel_ok, hot_ok, scaled = sem("at_ok"), sem("rel_ok"), sem("hot_ok"), sem("scaled")
        win_in = [sem("win_in0"), sem("win_in1")]
        g_in = [sem("g_in0"), sem("g_in1")]
        ell_in = [sem("ell_in0"), sem("ell_in1")]
        out_ok = [sem("bias_out0"), sem("bias_out1")]
        xt_ok, agg, deg_ok, st_ok, eidx_ok = sem("xt_ok_m"), sem("agg"), sem("deg_ok"), sem("st_ok"), sem("eidx_ok")
        codes_ok, codes_ps, lh_ok = sem("codes_ok"), sem("codes_ps"), sem("lh_ok")
        c_ps, c_ok, t_ps, ln_ok, masked, bias_ok = (sem("c_ps"), sem("c_ok"), sem("t_ps"), sem("ln_ok"), sem("masked"),
                                                    sem("bias_ok"))
        WINDOW_AFTER, SLOTS_AFTER = COLS // 2, COLS - 6
        pairs = [min(10, PAIRS - 10 * j) for j in range(CH)]
        cw = widths()
        block = ctx.enter_context(nc.Block())

        @block.gpsimd
        def _(pool):
            settled = Steps(pool, gps, 1)

            def settle():
                pool.wait_ge(gps, settled.done)
                nc.gpsimd.tensor_tensor(spare[:, :], lane[:, :], lane[:, :], ALU.add).then_inc(gps, 1)
                settled.done = settled.done + 1

            def window(t, par):
                pool.wait_ge(at_ok, t + 1)
                if not is_int(t) or t >= 2:
                    pool.wait_ge(hot_ok, t - 1)
                    pool.wait_ge(scaled, t - 1)
                settle()
                nc.gpsimd.indirect_dma_start(out=win[par][:, :], out_offset=None, in_=m["records"],
                                             in_offset=bass.IndirectOffsetOnAxis(ap=widx[par][:, :], axis=0)).then_inc(win_in[par], 16)

            nc.gpsimd.iota(lane[:, :], pattern=[[0, 1]], base=0, channel_multiplier=COLS,
                           allow_small_or_imprecise_dtypes=True).then_inc(gps, 1)
            pool.wait_ge(gps, 1)
            window(0, 0)
            nc.gpsimd.memset(tri[:, :, :], 1.0).then_inc(gps, 1)
            pool.wait_ge(gps, 3)
            for q in range(2):
                nc.gpsimd.affine_select(out=tri[:, q, :], in_=tri[:, q, :], compare_op=ALU.is_gt, fill=0.0,
                                        base=PAIRS * q, pattern=[[1, 64]], channel_multiplier=-1)
                nc.gpsimd.affine_select(out=tri[:, 2 + q, :], in_=tri[:, 2 + q, :], compare_op=ALU.is_equal, fill=0.0,
                                        base=PAIRS * q, pattern=[[1, 64]], channel_multiplier=-1).then_inc(gps, 1)
            pool.wait_ge(gps, 5)
            nc.gpsimd.memset(tri[:, 2, PAIRS:64], 0.0).then_inc(const, 1)

            def slots(u, par):
                pool.wait_ge(eidx_ok, u + 1)
                if not is_int(u) or u >= 2:
                    pool.wait_ge(codes_ok, u - 1)
                settle()
                for q in range(2):
                    nc.gpsimd.indirect_dma_start(out=ell[par][:, q, :], out_offset=None, in_=m["sources"],
                                                 in_offset=bass.IndirectOffsetOnAxis(ap=eidx[par][:, q:q + 1], axis=0)).then_inc(ell_in[par], 16)

            def step(t, par):
                settled.done = 4 + (1 + 2 * min(t, T) + max(0, t - 1) if is_int(t) else t * 3)
                if inside(t):
                    pool.wait_ge(rel_ok, t + 1)
                    if not is_int(t) or t >= 2:
                        pool.wait_ge(agg, t - 1)
                    settle()
                    for j in range(COLS):
                        nc.gpsimd.indirect_dma_start(out=G[:, par, j, 0:D], out_offset=None, in_=m["rel_table"],
                                                     in_offset=bass.IndirectOffsetOnAxis(ap=rel[par][:, j:j + 1], axis=0)).then_inc(g_in[par], 16)
                        if j == WINDOW_AFTER and (not is_int(t) or t + 1 < T):
                            window(t + 1, 1 - par)
                        if j == SLOTS_AFTER and inside(t - 1):
                            slots(t - 1, 1 - par)
                elif inside(t - 1):
                    slots(t - 1, 1 - par)

            pipeline_loop(pool, step)
            pool.wait_ge(win_in[T % 2], 16 * ((T + 1) // 2))

        @block.sync
        def _(sp):
            sp.wait_ge(const, 2)

            def step(t, par):
                v = t - 2
                if inside(v):
                    sp.wait_ge(bias_ok, (v + 1) * CH)
                    sp.dma_start(m["bias"][bass.ds(v, 1), :, :].rearrange("a p n -> (a p) n"), bias[par][:, :]).then_inc(out_ok[par], 16)
            pipeline_loop(sp, step)
            sp.wait_ge(out_ok[0], 16 * ((T + 1) // 2))
            sp.wait_ge(out_ok[1], 16 * (T // 2))

        @block.vector
        def _(v_):
            def window_at(t, par):
                nc.vector.tensor_tensor(widx[par][:, :], starts[:, bass.ds(t, 1)], lane[:, :], ALU.add).then_inc(at_ok, 1)

            V = nc.vector
            v_.wait_ge(gps, 1)
            window_at(0, 0)
            window_at(1, 1)
            V.memset(G[:, :, :, D:D + 1], 1.0)
            V.memset(loopw[:, D:D + 1], 0.0)
            V.memset(lbias[:, D:D + 1], 0.0)
            V.memset(tiny[:, :], 1.0e-37)
            V.memset(bias[0][96:128, :], 0.0)
            V.memset(bias[1][96:128, :], 0.0)
            V.memset(codes[64:128, :, :, :], 0.0)
            V.tensor_copy(iob[:, :], iota[:, :])
            V.engine_nop().then_inc(const, 1)
            V.tensor_copy(nodes[:, :], iota[:, 0:R]).then_inc(dve, 1)
            v_.wait_ge(dve, 1)
            v_.wait_ge(const, 2)

            def rows_at(t, par):
                v_.wait_ge(win_in[par], (half(t, par) + 1) * 16)
                if not is_int(t) or t >= 2:
                    v_.wait_ge(g_in[par], half(t, par) * (16 * COLS))
                V.tensor_copy(rel[par][:, :], win[par].rearrange("p (j c) -> p j c", c=3)[:, :, 0]).then_inc(rel_ok, 1)

            def main(t, par, then):
                v_.wait_ge(win_in[par], (half(t, par) + 1) * 16)
                if not is_int(t) or t + 2 < T:
                    window_at(t + 2, par)
                w3 = win[par].rearrange("p (j c) -> p j c", c=3)
                if not is_int(t) or t >= 2:
                    v_.wait_ge(agg, t - 1)
                V.tensor_tensor(A[:, par, :, :], nodes[:, :].unsqueeze(1).to_broadcast([128, COLS, R]),
                                w3[:, :, 1:2].to_broadcast([128, COLS, R]), ALU.is_equal).then_inc(hot_ok, 1)
                v_.wait_ge(hot_ok, t + 1)
                then(V.tensor_scalar_add(nodes[:, :], nodes[:, :], float(R)))

            def onehots(v, par, then):
                v_.wait_ge(ell_in[par], (half(v, par) + 1) * 32)
                wait(v_, codes_ok, v)
                for q in range(2):
                    last = V.tensor_scalar(off[:, q, :], iota[0:64, 0:SLOTS], dab[par][:, q:q + 1], -512.0, ALU.is_ge, ALU.mult)
                then(last)
                slot = ell[par].rearrange("p q (s c) -> p q s c", c=2)
                V.tensor_tensor(codes[0:64, 0, :, :], slot[:, :, :, 0], off[:, :, :], ALU.add)
                V.tensor_tensor(codes[0:64, 1, 0, :], slot[:, 0, :, 1], off[:, 0, :], ALU.add)
                V.scalar_tensor_tensor(codes[0:64, 1, 1, :], slot[:, 1, :, 1], float(T), off[:, 1, :], ALU.add, ALU.add).then_inc(codes_ok, 1)
                v_.wait_ge(codes_ps, v + 1)
                wait(v_, lh_ok, v)
                then(V.tensor_copy(codesT[:, :, :], psK[:, 0:256].rearrange("p (k n) -> p k n", k=2)[:, :, 0:64]))
                if not is_int(v) or v >= 1:
                    v_.wait_ge(c_ps, v * CH)
                V.tensor_tensor(L[:, :, :], iob[:, 0:R].unsqueeze(1).to_broadcast([128, PAIRS, R]),
                                codesT[:, 0, 0:PAIRS].unsqueeze(2).to_broadcast([128, PAIRS, R]), ALU.is_equal)
                V.tensor_tensor(H[:, :, :], iob[:, 0:2 * T].unsqueeze(1).to_broadcast([128, PAIRS, 2 * T]),
                                codesT[:, 1, 0:PAIRS].unsqueeze(2).to_broadcast([128, PAIRS, 2 * T]), ALU.is_equal).then_inc(lh_ok, 1)

            def sums(u, par, then):
                v_.wait_ge(agg, u + 1)
                V.tensor_scalar_max(h[:, bass.ds(u, 1), :].rearrange("p a f -> p (a f)"), psA[par][0:R, 0:D], 0.0)
                wait(v_, eidx_ok, u)
                V.tensor_copy(start[:, :], starts[0:64, bass.ds(u, 1)])
                V.tensor_copy(deg[par][:, :], psA[par][0:R, D:D + 1]).then_inc(deg_ok, 1)
                v_.wait_ge(deg_ok, u + 1)
                v_.wait_ge(st_ok, u + 1)
                if not is_int(u) or u >= 2:
                    v_.wait_ge(ell_in[par], half(u, par) * 32)
                V.tensor_copy(dab[par][:, :], psS[0:64, 2:4])
                V.tensor_scalar(eidx[par][:, :], psS[0:64, 0:2], start[:, :], None, ALU.add).then_inc(eidx_ok, 1)

            def bias_rows(v, par, then):
                if not is_int(v) or v >= 2:
                    v_.wait_ge(out_ok[par], half(v, par) * 16)
                for j in range(CH):
                    n = v * CH + j
                    row = bias[par][0:R, CW * j:CW * j + cw[j]]
                    v_.wait_ge(ln_ok, n + 1)
                    V.tensor_scalar(row, psT[(par + j) % 2][0:R, 0:cw[j]], 0.0, NEG, ALU.is_equal, ALU.mult).then_inc(masked, 1)
                    v_.wait_ge(masked, n + 1)
                    V.tensor_tensor(row, row, lns[(par + j) % 2][:, 0:cw[j]], ALU.add).then_inc(bias_ok, 1)

            def step(t, par):
                base = 1 + min(t, T) + 2 * max(0, t - 2) if is_int(t) else 3 * t - 3
                then = Steps(v_, dve, base)
                if inside(t - 2):
                    onehots(t - 2, par, then)
                if inside(t):
                    main(t, par, then)
                if inside(t - 1):
                    sums(t - 1, 1 - par, then)
                if inside(t + 1):
                    rows_at(t + 1, 1 - par)
                if inside(t - 2):
                    bias_rows(t - 2, par, then)

            rows_at(0, 0)
            pipeline_loop(v_, step)

        @block.tensor
        def _(pe):
            pe.wait_ge(const, 2)

            def step(t, par):
                v, u = t - 2, t - 1
                if inside(v):
                    pe.wait_ge(codes_ok, v + 1)
                    for k in range(2):
                        last = nc.tensor.transpose(psK[:, 128 * k:128 * (k + 1)], codes[:, k].rearrange("p q s -> p (q s)"),
                                                   eye[:, :])
                    last.then_inc(codes_ps, 1)
                if inside(u):
                    pe.wait_ge(xt_ok, u + 1)
                    if not is_int(u) or u >= 2:
                        pe.wait_ge(deg_ok, u - 1)
                    acc = psA[1 - par][0:R, 0:D + 1]
                    nc.tensor.matmul(acc, xt[1 - par][:, :], loopw[:, :], start=True, stop=False)
                    nc.tensor.matmul(acc, ones[0:1, 0:R], lbias[:, :], start=False, stop=False)
                    pe.wait_ge(hot_ok, u + 1)
                    pe.wait_ge(scaled, u + 1)
                    for j in range(COLS):
                        last = nc.tensor.matmul(acc, A[:, 1 - par, j, :], G[:, 1 - par, j, :], start=False, stop=(j == COLS - 1))
                    last.then_inc(agg, 1)
                if inside(u):
                    pe.wait_ge(deg_ok, u + 1)
                    for q in range(4):
                        last = nc.tensor.matmul(psS[0:64, q:q + 1], tri[0:R, q, :], deg[1 - par][:, :], start=True, stop=True)
                    last.then_inc(st_ok, 1)
                if inside(v):
                    pe.wait_ge(lh_ok, v + 1)
                    for j in range(CH):
                        if not is_int(v) or v * CH + j >= 2:
                            pe.wait_ge(c_ok, v * CH + j - 1)
                        for i in range(pairs[j]):
                            p = 10 * j + i
                            last = nc.tensor.matmul(psC[(par + j) % 2][0:R, 2 * T * i:2 * T * (i + 1)], L[:, p, :], H[:, p, :],
                                                    start=True, stop=True)
                        last.then_inc(c_ps, 1)
                if inside(v):
                    pe.wait_ge(c_ok, v * CH + CH)
                    for j in range(CH):
                        if not is_int(v) or v * CH + j >= 2:
                            pe.wait_ge(ln_ok, v * CH + j - 1)
                            pe.wait_ge(masked, v * CH + j - 1)
                        for i in range(cw[j] // R):
                            last = nc.tensor.transpose(psT[(par + j) % 2][0:R, R * i:R * (i + 1)], CT[:, 4 * j + i, 0:R], eye[0:R, 0:R])
                        last.then_inc(t_ps, 1)
            pipeline_loop(pe, step)

        @block.scalar
        def _(act):
            def step(t, par):
                v, u, up = t - 2, t - 1, 1 - par
                if inside(u):
                    if not is_int(u) or u >= 2:
                        act.wait_ge(agg, u - 1)
                    nc.scalar.copy(xt[up][:, :], xT[:, bass.ds(u * R, R)]).then_inc(xt_ok, 1)
                    act.wait_ge(g_in[up], (half(u, up) + 1) * (16 * COLS))
                    for j in range(COLS):
                        last = nc.scalar.mul(G[:, up, j, 0:D], G[:, up, j, 0:D], win[up][:, 3 * j + 2:3 * j + 3])
                    last.then_inc(scaled, 1)
                if inside(v):
                    if not is_int(v) or v >= 1:
                        act.wait_ge(t_ps, v * CH)
                    for j in range(CH):
                        act.wait_ge(c_ps, v * CH + j + 1)
                        k = pairs[j]
                        for q in range(2):
                            src = psC[(par + j) % 2][0:R, 0:2 * T * k].rearrange("p (i q c) -> p i q c", i=k, q=2)[:, :, q, :]
                            dst = CT[:, :, PAIRS * q + 10 * j:PAIRS * q + 10 * j + k].rearrange("p c i -> p i c")
                            last = nc.scalar.copy(dst, src)
                        last.then_inc(c_ok, 1)
                    for j in range(CH):
                        n = v * CH + j
                        act.wait_ge(t_ps, n + 1)
                        if not is_int(v) or n >= 2:
                            act.wait_ge(bias_ok, n - 1)
                        nc.scalar.activation(lns[(par + j) % 2][:, 0:cw[j]], psT[(par + j) % 2][0:R, 0:cw[j]], ACT.Ln,
                                             bias=tiny[0:R, :]).then_inc(ln_ok, 1)
            act.wait_ge(const, 2)
            pipeline_loop(act, step)


def message_any(nc, a, m):
    ctx = ExitStack()
    with ctx:
        def sb(name, shape, dt):
            return ctx.enter_context(nc.sbuf_tensor(f"{name}_any", shape, dt))

        def sem(name):
            return ctx.enter_context(nc.semaphore(f"{name}_any"))

        h, xT, ones, iota, ps = (m[k] for k in ("h", "xT", "ones", "iota", "ps"))
        edges = sb("edges", [128, BLOCKS, 3], F32)
        lohi = sb("lohi", [128, BLOCKS, 2], F32)
        srcs = sb("srcs", [128, BLOCKS, 1], F32)
        cur = sb("edge_now", [128, 4], F32)
        at = sb("rel_at", [128, 1], U32)
        G = sb("gathered", [128, D], F32)
        A = sb("dst_onehot", [128, R], F32)
        Ab = sb("dst_onehot_b", [128, R], BF16)
        B = sb("src_onehot", [128, NODES], BF16)
        every = sb("all_nodes", [128, NODES], F32)
        nodes = sb("tile_nodes", [128, R], F32)
        xt = sb("xT_tile", [128, R], F32)
        zero = sb("zero", [1, CW], F32)
        loopw, lbias = m["loop_w"][:, 0:D], m["loop_bias"][:, 0:D]
        lns = sb("ln", [R, NODES], F32)
        rows = sb("bias_rows", [128, NODES], F32)
        tiny = sb("tiny", [128, 1], F32)
        spare = sb("spare", [128, 1], F32)
        names = ("e_in", "iota_ok", "dve", "at_ok", "settled", "g_in", "stored", "m_in", "summed", "xt_ok", "ln_ok", "bias_out")
        z = {n: sem(n) for n in names}
        cw = widths()
        SUMS = BLOCKS + 2
        CHAIN = 4 * BLOCKS + 3
        block = ctx.enter_context(nc.Block())

        @block.sync
        def _(sp):
            n = 128 * BLOCKS
            sp.dma_start(edges[:, :, :], m["records"][0:n, :].rearrange("(p n) c -> p n c", p=128)).then_inc(z["e_in"], 16)
            sp.dma_start(lohi[:, :, :], m["sources"][0:n, :].rearrange("(p n) c -> p n c", p=128)).then_inc(z["e_in"], 16)
            with sp.Fori(0, BLOCKS) as b:
                sp.wait_ge(z["g_in"], (b + 1) * 16)
                sp.dma_start(m["messages"][bass.ds(b, 1), :, :].rearrange("a p f -> (a p) f"), G[:, :]).then_inc(z["stored"], 16)
            sp.wait_ge(z["stored"], 16 * (BLOCKS + 1))
            with sp.Fori(0, T) as t:
                with sp.Fori(0, BLOCKS) as b:
                    sp.wait_ge(z["summed"], t * SUMS + b + 1)
                    sp.dma_start(G[:, :], m["messages"][bass.ds(b, 1), :, :].rearrange("a p f -> (a p) f")).then_inc(z["m_in"], 16)
                sp.wait_ge(z["dve"], 1 + (t + 1) * CHAIN)
                sp.dma_start(m["bias"][bass.ds(t, 1), :, :].rearrange("a p n -> (a p) n"), rows[:, :]).then_inc(z["bias_out"], 16)
            sp.wait_ge(z["bias_out"], 16 * (T + 1))

        @block.gpsimd
        def _(pool):
            nc.gpsimd.iota(every[:, :], pattern=[[1, NODES]], base=0, channel_multiplier=0,
                           allow_small_or_imprecise_dtypes=True).then_inc(z["iota_ok"], 1)
            nc.gpsimd.memset(spare[:, :], 0.0).then_inc(z["settled"], 1)
            with pool.Fori(0, BLOCKS) as b:
                pool.wait_ge(z["at_ok"], b + 1)
                pool.wait_ge(z["settled"], b + 1)
                nc.gpsimd.tensor_tensor(spare[:, :], spare[:, :], spare[:, :], ALU.add).then_inc(z["settled"], 1)
                nc.gpsimd.indirect_dma_start(out=G[:, :], out_offset=None, in_=m["rel_table"],
                                             in_offset=bass.IndirectOffsetOnAxis(ap=at[:, :], axis=0)).then_inc(z["g_in"], 16)

        @block.scalar
        def _(act):
            with act.Fori(0, T) as t:
                act.wait_ge(z["dve"], 1 + t * CHAIN)
                nc.scalar.copy(xt[:, :], xT[:, bass.ds(t * R, R)]).then_inc(z["xt_ok"], 1)
                act.wait_ge(z["summed"], (t + 1) * SUMS)
                for j in range(CH):
                    last = nc.scalar.activation(lns[:, CW * j:CW * j + cw[j]], ps[j][0:R, 0:cw[j]], ACT.Ln, bias=tiny[0:R, :])
                last.then_inc(z["ln_ok"], 1)

        @block.tensor
        def _(pe):
            pe.wait_ge(z["e_in"], 32)
            with pe.Fori(0, T) as t:
                pe.wait_ge(z["dve"], 1 + t * CHAIN)
                pe.wait_ge(z["xt_ok"], t + 1)
                nc.tensor.matmul(ps[CH][0:R, 0:D], xt[:, :], loopw[:, :], start=True, stop=False)
                nc.tensor.matmul(ps[CH][0:R, 0:D], ones[0:1, 0:R], lbias[:, :], start=False, stop=False)
                for j in range(CH):
                    last = nc.tensor.matmul(ps[j][0:R, 0:cw[j]], zero[:, 0:R], zero[:, 0:cw[j]], start=True, stop=False)
                last.then_inc(z["summed"], 1)
                with pe.Fori(0, BLOCKS) as b:
                    pe.wait_ge(z["dve"], 1 + t * CHAIN + (b + 1) * 4)
                    nc.tensor.matmul(ps[CH][0:R, 0:D], A[:, :], G[:, :], start=False, stop=False)
                    for j in range(CH):
                        last = nc.tensor.matmul(ps[j][0:R, 0:cw[j]], Ab[:, :], B[:, CW * j:CW * j + cw[j]], start=False, stop=False)
                    last.then_inc(z["summed"], 1)
                nc.tensor.matmul(ps[CH][0:R, 0:D], zero[:, 0:R], zero[:, 0:D], start=False, stop=True)
                for j in range(CH):
                    last = nc.tensor.matmul(ps[j][0:R, 0:cw[j]], zero[:, 0:R], zero[:, 0:cw[j]], start=False, stop=True)
                last.then_inc(z["summed"], 1)

        @block.vector
        def _(v):
            V = nc.vector
            V.memset(tiny[:, :], 1.0e-37)
            V.memset(zero[:, :], 0.0)
            V.memset(rows[96:128, :], 0.0)
            V.tensor_copy(nodes[:, :], iota[:, 0:R])
            v.wait_ge(z["e_in"], 32)
            v.wait_ge(z["iota_ok"], 1)
            V.scalar_tensor_tensor(srcs[:, :, 0], lohi[:, :, 1], float(R), lohi[:, :, 0], ALU.mult, ALU.add).then_inc(z["dve"], 1)
            v.wait_ge(z["dve"], 1)
            V.engine_nop().then_inc(z["bias_out"], 16)
            V.engine_nop().then_inc(z["stored"], 16)
            with v.Fori(0, BLOCKS) as b:
                v.wait_ge(z["stored"], (b + 1) * 16)
                V.tensor_copy(at[:, :], edges[:, bass.ds(b, 1), 0:1].rearrange("p a c -> p (a c)")).then_inc(z["at_ok"], 1)
            with v.Fori(0, T) as t:
                with v.Fori(0, BLOCKS) as b:
                    then = Steps(v, z["dve"], 1 + t * CHAIN + b * 4)
                    v.wait_ge(z["summed"], t * SUMS + b + 1)
                    V.tensor_copy(cur[:, 0:3], edges[:, bass.ds(b, 1), :].rearrange("p a c -> p (a c)"))
                    then(V.tensor_copy(cur[:, 3:4], srcs[:, bass.ds(b, 1), :].rearrange("p a c -> p (a c)")))
                    V.tensor_scalar(B[:, :], every[:, :], cur[:, 3:4], None, ALU.is_equal)
                    then(V.tensor_scalar(A[:, :], nodes[:, :], cur[:, 1:2], None, ALU.is_equal))
                    then(V.tensor_copy(Ab[:, :], A[:, :]))
                    v.wait_ge(z["m_in"], (t * BLOCKS + b + 1) * 16)
                    then(V.tensor_scalar(G[:, :], G[:, :], cur[:, 2:3], None, ALU.mult))
                then = Steps(v, z["dve"], 1 + t * CHAIN + 4 * BLOCKS)
                v.wait_ge(z["summed"], (t + 1) * SUMS)
                v.wait_ge(z["ln_ok"], t + 1)
                v.wait_ge(z["bias_out"], 16 * (t + 1))
                V.tensor_scalar_max(h[:, bass.ds(t, 1), :].rearrange("p a f -> p (a f)"), ps[CH][0:R, 0:D], 0.0)
                for j in range(CH):
                    last = V.tensor_scalar(rows[0:R, CW * j:CW * j + cw[j]], ps[j][0:R, 0:cw[j]], 0.0, NEG, ALU.is_equal, ALU.mult)
                then(last)
                then(V.tensor_tensor(rows[0:R, :], rows[0:R, :], lns[:, :], ALU.add))
                then(V.tensor_scalar_add(nodes[:, :], nodes[:, :], float(R)))


def pipeline_loop(eng, step):
    for t in range(FIRST):
        step(t, t % 2)
    with eng.Fori(0, (T - FIRST) // 2) as k:
        step(k * 2 + FIRST, FIRST % 2)
        step(k * 2 + FIRST + 1, (FIRST + 1) % 2)
    for t in range(T, T + 2):
        step(t, t % 2)


def first_norms(nc, a, m):
    ctx = ExitStack()
    with ctx:
        def sb(name, shape, dt):
            return ctx.enter_context(nc.sbuf_tensor(name, shape, dt))

        def sem(name):
            return ctx.enter_context(nc.semaphore(name))

        x, xT, h, eye, ones, ps = m["x"], m["xT"], m["h"], m["eye"], m["ones"], m["ps"]
        ffnT, ffnb, gain, shift = m["ffnT"], m["ffn_b"], m["ln_g"], m["ln_b"]
        hT = [sb(f"hT{i}", [D, 4 * R], F32) for i in range(2)]
        y = sb("y_rows", [R, T, D], F32)
        shifted = sb("x_shifted", [R, T, D], F32)
        stats = [sb(f"stats{i}", [R, T, 6], F32) for i in range(2)]
        mean = [sb(f"mean{i}", [R, T, 2], F32) for i in range(2)]
        rstd = [sb(f"rstd{i}", [R, T, 1], F32) for i in range(2)]
        half_power = sb("minus_half", [R, 4, 1], F32)
        dve, h_ps, h_ok, y_ps, y_ok, x_ok, t_ps, t_ok, asked, rooted, half_ok, shift_ok, kept = (
            sem("f_" + n) for n in ("dve", "h_ps", "h_ok", "y_ps", "y_ok", "x_ok", "t_ps", "t_ok", "asked", "rooted",
                                    "half_ok", "shift_ok", "kept"))
        groups = [(g, min(4, T - g)) for g in range(0, T, 4)]
        N = len(groups)
        stages = [(i, n - i) for n in range(N + 2) for i in range(3) if 0 <= n - i < N]
        powers = [s for s in stages if s[0] < 2]
        block = ctx.enter_context(nc.Block())

        @block.sync
        def _(sp):
            for n, (g, k) in enumerate(groups):
                sp.wait_ge(x_ok, n + 1)
                sp.dma_start(m["x1"].rearrange("(t p) f -> p t f", p=R)[:, g:g + k, :], x[:, g:g + k, :]).then_inc(kept, 16)
            sp.wait_ge(kept, 16 * N)

        @block.gpsimd
        def _(pool):
            nc.gpsimd.memset(half_power[:, :, :], -0.5).then_inc(half_ok, 1)
            pool.wait_ge(half_ok, 1)
            for i, (which, n) in enumerate(powers):
                g, k = groups[n]
                if which == 0:
                    nc.gpsimd.tensor_tensor(shifted[:, g:g + k, :], x[:, g:g + k, :],
                                            shift[:, :].unsqueeze(1).to_broadcast([R, k, D]), ALU.add).then_inc(shift_ok, 1)
                pool.wait_ge(asked, i + 1)
                r = rstd[which][:, g:g + k, :]
                nc.gpsimd.tensor_tensor(r, r, half_power[:, 0:k, :], ALU.pow).then_inc(rooted, 1)

        @block.tensor
        def _(pe):
            def turn_h(n):
                g, k = groups[n]
                if n >= 2:
                    pe.wait_ge(h_ok, n - 1)
                for i in range(k):
                    last = nc.tensor.transpose(ps[n % 2][:, i * R:(i + 1) * R], h[:, g + i, :], eye[0:R, 0:R])
                last.then_inc(h_ps, 1)

            def turn_x(n):
                g, k = groups[n]
                pe.wait_ge(x_ok, n + 1)
                if n >= 2:
                    pe.wait_ge(t_ok, n - 1)
                for i in range(k):
                    last = nc.tensor.transpose(ps[4 + n % 2][:, i * R:(i + 1) * R], x[:, g + i, :], eye[0:R, 0:R])
                last.then_inc(t_ps, 1)

            turn_h(0)
            for n, (g, k) in enumerate(groups):
                if n + 1 < N:
                    turn_h(n + 1)
                pe.wait_ge(h_ok, n + 1)
                if n >= 2:
                    pe.wait_ge(y_ok, n - 1)
                for i in range(k):
                    to = ps[2 + n % 2][0:R, i * D:(i + 1) * D]
                    nc.tensor.matmul(to, ones[0:1, 0:R], ffnb[:, :], start=True, stop=False)
                    last = nc.tensor.matmul(to, hT[n % 2][:, i * R:(i + 1) * R], ffnT[:, :], start=False, stop=True)
                last.then_inc(y_ps, 1)
                if n >= 4:
                    turn_x(n - 4)
            for n in range(N - 4, N):
                turn_x(n)

        @block.scalar
        def _(act):
            def turn(n):
                g, k = groups[n]
                act.wait_ge(t_ps, n + 1)
                nc.scalar.copy(xT[:, g * R:(g + k) * R], ps[4 + n % 2][:, 0:k * R]).then_inc(t_ok, 1)

            for n, (g, k) in enumerate(groups):
                act.wait_ge(h_ps, n + 1)
                if n >= 2:
                    act.wait_ge(y_ps, n - 1)
                nc.scalar.copy(hT[n % 2][:, 0:k * R], ps[n % 2][:, 0:k * R]).then_inc(h_ok, 1)
                if n >= 5:
                    turn(n - 5)
            for n in range(N - 5, N):
                turn(n)

        @block.vector
        def _(v):
            then = Steps(v, dve)
            V = nc.vector

            def moments(rows, which, n, eps):
                g, k = groups[n]
                for i in range(k):
                    last = V.bn_stats(stats[which][:, g + i, :], rows[:, g + i, :])
                then(last)
                for i in range(k):
                    last = V.bn_aggr(mean[which][:, g + i, :], stats[which][:, g + i, :])
                then(last)
                V.tensor_scalar_add(rstd[which][:, g:g + k, :], mean[which][:, g:g + k, 1:2], eps).then_inc(asked, 1)

            for stage, n in stages:
                g, k = groups[n]
                if stage > 0:
                    v.wait_ge(rooted, powers.index((stage - 1, n)) + 1)
                if stage == 0:
                    v.wait_ge(y_ps, n + 1)
                    V.tensor_tensor(y[:, g:g + k, :], ps[2 + n % 2][0:R, 0:k * D].rearrange("p (t f) -> p t f", f=D),
                                    x[:, g:g + k, :], ALU.add).then_inc(y_ok, 1)
                    v.wait_ge(y_ok, n + 1)
                    moments(y, 0, n, 1.0e-8)
                elif stage == 1:
                    v.wait_ge(shift_ok, n + 1)
                    for i in range(g, g + k):
                        last = V.scalar_tensor_tensor(y[:, i, :], y[:, i, :], mean[0][:, i, 0:1], gain[:, :], ALU.subtract, ALU.mult)
                    then(last)
                    for i in range(g, g + k):
                        last = V.scalar_tensor_tensor(y[:, i, :], y[:, i, :], rstd[0][:, i, :], shifted[:, i, :], ALU.mult, ALU.add)
                    then(last)
                    moments(y, 1, n, 1.0e-5)
                else:
                    for i in range(g, g + k):
                        last = V.tensor_scalar(x[:, i, :], y[:, i, :], mean[1][:, i, 0:1], rstd[1][:, i, :], ALU.subtract, ALU.mult)
                    last.then_inc(x_ok, 1)


def norm_rows(V, then, to, rows, stats, mean, rstd, k, eps, asked, root, spare=None):
    for i in range(k):
        last = V.bn_stats(stats[:, i, :], rows[:, i, :])
    then(last)
    if spare is not None:
        V.memset(spare, 0.0).then_inc(then.sem, 1)
        then.done = then.done + 1
    for i in range(k):
        last = V.bn_aggr(mean[:, i, :], stats[:, i, :])
    then(last)
    V.tensor_scalar_add(rstd[:, 0:k, :], mean[:, 0:k, 1:2], eps).then_inc(asked, 1)
    root()
    for i in range(k):
        last = V.tensor_scalar(to[:, i, :], rows[:, i, :], mean[:, i, 0:1], rstd[:, i, :], ALU.subtract, ALU.mult)
    return last


def conv(nc, a, m, layer, out):
    ctx = ExitStack()
    with ctx:
        def sb(name, shape, dt):
            return ctx.enter_context(nc.sbuf_tensor(f"{name}_l{layer}", shape, dt))

        def sem(name):
            return ctx.enter_context(nc.semaphore(f"{name}_l{layer}"))

        eye, ones, ps = m["eye"], m["ones"], m["ps"]
        inT = m["xT"] if layer == 1 else m["hT"]
        W = {c: m[f"W{c}{layer}"] for c in "qvs"}
        Wk = m[f"Wk{layer}"]
        bq, bk, bv, bs = (m[f"b{c}{layer}"] for c in "qkvs")
        qT = sb("qT", [128, NODES + R], F32)
        kparts = sb("k_parts", [128, HEADS, 3, NODES], BF16)
        qparts = [sb(f"q_parts{i}", [128, HEADS, 2, R], BF16) for i in range(2)]
        q_now = sb("q_tile", [128, R], F32)
        spare3 = sb("spare3", [R, 1], F32)
        qhi, qsmall, qrest = sb("q_hi", [128, 1, R], BF16), sb("q_mid_lo", [128, 2, R], BF16), sb("q_rest", [128, R], F32)
        krest = [sb(f"k_rest{i}", [128, CW], F32) for i in range(2)]
        vals = sb("values", [R, T, HEADS, HD + 1], F32)
        x_now = [sb(f"in_tile{i}", [128, R], F32) for i in range(2)]
        bias = [sb(f"bias_rows{i}", [128, NODES], F32) for i in range(2)]
        S = [sb(f"scores{i}", [R, HEADS, NODES], F32) for i in range(2)]
        PT = [sb(f"weightsT{i}", [R, CW], F32) for i in range(4)]
        mx = [sb(f"chunk_max{i}", [R, HEADS, CH], F32) for i in range(2)]
        top = sb("top", [R, HEADS], F32)
        neg = [sb(f"neg_max{i}", [R, HEADS], F32) for i in range(2)]
        den = sb("sum", [R, HEADS, 1], F32)
        rows = [sb(f"rows{i}", [R, 1, D], F32) for i in range(2)]
        x_old = [sb(f"x_rows{i}", [R, 1, D], F32) for i in range(2)]
        skip = sb("skip", [R, D], F32)
        OT = [sb(f"sumsT{i}", [HD + 1, HEADS, R], F32) for i in range(2)]
        stats, mean, rstd = sb("stats", [R, 1, 6], F32), sb("mean", [R, 1, 2], F32), sb("rstd", [R, 1, 1], F32)
        half_power = sb("minus_half", [R, 1, 1], F32)
        spare, spare2 = sb("spare", [R, 1], F32), sb("spare2", [R, 1], F32)

        names = ("dve", "q_ps", "q_ok", "k_ok", "v_ps", "v_ok", "qk", "masked", "neg_ok", "exp_ok", "t_ps", "pa_ok",
                 "pv_ok", "pt", "skip_ok", "rows_ok", "r_ps", "r_ok", "one", "fin_ok", "dve2", "asked",
                 "rooted", "carried", "ot_ok", "o_ps", "x_cur", "q_laid", "kk_ps", "khi_ok",
                 "krest_ok", "kmid_ok", "pool")
        z = {n: sem(n) for n in names}
        b_in = [sem("b_in0"), sem("b_in1")]
        x_in = [sem("x_rows_in0"), sem("x_rows_in1")]
        out_ok = [sem("rows_out0"), sem("rows_out1")]
        groups = [(g, min(4, T - g)) for g in range(0, T, 4)]
        cw = widths()
        psS, psT, psO = ps[0:4], ps[4:6], ps[6:8]
        ON_V = (1, 4, 7, 10, 13)
        NT = HEADS * CH
        TURN = [((), ()), ((0,), (1,)), ((2,), (3,)), ((4,), (5,)), ((6,), (7, 8)), ((9,), (10, 11)), ((12,), (13,))]
        KU = CH * HEADS
        Q_STEPS = 6
        EXP_BEFORE = {3: 2, 6: 3}
        EXP_AT = 3
        on_v = [sum(c < i for c in ON_V) for i in range(NT + 1)]
        block = ctx.enter_context(nc.Block())

        def chunk_out(eng, u, i):
            if i in ON_V:
                wait(eng, z["pt"], u * len(ON_V) + (on_v[i] + 1))
            else:
                wait(eng, z["pa_ok"], u * (NT - len(ON_V)) + (i - on_v[i] + 1))

        @block.sync
        def _(sp):
            def step(t, par):
                if inside(t):
                    if not is_int(t) or t >= 2:
                        sp.wait_ge(z["masked"], (t - 1) * NT)
                    sp.dma_start(bias[par][:, :], m["bias"][bass.ds(t, 1), :, :].rearrange("a p n -> (a p) n")).then_inc(b_in[par], 16)
                if layer == 2 and inside(t):
                    if not is_int(t) or t >= 2:
                        sp.wait_ge(z["asked"], t - 1)
                    sp.dma_start(x_old[par][:, 0, :], m["x1"][bass.ds(t * R, R), :]).then_inc(x_in[par], 16)
                if layer == 2 and inside(t - 2):
                    sp.wait_ge(z["rows_ok"], t - 1)
                    sp.dma_start(out[bass.ds((t - 2) * R, R), :], rows[par][:, 0, :]).then_inc(out_ok[par], 16)
            pipeline_loop(sp, step)
            if layer == 2:
                sp.wait_ge(out_ok[0], 16 * ((T + 1) // 2))
                sp.wait_ge(out_ok[1], 16 * (T // 2))

        @block.gpsimd
        def _(pool):
            nc.gpsimd.memset(half_power[:, :, :], -0.5)
            nc.gpsimd.memset(vals[:, :, :, HD:HD + 1], 1.0).then_inc(z["one"], 1)
            pool.wait_ge(z["one"], 1)
            pool.wait_ge(z["q_ok"], CH)

            def split_q(t):
                pq = Steps(pool, z["pool"], t * Q_STEPS)
                if not is_int(t) or t >= 1:
                    pool.wait_ge(z["pool"], t * Q_STEPS)
                    pool.wait_ge(z["q_laid"], t)
                nc.gpsimd.tensor_tensor(spare3[:, :], half_power[:, 0, :], half_power[:, 0, :], ALU.mult).then_inc(z["pool"], 1)
                pq.done = pq.done + 1
                pq(nc.gpsimd.tensor_copy(q_now[:, :], qT[:, bass.ds(t * R, R)]))
                pq(nc.gpsimd.tensor_tensor(qhi[:, 0, :], q_now[:, :], ones[:, 0:R], ALU.mult))
                pq(nc.gpsimd.tensor_tensor(qrest[:, :], q_now[:, :], qhi[:, 0, :], ALU.subtract))
                pq(nc.gpsimd.tensor_tensor(qsmall[:, 0, :], qrest[:, :], ones[:, 0:R], ALU.mult))
                nc.gpsimd.tensor_tensor(qsmall[:, 1, :], qrest[:, :], qsmall[:, 0, :], ALU.subtract).then_inc(z["pool"], 1)

            split_q(0)

            def step(t, par):
                if inside(t + 1):
                    split_q(t + 1)
                if inside(t - 2):
                    if not is_int(t) or t >= 4:
                        pool.wait_ge(z["o_ps"], t - 3)
                    nc.gpsimd.tensor_copy(x_now[par][:, :], inT[:, bass.ds((t - 2) * R, R)]).then_inc(z["x_cur"], 1)
                if layer == 2 and inside(t - 2):
                    pool.wait_ge(z["asked"], t - 1)
                    nc.gpsimd.tensor_tensor(rstd[:, :, :], rstd[:, :, :], half_power[:, :, :], ALU.pow).then_inc(z["rooted"], 1)
            pipeline_loop(pool, step)

        @block.tensor
        def _(pe):
            for j in range(CH):
                if j >= 2:
                    pe.wait_ge(z["q_ok"], j - 1)
                    pe.wait_ge(z["krest_ok"], 2 * j - 2)
                nc.tensor.matmul(ps[j % 2][:, 0:cw[j]], W["q"][:, :], inT[:, CW * j:CW * j + cw[j]], start=True, stop=True).then_inc(z["q_ps"], 1)
                for hd in range(HEADS):
                    nc.tensor.matmul(ps[(2, 3, 6, 7)[(2 * j + hd) % 4]][:, 0:cw[j]], Wk[:, hd, :, :].rearrange("f i c -> f (i c)"),
                                     inT[:, CW * j:CW * j + cw[j]], start=True, stop=True).then_inc(z["kk_ps"], 1)
                g, k = groups[j]
                if j >= 2:
                    pe.wait_ge(z["v_ok"], j - 1)
                for i in range(k):
                    to = ps[4 + j % 2][0:R, i * D:(i + 1) * D]
                    nc.tensor.matmul(to, ones[0:1, 0:R], bv[:, :], start=True, stop=False)
                    last = nc.tensor.matmul(to, inT[:, (g + i) * R:(g + i + 1) * R], W["v"][:, :], start=False, stop=True)
                last.then_inc(z["v_ps"], 1)
            pe.wait_ge(z["q_ok"], CH)
            pe.wait_ge(z["k_ok"], KU)
            pe.wait_ge(z["v_ok"], len(groups))
            pe.wait_ge(z["one"], 1)

            def product(u, up, i):
                hd, c = i // CH, i % CH
                chunk_out(pe, u, i)
                to = psO[up][0:HD + 1, R * hd:R * (hd + 1)]
                for b in range(cw[c] // R):
                    last = nc.tensor.matmul(to, vals[:, 4 * c + b, hd, :], PT[(2 * up + i) % 4][:, b * R:(b + 1) * R],
                                            start=(c == 0 and b == 0), stop=(c == CH - 1 and b == 0))
                last.then_inc(z["pv_ok"], 1)

            def scores(t, par, j, hd):
                if j == 0 and hd == 0:
                    pe.wait_ge(z["q_laid"], t + 1)
                if not is_int(t) or t * CH + j >= 2:
                    pe.wait_ge(z["masked"], (t * CH + (j - 2)) * 2 + (hd + 1))
                for i, (q, k) in enumerate(((0, 0), (0, 1), (1, 2))):
                    last = nc.tensor.matmul(psS[2 * ((par + j) % 2) + hd][0:R, 0:cw[j]], qparts[par][:, hd, q, :],
                                            kparts[:, hd, k, CW * j:CW * j + cw[j]], start=(i == 0), stop=(i == 2))
                last.then_inc(z["qk"], 1)

            def step(t, par):
                u, up, w = t - 1, 1 - par, t - 2
                for j in range(CH):
                    for hd_s in range(HEADS):
                        if inside(t):
                            scores(t, par, j, hd_s)
                        if j == 0 and inside(w):
                            product(w, par, NT - 2 + hd_s)
                        if not inside(u):
                            continue
                        for i in TURN[j][hd_s]:
                            hd, c = i // CH, i % CH
                            if c in (0, EXP_AT):
                                pe.wait_ge(z["exp_ok"], u * 4 + (2 * hd + 1 + (c > 0)))
                            if i >= 2:
                                chunk_out(pe, u, i - 2)
                            elif not is_int(u) or u >= 1:
                                chunk_out(pe, u - 1, i - 2 + NT)
                            for b in range(cw[c] // R):
                                n = 4 * c + b
                                last = nc.tensor.transpose(psT[i % 2][0:R, b * R:(b + 1) * R], S[up][:, hd, n * R:(n + 1) * R],
                                                           eye[0:R, 0:R])
                            last.then_inc(z["t_ps"], 1)
                            if i == 2 and (not is_int(u) or u >= 2):
                                pe.wait_ge(z["fin_ok"], u - 1)
                            if i >= 2:
                                product(u, up, i - 2)
                    if j == 2 and inside(w):
                        pe.wait_ge(z["ot_ok"], w + 1)
                        pe.wait_ge(z["x_cur"], w + 1)
                        for hd in range(HEADS):
                            nc.tensor.transpose(psO[par][0:R, 256 + 128 * hd:256 + 128 * hd + HD + 1], OT[par][:, hd, :],
                                                       eye[0:HD + 1, 0:HD + 1])
                        to = psO[par][0:R, 0:D]
                        nc.tensor.matmul(to, ones[0:1, 0:R], bs[:, :], start=True, stop=False)
                        nc.tensor.matmul(to, x_now[par][:, :], W["s"][:, :], start=False, stop=True).then_inc(z["o_ps"], 1)
                    if layer == 1 and j == 5 and inside(w):
                        pe.wait_ge(z["rows_ok"], w + 1)
                        nc.tensor.transpose(psO[par][:, 128:128 + R], rows[par][:, 0, :], eye[0:R, 0:R]).then_inc(z["r_ps"], 1)
            pipeline_loop(pe, step)

        @block.scalar
        def _(act):
            def k_mid(n):
                j, hd = n // 2, n % 2
                act.wait_ge(z["krest_ok"], n + 1)
                nc.scalar.copy(kparts[:, hd, 1, CW * j:CW * j + cw[j]], krest[n % 2][:, 0:cw[j]]).then_inc(z["kmid_ok"], 1)

            for n in range(KU):
                j, hd = n // 2, n % 2
                act.wait_ge(z["kk_ps"], n + 1)
                nc.scalar.activation(kparts[:, hd, 0, CW * j:CW * j + cw[j]], ps[(2, 3, 6, 7)[n % 4]][:, 0:cw[j]], ACT.Identity,
                                     bias=bk[:, hd:hd + 1]).then_inc(z["khi_ok"], 1)
                if n >= 1:
                    k_mid(n - 1)
                if hd == 1:
                    g, k = groups[j]
                    act.wait_ge(z["v_ps"], j + 1)
                    nc.scalar.copy(vals[:, g:g + k, :, 0:HD], ps[4 + j % 2][0:R, 0:k * D].rearrange("p (t h f) -> p t h f", h=HEADS, f=HD)).then_inc(z["v_ok"], 1)
            k_mid(KU - 1)

            def lay_q(t, par):
                act.wait_ge(z["pool"], (t + 1) * Q_STEPS)
                if not is_int(t) or t >= 2:
                    act.wait_ge(z["qk"], (t - 1) * NT)
                for hd in range(HEADS):
                    own, other = slice(HD * hd, HD * (hd + 1)), slice(HD * (1 - hd), HD * (2 - hd))
                    nc.scalar.copy(qparts[par][own, hd, :, :], qhi[own, :, :].to_broadcast([HD, 2, R]))
                    last = nc.scalar.copy(qparts[par][other, hd, :, :], qsmall[own, :, :])
                last.then_inc(z["q_laid"], 1)

            def sums_out(w, par):
                act.wait_ge(z["pv_ok"], (w + 1) * NT)
                if not is_int(w) or w >= 2:
                    act.wait_ge(z["o_ps"], w - 1)
                nc.scalar.copy(OT[par][:, :, :], psO[par][0:HD + 1, 0:2 * R].rearrange("p (h n) -> p h n", h=HEADS)).then_inc(z["ot_ok"], 1)

            def step(t, par):
                u, up, w = t - 1, 1 - par, t - 2
                def exps(n):
                    hd, (lo, hi) = n // 2, ((0, CW * EXP_AT), (CW * EXP_AT, NODES))[n % 2]
                    part = S[up][:, hd, lo:hi]
                    nc.scalar.activation(part, part, ACT.Exp, bias=neg[up][:, hd:hd + 1]).then_inc(z["exp_ok"], 1)

                if inside(u):
                    act.wait_ge(z["neg_ok"], u + 1)
                    exps(0)
                    exps(1)
                if inside(w):
                    sums_out(w, par)
                if inside(u):
                    for i in range(NT):
                        if i in EXP_BEFORE:
                            exps(EXP_BEFORE[i])
                        if i in ON_V:
                            continue
                        c = i % CH
                        act.wait_ge(z["t_ps"], u * NT + (i + 1))
                        if i >= 4 or not is_int(u) or u >= 1:
                            act.wait_ge(z["pv_ok"], u * NT + (i - 3))
                        nc.scalar.copy(PT[(2 * up + i) % 4][:, 0:cw[c]], psT[i % 2][0:R, 0:cw[c]]).then_inc(z["pa_ok"], 1)
                        if i == 9:
                            if inside(t + 1):
                                lay_q(t + 1, 1 - par)
                        if layer == 1 and i == 12 and inside(w):
                            turned(w, par)
                elif layer == 1 and inside(w):
                    turned(w, par)
                if is_int(t) and t == 0:
                    lay_q(1, 1)

            def turned(w, par):
                act.wait_ge(z["r_ps"], w + 1)
                nc.scalar.copy(m["hT"][:, bass.ds(w * R, R)], psO[par][:, 128:128 + R]).then_inc(z["r_ok"], 1)
            lay_q(0, 0)
            pipeline_loop(act, step)

        @block.vector
        def _(v):
            V = nc.vector
            V.memset(qT[:, NODES:NODES + R], 0.0)
            def k_low(n):
                j, hd = n // 2, n % 2
                own, other = slice(HD * hd, HD * (hd + 1)), slice(HD * (1 - hd), HD * (2 - hd))
                at = slice(CW * j, CW * j + cw[j])
                V.tensor_copy(kparts[other, hd, 2, at], kparts[other, hd, 0, at])
                v.wait_ge(z["kmid_ok"], n + 1)
                V.tensor_tensor(kparts[own, hd, 2, at], krest[n % 2][own, 0:cw[j]], kparts[own, hd, 1, at], ALU.subtract).then_inc(z["k_ok"], 1)

            for n in range(KU):
                j, hd = n // 2, n % 2
                v.wait_ge(z["khi_ok"], n + 1)
                if n >= 2:
                    v.wait_ge(z["k_ok"], n - 1)
                V.scalar_tensor_tensor(krest[n % 2][:, 0:cw[j]], ps[(2, 3, 6, 7)[n % 4]][:, 0:cw[j]], bk[:, hd:hd + 1],
                                       kparts[:, hd, 0, CW * j:CW * j + cw[j]], ALU.add, ALU.subtract).then_inc(z["krest_ok"], 1)
                if n >= 1:
                    k_low(n - 1)
                if hd == 1:
                    continue
                v.wait_ge(z["q_ps"], j + 1)
                V.tensor_scalar(qT[:, CW * j:CW * j + cw[j]], ps[j % 2][:, 0:cw[j]], bq[:, :], float(HD) ** -0.5, ALU.add, ALU.mult).then_inc(z["q_ok"], 1)
            k_low(KU - 1)

            def finish(w, par, then):
                v.wait_ge(z["o_ps"], w + 1)
                O = psO[par][0:R, 256:512].rearrange("p (h f) -> p h f", h=HEADS)
                then(V.tensor_scalar_max(den[:, :, :], O[:, :, HD:HD + 1], 1.0e-30))
                V.tensor_copy(skip[:, :], psO[par][0:R, 0:D])
                then(V.reciprocal(den[:, :, :], den[:, :, :]))
                if layer == 2 and (not is_int(w) or w >= 2):
                    v.wait_ge(out_ok[par], half(w, par) * 16)
                for hd in range(HEADS):
                    last = V.scalar_tensor_tensor(rows[par][:, 0, HD * hd:HD * (hd + 1)], O[:, hd, 0:HD], den[:, hd, :],
                                                  skip[:, HD * hd:HD * (hd + 1)], ALU.mult, ALU.add)
                last.then_inc(z["fin_ok"], 1)
                v.wait_ge(z["fin_ok"], w + 1)
                r = rows[par]
                if layer == 1:
                    V.tensor_scalar_max(r[:, :, :], r[:, :, :], 0.0).then_inc(z["rows_ok"], 1)
                else:
                    v.wait_ge(x_in[par], (half(w, par) + 1) * 16)
                    then(V.tensor_tensor(r[:, :, :], r[:, :, :], x_old[par][:, :, :], ALU.add))
                    norm_rows(V, then, r, r, stats, mean, rstd, 1, 1.0e-5, z["asked"],
                              lambda: v.wait_ge(z["rooted"], w + 1), spare2[:, :]).then_inc(z["rows_ok"], 1)
                v.wait_ge(z["rows_ok"], w + 1)

            CHAIN = 2 if layer == 1 else 6

            def step(t, par):
                u, up, w = t - 1, 1 - par, t - 2
                then = Steps(v, z["dve"], w * CHAIN if not is_int(w) else CHAIN * max(0, w))
                if inside(t):
                    v.wait_ge(b_in[par], (half(t, par) + 1) * 16)
                    if not is_int(t) or t >= 2:
                        v.wait_ge(z["t_ps"], (t - 1) * NT)
                        v.wait_ge(z["neg_ok"], t - 1)
                for j in range(CH):
                    if inside(t):
                        v.wait_ge(z["carried"], t * CH + j) if not is_int(t) or t * CH + j > 0 else None
                        v.wait_ge(z["qk"], (t * CH + (j + 1)) * 2)
                        V.memset(spare[:, :], 0.0).then_inc(z["carried"], 1)
                        for hd in range(HEADS):
                            lo, hi = CW * j, CW * j + cw[j]
                            V.tensor_tensor_reduce(S[par][:, hd, lo:hi], psS[2 * ((par + j) % 2) + hd][0:R, 0:cw[j]],
                                                   bias[par][0:R, lo:hi], 1.0, FLOOR, ALU.add, ALU.max,
                                                   mx[par][:, hd, j:j + 1]).then_inc(z["masked"], 1)
                    if inside(u):
                        for i in TURN[j][0] + TURN[j][1]:
                            if i in ON_V:
                                c = i % CH
                                v.wait_ge(z["t_ps"], u * NT + (i + 1))
                                if i >= 4 or not is_int(u) or u >= 1:
                                    v.wait_ge(z["pv_ok"], u * NT + (i - 3))
                                V.tensor_copy(PT[(2 * up + i) % 4][:, 0:cw[c]], psT[i % 2][0:R, 0:cw[c]]).then_inc(z["pt"], 1)
                    if j == 3 and inside(w):
                        finish(w, par, then)
                if inside(t):
                    v.wait_ge(z["masked"], (t + 1) * NT)
                    wait(v, z["neg_ok"], t)
                    V.tensor_reduce(top[:, :], mx[par][:, :, :], AX.X, ALU.max).then_inc(z["dve2"], 1)
                    v.wait_ge(z["dve2"], t + 1)
                    if not is_int(t) or t >= 2:
                        v.wait_ge(z["exp_ok"], (t - 1) * 4)
                    V.tensor_scalar_mul(neg[par][:, :], top[:, :], -1.0).then_inc(z["neg_ok"], 1)
            pipeline_loop(v, step)


INPUTS = ['x', 'src', 'dst', 'edge_type_8', 'edge_weight', 'L0_gnn_V', 'L0_gnn_w_comp', 'L0_gnn_loop_w', 'L0_gnn_bias',
          'L0_gnn_ffn_w', 'L0_gnn_ffn_b', 'L0_gnn_ln_g', 'L0_gnn_ln_b'] + [
              f'L1_gnn_{w}{k}{l}' for l in (1, 2) for k in 'qkvs' for w in 'Wb']


def kernel(**inputs):
    import numpy as np
    import concourse.bacc as bacc
    from concourse.bass_utils import run_bass_kernel_spmd

    nc = bacc.Bacc("TRN2", target_bir_lowering=False, num_devices=1)
    arrays, args = {}, {}
    for name in INPUTS:
        value = np.ascontiguousarray(inputs[name])
        arrays[f"in_{name}"] = value
        args[name] = nc.dram_tensor(f"in_{name}", value.shape, mybir.dt.from_np(value.dtype), kind="ExternalInput").ap()
    out = nc.dram_tensor("out", (NODES, D), F32, kind="ExternalOutput").ap()
    build(nc, args, out)
    return run_bass_kernel_spmd(nc, [arrays], core_ids=[0]).results[0]["out"]
```

```python
from contextlib import ExitStack

import concourse.bass as bass
from concourse import mybir

F32 = mybir.dt.float32
BF16 = mybir.dt.bfloat16
I32 = mybir.dt.int32
U32 = mybir.dt.uint32
ALU = mybir.AluOpType
ACT = mybir.ActivationFunctionType
AX = mybir.AxisListType

NODES, EDGES, D = 3125, 103125, 128
RELS, BASES = 8, 4
HEADS, HD = 2, 64
T = 25
R = NODES // T
EC = EDGES // R
SLOTS = 64
COLS = 34
PAD = COLS * 128
BLOCKS = -(-EDGES // 128)
PAIRS = 63
CW = 500
CH = 7
FIRST = 5
NEG = -1.0e30
FLOOR = -1.0e29
MAGIC = 12582912.0


def widths():
    return [min(CW, NODES - CW * j) for j in range(CH)]


class Steps:

    def __init__(self, eng, sem, done=0):
        self.eng, self.sem, self.done = eng, sem, done

    def __call__(self, ins):
        ins.then_inc(self.sem, 1)
        self.done = self.done + 1
        self.eng.wait_ge(self.sem, self.done)


def is_int(t):
    return isinstance(t, int)


def inside(t):
    return not is_int(t) or 0 <= t < T


def half(t, par):
    if is_int(t):
        return t // 2
    return (t - par) // 2


def wait(eng, sem, value):
    if not is_int(value) or value > 0:
        eng.wait_ge(sem, value)


def build(nc, a, out):
    ctx = ExitStack()
    with ctx:
        ctx.enter_context(nc.allow_non_contiguous_dma(reason="small transposed rows"))

        def dram(name, shape, dt):
            return nc.dram_tensor(name, shape, dt, kind="Internal").ap()

        m = {
            "rel_table": dram("rel_table", (RELS * NODES, D), F32),
            "records": dram("records", (EDGES + PAD, 3), F32),
            "sources": dram("sources", (EDGES + PAD, 2), F32),
            "messages": dram("messages", (BLOCKS, 128, D), F32),
            "x1": dram("x1", (NODES, D), F32),
            "bias": dram("bias", (T, 128, NODES), F32),
        }
        kept = ExitStack()
        with kept:
            def sb(name, shape, dt):
                return kept.enter_context(nc.sbuf_tensor(name, shape, dt))
            m["eye"] = sb("eye", [128, 128], F32)
            m["ones"] = sb("ones", [128, 128], F32)
            m["xT"] = sb("xT", [128, NODES], F32)
            m["ps"] = [kept.enter_context(nc.psum_tensor(f"ps{i}", [128, 512], F32)) for i in range(8)]
            m["loop_w"], m["loop_bias"] = sb("loop_w", [128, D + 1], F32), sb("loop_bias", [1, D + 1], F32)
            m["ffnT"], m["ffn_b"] = sb("ffnT", [D, D], F32), sb("ffn_b", [1, D], F32)
            m["ln_g"], m["ln_b"] = sb("ln_g", [R, D], F32), sb("ln_b", [R, D], F32)
            for layer in (1, 2):
                for c in "qvs":
                    m[f"W{c}{layer}"] = sb(f"W{c}{layer}", [D, D], F32)
                m[f"Wk{layer}"] = sb(f"Wk{layer}", [D, HEADS, 2, HD], F32)
                m[f"bq{layer}"], m[f"bk{layer}"] = sb(f"bq{layer}", [D, 1], F32), sb(f"bk{layer}", [D, HEADS], F32)
                m[f"bv{layer}"], m[f"bs{layer}"] = sb(f"bv{layer}", [1, D], F32), sb(f"bs{layer}", [R, D], F32)
            with ExitStack() as first:
                def sb1(name, shape, dt):
                    return first.enter_context(nc.sbuf_tensor(name, shape, dt))
                m["x"] = sb1("x_rows", [R, T, D], F32)
                m["starts"] = sb1("starts", [128, T + 2], F32)
                m["start_rows"] = sb1("start_rows", [1, T + 2], I32)
                m["flag"] = sb1("flag", [1, 1], I32)
                m["iota"] = sb1("iota", [128, 128], F32)
                prepare(nc, a, m)
                irregular = nc.values_load(m["flag"][0:1, 0:1], min_val=0, max_val=1)
                sems = nc.snapshot_sems()
                with nc.If(irregular):
                    m["h"] = sb1("h_rows", [R, T, D], F32)
                    message_any(nc, a, m)
                    first_norms(nc, a, m)
                nc.restore_sems(sems)
                with nc.Else():
                    message(nc, a, m)
            m["hT"] = sb("hT", [128, NODES], F32)
            conv(nc, a, m, 1, None)
            conv(nc, a, m, 2, out)


def prepare(nc, a, m):
    ctx = ExitStack()
    with ctx:
        def sb(name, shape, dt):
            return ctx.enter_context(nc.sbuf_tensor(name, shape, dt))

        def sem(name):
            return ctx.enter_context(nc.semaphore(name))

        ROWS = 4
        x, xT, eye, ones, ps = m["x"], m["xT"], m["eye"], m["ones"], m["ps"]
        V = sb("V", [128, BASES, D], F32)
        comp = sb("comp", [128, RELS * BASES], F32)
        W = sb("W", [128, RELS, D], F32)
        rows = sb("rel_rows", [128, ROWS, RELS, D], F32)
        si = sb("src_int", [R, EC], I32)
        di = sb("dst_int", [R, EC], I32)
        dn = sb("dst_next", [R, SLOTS], I32)
        ti = sb("type_int", [R, EC], I32)
        wf = sb("weight", [R, EC], F32)
        sf = sb("src_f", [R, EC], F32)
        df = sb("dst_f", [R, EC + SLOTS], F32)
        tf = sb("type_f", [R, EC], F32)
        cf = sb("chunk_f", [R, EC], F32)
        rec = sb("rec", [R, EC, 3], F32)
        srcs = sb("srcs", [R, EC, 2], F32)
        junk = sb("junk", [R, EC], F32)
        ffn = sb("ffn", [D, D], F32)
        f_in, f_ps, f_ok = sem("f_in"), sem("f_ps"), sem("f_ok")
        count = sb("count", [R, T + 4], F32)
        sizes = sb("sizes", [1, T], F32)
        large = sb("large", [1, 1], F32)
        bad = sb("bad", [1, 2], F32)
        pad_rec = sb("pad_rec", [128, COLS, 3], F32)
        pad_src = sb("pad_src", [128, COLS, 2], F32)

        x_in, v_in, w_in, e_in, n_in = sem("x_in"), sem("v_in"), sem("w_in"), sem("e_in"), sem("n_in")
        const, dve, sent = sem("const"), sem("dve_p"), sem("sent")
        xt_ps, xt_ok, w_ok = sem("xt_ps"), sem("xt_ok"), sem("w_ok")
        rel_ps, rel_a = sem("rel_ps"), sem("rel_a")
        rel_out = [sem(f"rel_out{i}") for i in range(ROWS)]
        rec_ok, src_ok, pad_ok, cnt_ok, cnt_ps = sem("rec_ok"), sem("src_ok"), sem("pad_ok"), sem("cnt_ok"), sem("cnt_ps")
        block = ctx.enter_context(nc.Block())
        groups = [(g, min(4, T - g)) for g in range(0, T, 4)]

        def load_constants(sp):
            def load(to, src):
                sp.dma_start(to, src).then_inc(w_in, 16)

            load(m["loop_w"][:, 0:D], a["L0_gnn_loop_w"])
            load(m["loop_bias"][:, 0:D], a["L0_gnn_bias"].rearrange("(a n) -> a n", a=1))
            sp.dma_start(ffn[:, :], a["L0_gnn_ffn_w"]).then_inc(f_in, 16)
            load(m["ffn_b"][:, :], a["L0_gnn_ffn_b"].rearrange("(a n) -> a n", a=1))
            load(m["ln_g"][:, :], a["L0_gnn_ln_g"].partition_broadcast(R))
            load(m["ln_b"][:, :], a["L0_gnn_ln_b"].partition_broadcast(R))
            for layer in (1, 2):
                for c in "qvs":
                    load(m[f"W{c}{layer}"][:, :], a[f"L1_gnn_W{c}{layer}"])
                for i in range(2):
                    load(m[f"Wk{layer}"][:, :, i, :], a[f"L1_gnn_Wk{layer}"].rearrange("f (h c) -> f h c", h=HEADS))
                    load(m[f"bk{layer}"][HD * i:HD * (i + 1), :], a[f"L1_gnn_bk{layer}"].rearrange("(h c) -> c h", h=HEADS))
                load(m[f"bq{layer}"][:, :], a[f"L1_gnn_bq{layer}"].rearrange("(n a) -> n a", a=1))
                load(m[f"bv{layer}"][:, :], a[f"L1_gnn_bv{layer}"].rearrange("(a n) -> a n", a=1))
                load(m[f"bs{layer}"][:, :], a[f"L1_gnn_bs{layer}"].partition_broadcast(R))

        W_IN = 16 * (5 + 2 * 10)

        @block.sync
        def _(sp):
            sp.dma_start(x[:, :, :], a["x"].rearrange("(t p) f -> p t f", p=R)).then_inc(x_in, 16)
            sp.dma_start(V[:, :, :], a["L0_gnn_V"].rearrange("b i o -> i b o")).then_inc(v_in, 16)
            sp.dma_start(comp[:, :], a["L0_gnn_w_comp"].rearrange("r b -> (r b)").partition_broadcast(128)).then_inc(v_in, 16)
            sp.dma_start(di[:, :], a["dst"].rearrange("(p n) -> p n", n=EC)).then_inc(e_in, 16)
            sp.dma_start(dn[0:R - 1, :], a["dst"].rearrange("(p n) -> p n", n=EC)[1:R, 0:SLOTS]).then_inc(e_in, 16)
            sp.dma_start(si[:, :], a["src"].rearrange("(p n) -> p n", n=EC)).then_inc(n_in, 16)
            sp.dma_start(ti[:, :], a["edge_type_8"].rearrange("(p n) -> p n", n=EC)).then_inc(n_in, 16)
            sp.dma_start(wf[:, :], a["edge_weight"].rearrange("(p n) -> p n", n=EC)).then_inc(n_in, 16)
            load_constants(sp)
            table = m["rel_table"].rearrange("(r n) f -> n r f", r=RELS)
            for t in range(T):
                n = min(128, NODES - 128 * t)
                sp.wait_ge(rel_a, t + 1)
                sp.dma_start(table[128 * t:128 * t + n], rows[0:n, t % ROWS]).then_inc(rel_out[t % ROWS], 16)
            sp.wait_ge(w_in, W_IN)
            for i in range(ROWS):
                sp.wait_ge(rel_out[i], 16 * len(range(i, T, ROWS)))

        @block.gpsimd
        def _(pool):
            nc.gpsimd.iota(m["iota"][:, :], pattern=[[1, 128]], base=0, channel_multiplier=0,
                           allow_small_or_imprecise_dtypes=True).then_inc(const, 1)
            nc.gpsimd.memset(ones[:, :], 1.0).then_inc(const, 1)
            pool.wait_ge(const, 2)
            nc.gpsimd.affine_select(out=eye[:, :], in_=ones[:, :], compare_op=ALU.is_equal, fill=0.0, base=0,
                                    pattern=[[-1, 128]], channel_multiplier=1).then_inc(const, 1)
            pool.wait_ge(pad_ok, 1)
            pool.dma_start(m["records"][EDGES:EDGES + PAD, :].rearrange("(p n) c -> p n c", p=128), pad_rec[:, :, :]).then_inc(sent, 16)
            pool.dma_start(m["sources"][EDGES:EDGES + PAD, :].rearrange("(p n) c -> p n c", p=128), pad_src[:, :, :]).then_inc(sent, 16)
            pool.wait_ge(rec_ok, 1)
            pool.dma_start(m["records"][0:EDGES, :].rearrange("(p n) c -> p n c", n=EC), rec[:, :, :]).then_inc(sent, 16)
            pool.wait_ge(src_ok, 1)
            pool.dma_start(m["sources"][0:EDGES, :].rearrange("(p n) c -> p n c", n=EC), srcs[:, :, :]).then_inc(sent, 16)
            pool.wait_ge(sent, 64)

        @block.tensor
        def _(pe):
            pe.wait_ge(x_in, 16)
            pe.wait_ge(const, 3)
            for n, (g, k) in enumerate(groups):
                if n >= 2:
                    pe.wait_ge(xt_ok, n - 1)
                for i in range(k):
                    last = nc.tensor.transpose(ps[n % 2][0:128, i * R:(i + 1) * R], x[:, g + i, :], eye[0:R, 0:R])
                last.then_inc(xt_ps, 1)
            pe.wait_ge(w_ok, 1)
            pe.wait_ge(xt_ok, len(groups))
            for t in range(T):
                n = min(128, NODES - 128 * t)
                if t >= 2:
                    pe.wait_ge(rel_a, t - 1)
                for h in range(2):
                    last = nc.tensor.matmul(ps[4 + 2 * (t % 2) + h][0:n, :], xT[:, 128 * t:128 * t + n],
                                            W[:, 4 * h:4 * h + 4, :], start=True, stop=True)
                last.then_inc(rel_ps, 1)
                if t == T - 4:
                    pe.wait_ge(f_in, 16)
                    nc.tensor.transpose(ps[3][:, 0:D], ffn[:, :], eye[:, :]).then_inc(f_ps, 1)
                    pe.wait_ge(cnt_ok, 1)
                    nc.tensor.matmul(ps[2][:, 0:T + 4], ones[0:R, 0:128], count[:, :], start=True, stop=True).then_inc(cnt_ps, 1)

        @block.scalar
        def _(act):
            for n, (g, k) in enumerate(groups):
                act.wait_ge(xt_ps, n + 1)
                nc.scalar.copy(xT[:, g * R:(g + k) * R], ps[n % 2][:, 0:k * R]).then_inc(xt_ok, 1)
            for t in range(T):
                act.wait_ge(rel_ps, t + 1)
                if t >= ROWS:
                    act.wait_ge(rel_out[t % ROWS], 16 * (t // ROWS))
                n = min(128, NODES - 128 * t)
                for h in range(2):
                    last = nc.scalar.copy(rows[0:n, t % ROWS, 4 * h:4 * h + 4, :],
                                          ps[4 + 2 * (t % 2) + h][0:n, :].rearrange("p (r f) -> p r f", f=D))
                last.then_inc(rel_a, 1)
            act.wait_ge(f_ps, 1)
            nc.scalar.copy(m["ffnT"][:, :], ps[3][:, 0:D]).then_inc(f_ok, 1)

        @block.vector
        def _(v):
            then = Steps(v, dve)
            V_ = nc.vector
            V_.memset(pad_rec[:, :, :], 0.0)
            V_.memset(count[:, :], 0.0)
            V_.memset(df[:, EC:EC + SLOTS], 1.0e6)
            then(V_.memset(pad_src[:, :, :], -512.0))
            V_.memset(pad_rec[:, :, 1:2], -1000.0).then_inc(pad_ok, 1)
            v.wait_ge(v_in, 32)
            for r in range(RELS):
                V_.tensor_scalar(W[:, r, :], V[:, 0, :], comp[:, BASES * r:BASES * r + 1], None, ALU.mult)
            then(V_.memset(bad[:, :], 0.0))
            for b in range(1, BASES):
                for r in range(RELS):
                    last = V_.scalar_tensor_tensor(W[:, r, :], V[:, b, :], comp[:, BASES * r + b:BASES * r + b + 1],
                                                   W[:, r, :], ALU.mult, ALU.add)
                    if r == RELS - 1 and b < BASES - 1:
                        then(last)
            last.then_inc(w_ok, 1)
            v.wait_ge(e_in, 32)
            V_.tensor_copy(df[:, 0:EC], di[:, :])
            then(V_.tensor_copy(df[0:R - 1, EC:EC + SLOTS], dn[0:R - 1, :]))
            for t in range(1, T + 1):
                then(V_.tensor_scalar(junk[:, :], df[:, 0:EC], float(R * t), None, ALU.is_lt, ALU.add, accum_out=count[:, t:t + 1]))
            then(V_.tensor_tensor(junk[:, :], df[:, 0:EC], df[:, 1:EC + 1], ALU.is_gt))
            then(V_.tensor_reduce(count[:, T + 2:T + 3], junk[:, :], AX.X, ALU.add))
            then(V_.tensor_tensor(junk[:, :], df[:, 0:EC], df[:, SLOTS:EC + SLOTS], ALU.is_equal))
            V_.tensor_reduce(count[:, T + 3:T + 4], junk[:, :], AX.X, ALU.add).then_inc(cnt_ok, 1)
            v.wait_ge(n_in, 48)
            V_.tensor_copy(sf[:, :], si[:, :])
            then(V_.tensor_copy(tf[:, :], ti[:, :]))
            V_.scalar_tensor_tensor(rec[:, :, 0], tf[:, :], float(NODES), sf[:, :], ALU.mult, ALU.add)
            V_.tensor_copy(rec[:, :, 1], df[:, 0:EC])
            V_.tensor_copy(rec[:, :, 2], wf[:, :]).then_inc(rec_ok, 1)
            then(V_.tensor_scalar(cf[:, :], sf[:, :], 1.0 / R, -0.496, ALU.mult, ALU.add))
            then(V_.tensor_scalar_add(cf[:, :], cf[:, :], MAGIC))
            then(V_.tensor_scalar_add(cf[:, :], cf[:, :], -MAGIC))
            V_.tensor_copy(srcs[:, :, 1], cf[:, :])
            V_.scalar_tensor_tensor(srcs[:, :, 0], cf[:, :], -float(R), sf[:, :], ALU.mult, ALU.add).then_inc(src_ok, 1)
            v.wait_ge(cnt_ps, 1)
            V_.tensor_copy(m["starts"][:, :], ps[2][:, 0:T + 2])
            V_.tensor_copy(m["start_rows"][:, :], ps[2][0:1, 0:T + 2])
            then(V_.tensor_copy(bad[:, :], ps[2][0:1, T + 2:T + 4]))
            then(V_.tensor_tensor(sizes[:, :], m["starts"][0:1, 1:T + 1], m["starts"][0:1, 0:T], ALU.subtract))
            then(V_.tensor_scalar(sizes[:, :], sizes[:, :], float(PAD), None, ALU.is_gt))
            then(V_.tensor_reduce(large[:, :], sizes[:, :], AX.X, ALU.add))
            then(V_.tensor_tensor(bad[:, 0:1], bad[:, 0:1], bad[:, 1:2], ALU.add))
            then(V_.tensor_tensor(bad[:, 0:1], bad[:, 0:1], large[:, :], ALU.add))
            then(V_.tensor_scalar(m["flag"][:, :], bad[:, 0:1], 0.0, None, ALU.is_gt))


def message(nc, a, m):
    ctx = ExitStack()
    with ctx:
        def sb(name, shape, dt):
            return ctx.enter_context(nc.sbuf_tensor(name, shape, dt))

        def sem(name):
            return ctx.enter_context(nc.semaphore(name))

        x, xT, eye, ones, iota, starts, ps = (m[k] for k in ("x", "xT", "eye", "ones", "iota", "starts", "ps"))
        G = sb("gathered", [128, 2, COLS, D + 1], F32)
        A = sb("dst_onehot", [128, 2, COLS, R], F32)
        win = [sb(f"window{i}", [128, COLS * 3], F32) for i in range(2)]
        rel = [sb(f"rel_at{i}", [128, COLS], U32) for i in range(2)]
        ell = [sb(f"slots{i}", [128, SLOTS * 2], F32) for i in range(2)]
        eidx = [sb(f"slots_at{i}", [128, 1], U32) for i in range(2)]
        deg = [sb(f"degree{i}", [128, 1], F32) for i in range(2)]
        xt = [sb(f"xT_tile{i}", [128, R], F32) for i in range(2)]
        start = sb("tile_start", [128, 1], F32)
        nodes = sb("tile_nodes", [128, R], F32)
        tri = sb("tri", [128, 128], F32)
        loopw, lbias = m["loop_w"], m["loop_bias"]
        off = sb("unused", [128, SLOTS], F32)
        codes = sb("codes", [128, 2, 2, SLOTS], F32)
        codesT = sb("codesT", [128, 2, 64], BF16)
        iob = sb("iota_b", [128, 128], BF16)
        L = sb("low_onehot", [128, PAIRS, R], BF16)
        H = sb("high_onehot", [128, PAIRS, 2 * T], BF16)
        CT = sb("countsT", [R, T, 2 * PAIRS], F32)
        bias = [sb(f"bias{i}", [128, NODES], F32) for i in range(2)]
        lns = [sb(f"ln{i}", [R, CW], F32) for i in range(2)]
        tiny = sb("tiny", [128, 1], F32)
        spare = sb("spare", [128, 1], F32)

        psA, psS, psC, psT, psK = ps[0:2], ps[2], ps[3:5], ps[5:7], ps[7]
        const, dve, gps = sem("m_const"), sem("dve_m"), sem("pool_m")
        rel_ok, hot_ok, scaled = sem("rel_ok"), sem("hot_ok"), sem("scaled")
        win_in = [sem("win_in0"), sem("win_in1")]
        g_in = [[sem(f"g_in{i}_{part}") for part in range(2)] for i in range(2)]
        PARTS = (COLS // 2, COLS - COLS // 2)
        ell_in = [sem("ell_in0"), sem("ell_in1")]
        out_ok = [sem("bias_out0"), sem("bias_out1")]
        xt_ok, agg, deg_ok, st_ok, eidx_ok = sem("xt_ok_m"), sem("agg"), sem("deg_ok"), sem("st_ok"), sem("eidx_ok")
        codes_ok, codes_ps, lh_ok = sem("codes_ok"), sem("codes_ps"), sem("lh_ok")
        c_ps, c_ok, t_ps, ln_ok, masked, bias_ok = (sem("c_ps"), sem("c_ok"), sem("t_ps"), sem("ln_ok"), sem("masked"),
                                                    sem("bias_ok"))
        ROOTS_AFTER = 17
        SLOTS_AFTER = COLS - 3
        pairs = [min(10, PAIRS - 10 * j) for j in range(CH)]
        cw = widths()
        AFTER = 4
        gain, shift, ffnT, ffnb = m["ln_g"], m["ln_b"], m["ffnT"], m["ffn_b"]
        hrow = [sb(f"m_h_rows{i}", [R, D], F32) for i in range(2)]
        hT = sb("m_hT", [D, R], F32)
        ya = [sb(f"m_y_rows{i}", [R, D], F32) for i in range(2)]
        yb = [sb(f"z_rows{i}", [R, D], F32) for i in range(2)]
        shifted = [sb(f"x_shifted{i}", [R, D], F32) for i in range(2)]
        xnew = [sb(f"x1_rows{i}", [R, D], F32) for i in range(2)]
        roots = [sb(f"m_rstd{i}", [R, 2], F32) for i in range(2)]
        means = [[sb(f"m_mean{which}_{i}", [R, 2], F32) for i in range(2)] for which in range(2)]
        stats = [sb(f"m_stats{which}", [R, 6], F32) for which in range(2)]
        half_power, spare2 = sb("minus_half_m", [R, 2], F32), sb("spare2", [R, 1], F32)
        h_ps, h_ok, y_ps, y_ok, x_ok, x_ps, x_t_ok, asked, rooted, nrm = (
            sem("m_" + n) for n in ("h_ps", "h_ok", "y_ps", "y_ok", "x_ok", "x_ps", "x_t_ok", "asked", "rooted", "norms"))
        kept = [sem("x1_out0"), sem("x1_out1")]
        block = ctx.enter_context(nc.Block())

        @block.gpsimd
        def _(pool):
            settled = Steps(pool, gps, 1)

            def settle():
                pool.wait_ge(gps, settled.done)
                nc.gpsimd.tensor_tensor(spare[:, :], spare[:, :], spare[:, :], ALU.add).then_inc(gps, 1)
                settled.done = settled.done + 1

            nc.gpsimd.memset(spare[:, :], 0.0)
            nc.gpsimd.memset(half_power[:, :], -0.5)
            nc.gpsimd.memset(tri[:, :], 1.0).then_inc(gps, 1)
            pool.wait_ge(gps, 1)
            nc.gpsimd.affine_select(out=tri[:, :], in_=tri[:, :], compare_op=ALU.is_gt, fill=0.0,
                                    base=0, pattern=[[1, 128]], channel_multiplier=-1).then_inc(const, 1)

            def slots(u, par):
                pool.wait_ge(eidx_ok, u + 1)
                if not is_int(u) or u >= 2:
                    pool.wait_ge(codes_ok, u - 1)
                settle()
                nc.gpsimd.indirect_dma_start(out=ell[par][:, :], out_offset=None, in_=m["sources"],
                                             in_offset=bass.IndirectOffsetOnAxis(ap=eidx[par][:, :], axis=0)).then_inc(ell_in[par], 16)

            def root(t, par):
                pool.wait_ge(asked, t - 2)
                nc.gpsimd.tensor_tensor(roots[1 - par][:, :], roots[1 - par][:, :], half_power[:, :], ALU.pow).then_inc(rooted, 1)

            def step(t, par):
                settled.done = 1 + (min(t, T) + max(0, t - 1) if is_int(t) else t * 2 - 1)
                if inside(t):
                    pool.wait_ge(rel_ok, t + 1)
                    if not is_int(t) or t >= 2:
                        pool.wait_ge(agg, t - 1)
                    settle()
                    for j in range(COLS):
                        nc.gpsimd.indirect_dma_start(out=G[:, par, j, 0:D], out_offset=None, in_=m["rel_table"],
                                                     in_offset=bass.IndirectOffsetOnAxis(ap=rel[par][:, j:j + 1], axis=0)).then_inc(g_in[par][j >= PARTS[0]], 16)
                        if j == ROOTS_AFTER and (not is_int(t) or t >= 3):
                            root(t, par)
                        if j == SLOTS_AFTER and inside(t - 1):
                            slots(t - 1, 1 - par)
                else:
                    root(t, par)
                    if inside(t - 1):
                        slots(t - 1, 1 - par)

            pipeline_loop(pool, step, AFTER)

        @block.sync
        def _(sp):
            def window(t, par):
                at = sp.value_load(m["start_rows"][0:1, bass.ds(t, 1)], min_val=0, max_val=EDGES)
                if not is_int(t) or t >= 2:
                    sp.wait_ge(scaled, (t - 1) * 2)
                    sp.wait_ge(hot_ok, t - 1)
                sp.dma_start(win[par][:, :], m["records"][bass.ds(at, PAD), :].rearrange("(p n) c -> p (n c)", p=128)).then_inc(win_in[par], 16)

            window(0, 0)
            sp.wait_ge(const, 2)

            def step(t, par):
                v = t - 2
                if inside(t + 1):
                    window(t + 1, 1 - par)
                if inside(t - 4):
                    sp.wait_ge(x_ok, t - 3)
                    sp.dma_start(m["x1"][bass.ds((t - 4) * R, R), :], xnew[par][:, :]).then_inc(kept[par], 16)
                if inside(v):
                    sp.wait_ge(bias_ok, (v + 1) * CH)
                    sp.dma_start(m["bias"][bass.ds(v, 1), :, :].rearrange("a p n -> (a p) n"), bias[par][:, :]).then_inc(out_ok[par], 16)
            pipeline_loop(sp, step, AFTER)
            sp.wait_ge(out_ok[0], 16 * ((T + 1) // 2))
            sp.wait_ge(out_ok[1], 16 * (T // 2))
            sp.wait_ge(kept[0], 16 * ((T + 1) // 2))
            sp.wait_ge(kept[1], 16 * (T // 2))
            sp.wait_ge(win_in[T % 2], 16 * ((T + 1) // 2))

        @block.vector
        def _(v_):
            V = nc.vector
            V.memset(deg[0][:, :], 0.0)
            V.memset(deg[1][:, :], 0.0)
            V.memset(roots[0][:, :], 1.0)
            V.memset(roots[1][:, :], 1.0)
            V.memset(G[:, :, :, D:D + 1], 1.0)
            V.memset(loopw[:, D:D + 1], 0.0)
            V.memset(lbias[:, D:D + 1], 0.0)
            V.memset(tiny[:, :], 1.0e-37)
            V.tensor_copy(iob[:, :], iota[:, :])
            V.engine_nop().then_inc(const, 1)
            V.tensor_copy(nodes[:, :], iota[:, 0:R]).then_inc(dve, 1)
            v_.wait_ge(dve, 1)
            v_.wait_ge(const, 2)

            def rows_at(t, par):
                v_.wait_ge(win_in[par], (half(t, par) + 1) * 16)
                if not is_int(t) or t >= 2:
                    for part in range(2):
                        v_.wait_ge(g_in[par][part], half(t, par) * (16 * PARTS[part]))
                V.tensor_copy(rel[par][:, :], win[par].rearrange("p (j c) -> p j c", c=3)[:, :, 0]).then_inc(rel_ok, 1)

            def main(t, par, then):
                v_.wait_ge(win_in[par], (half(t, par) + 1) * 16)
                w3 = win[par].rearrange("p (j c) -> p j c", c=3)
                if not is_int(t) or t >= 2:
                    v_.wait_ge(agg, t - 1)
                V.tensor_tensor(A[:, par, :, :], nodes[:, :].unsqueeze(1).to_broadcast([128, COLS, R]),
                                w3[:, :, 1:2].to_broadcast([128, COLS, R]), ALU.is_equal).then_inc(hot_ok, 1)
                v_.wait_ge(hot_ok, t + 1)
                then(V.tensor_scalar_add(nodes[:, :], nodes[:, :], float(R)))

            def onehots(v, par, then):
                v_.wait_ge(ell_in[par], (half(v, par) + 1) * 16)
                wait(v_, codes_ok, v)
                then(V.tensor_scalar(off[:, :], iota[:, 0:SLOTS], deg[par][:, :], -512.0, ALU.is_ge, ALU.mult))
                slot = ell[par].rearrange("p (s c) -> p c s", c=2)
                for k in range(2):
                    last = V.tensor_tensor(codes[:, k, :, :], slot[:, k:k + 1, :].to_broadcast([128, 2, SLOTS]),
                                           off[:, :].unsqueeze(1).to_broadcast([128, 2, SLOTS]), ALU.add)
                then(last)
                V.tensor_scalar_add(codes[:, 1, 1, :], codes[:, 1, 1, :], float(T)).then_inc(codes_ok, 1)
                v_.wait_ge(codes_ps, v + 1)
                wait(v_, lh_ok, v)
                for q in range(2):
                    rows = slice(64 * q, 64 * (q + 1))
                    last = V.tensor_copy(codesT[rows, :, :], psK[rows, 0:256].rearrange("p (k q n) -> p k q n", k=2, q=2)[:, :, q, :])
                then(last)
                if not is_int(v) or v >= 1:
                    v_.wait_ge(c_ps, v * CH)
                V.tensor_tensor(L[:, :, :], iob[:, 0:R].unsqueeze(1).to_broadcast([128, PAIRS, R]),
                                codesT[:, 0, 0:PAIRS].unsqueeze(2).to_broadcast([128, PAIRS, R]), ALU.is_equal)
                V.tensor_tensor(H[:, :, :], iob[:, 0:2 * T].unsqueeze(1).to_broadcast([128, PAIRS, 2 * T]),
                                codesT[:, 1, 0:PAIRS].unsqueeze(2).to_broadcast([128, PAIRS, 2 * T]), ALU.is_equal).then_inc(lh_ok, 1)

            def sums(u, par, then):
                v_.wait_ge(agg, u + 1)
                if not is_int(u) or u >= 2:
                    v_.wait_ge(h_ps, u - 1)
                V.tensor_scalar_max(hrow[par][:, :], psA[par][0:R, 0:D], 0.0)
                wait(v_, eidx_ok, u)
                V.tensor_copy(start[:, :], starts[:, bass.ds(u, 1)])
                V.tensor_copy(deg[par][0:R, :], psA[par][0:R, D:D + 1]).then_inc(deg_ok, 1)
                v_.wait_ge(deg_ok, u + 1)
                v_.wait_ge(st_ok, u + 1)
                if not is_int(u) or u >= 2:
                    v_.wait_ge(ell_in[par], half(u, par) * 16)
                V.tensor_scalar(eidx[par][:, :], psS[:, 0:1], start[:, :], None, ALU.add).then_inc(eidx_ok, 1)

            def bias_rows(v, par, then):
                if not is_int(v) or v >= 2:
                    v_.wait_ge(out_ok[par], half(v, par) * 16)
                for j in range(CH):
                    n = v * CH + j
                    row = bias[par][0:R, CW * j:CW * j + cw[j]]
                    v_.wait_ge(ln_ok, n + 1)
                    V.tensor_scalar(row, psT[(par + j) % 2][0:R, 0:cw[j]], 0.0, NEG, ALU.is_equal, ALU.mult).then_inc(masked, 1)
                    v_.wait_ge(masked, n + 1)
                    V.tensor_tensor(row, row, lns[(par + j) % 2][:, 0:cw[j]], ALU.add).then_inc(bias_ok, 1)

            def moments(rows, which, par, to, eps, then):
                then(V.bn_stats(stats[which][:, :], rows))
                V.memset(spare2[:, :], 0.0).then_inc(then.sem, 1)
                then.done = then.done + 1
                then(V.bn_aggr(means[which][par][:, :], stats[which][:, :]))
                return V.tensor_scalar_add(to, means[which][par][:, 1:2], eps)

            def first(n, par, then):
                xs = x[:, bass.ds(n, 1), :].rearrange("p a f -> p (a f)")
                v_.wait_ge(y_ps, n + 1)
                V.tensor_tensor(ya[par][:, :], psK[0:R, 384:512], xs, ALU.add).then_inc(y_ok, 1)
                V.tensor_tensor(shifted[par][:, :], xs, shift[:, :], ALU.add)
                v_.wait_ge(y_ok, n + 1)
                return moments(ya[par][:, :], 0, par, roots[par][:, 0:1], 1.0e-8, then)

            def second(n, par, then):
                then(V.scalar_tensor_tensor(yb[par][:, :], ya[par][:, :], means[0][par][:, 0:1], gain[:, :], ALU.subtract, ALU.mult))
                then(V.scalar_tensor_tensor(yb[par][:, :], yb[par][:, :], roots[par][:, 0:1], shifted[par][:, :], ALU.mult, ALU.add))
                return moments(yb[par][:, :], 1, par, roots[1 - par][:, 1:2], 1.0e-5, then)

            def third(n, par):
                if not is_int(n) or n >= 2:
                    v_.wait_ge(x_ps, n - 1)
                    v_.wait_ge(kept[par], half(n, par) * 16)
                V.tensor_scalar(xnew[par][:, :], yb[par][:, :], means[1][par][:, 0:1], roots[1 - par][:, 1:2],
                                ALU.subtract, ALU.mult).then_inc(x_ok, 1)

            def step(t, par):
                count = Steps(v_, nrm, 5 * min(max(0, t - 3), T) + 3 * min(max(0, t - 2), T) if is_int(t) else 8 * t - 21)
                base = 1 + min(t, T) + 3 * max(0, t - 2) if is_int(t) else 4 * t - 5
                then = Steps(v_, dve, base)
                if inside(t - 2):
                    onehots(t - 2, par, then)
                if inside(t - 1):
                    sums(t - 1, 1 - par, then)
                if inside(t + 1):
                    rows_at(t + 1, 1 - par)
                if inside(t):
                    main(t, par, then)
                last = None
                if not is_int(t) or t >= 3:
                    v_.wait_ge(rooted, t - 2)
                if inside(t - 4):
                    third(t - 4, par)
                if inside(t - 3):
                    last = second(t - 3, 1 - par, count)
                if inside(t - 2):
                    bias_rows(t - 2, par, then)
                    last = first(t - 2, par, count)
                if last is not None:
                    last.then_inc(asked, 1)

            rows_at(0, 0)
            V.memset(bias[0][96:128, :], 0.0)
            V.memset(bias[1][96:128, :], 0.0)
            pipeline_loop(v_, step, AFTER)

        @block.tensor
        def _(pe):
            pe.wait_ge(const, 2)

            def step(t, par):
                v, u = t - 2, t - 1
                if inside(v):
                    pe.wait_ge(codes_ok, v + 1)
                    if not is_int(v) or v >= 1:
                        pe.wait_ge(y_ok, v)
                    for k in range(2):
                        for q in range(2):
                            last = nc.tensor.matmul(psK[:, 128 * k + 64 * q:128 * k + 64 * (q + 1)],
                                                    codes[:, k].rearrange("p q s -> p (q s)"),
                                                    eye[:, PAIRS * q:PAIRS * q + 64], start=True, stop=True)
                    last.then_inc(codes_ps, 1)
                if inside(u):
                    pe.wait_ge(xt_ok, u + 1)
                    if not is_int(u) or u >= 2:
                        pe.wait_ge(deg_ok, u - 1)
                    acc = psA[1 - par][0:R, 0:D + 1]
                    nc.tensor.matmul(acc, xt[1 - par][:, :], loopw[:, :], start=True, stop=False)
                    nc.tensor.matmul(acc, ones[0:1, 0:R], lbias[:, :], start=False, stop=False)
                    pe.wait_ge(hot_ok, u + 1)
                    for j in range(COLS):
                        if j in (0, PARTS[0]):
                            pe.wait_ge(scaled, u * 2 + (1 if j == 0 else 2))
                        last = nc.tensor.matmul(acc, A[:, 1 - par, j, :], G[:, 1 - par, j, :], start=False, stop=(j == COLS - 1))
                    last.then_inc(agg, 1)
                    pe.wait_ge(deg_ok, u + 1)
                    if not is_int(t) or t >= 5:
                        pe.wait_ge(x_t_ok, t - 4)
                    nc.tensor.matmul(psS[:, 0:1], tri[:, :], deg[1 - par][:, :], start=True, stop=True).then_inc(st_ok, 1)
                if inside(v):
                    pe.wait_ge(lh_ok, v + 1)
                    for j in range(CH):
                        if not is_int(v) or v * CH + j >= 2:
                            pe.wait_ge(c_ok, v * CH + j - 1)
                        for i in range(pairs[j]):
                            p = 10 * j + i
                            last = nc.tensor.matmul(psC[(par + j) % 2][0:R, 2 * T * i:2 * T * (i + 1)], L[:, p, :], H[:, p, :],
                                                    start=True, stop=True)
                        last.then_inc(c_ps, 1)
                if inside(v):
                    nc.tensor.transpose(psK[:, 256:256 + R], hrow[par][:, :], eye[0:R, 0:R]).then_inc(h_ps, 1)
                    pe.wait_ge(c_ok, v * CH + CH)
                    for j in range(CH):
                        if not is_int(v) or v * CH + j >= 2:
                            pe.wait_ge(ln_ok, v * CH + j - 1)
                            pe.wait_ge(masked, v * CH + j - 1)
                        for i in range(cw[j] // R):
                            last = nc.tensor.transpose(psT[(par + j) % 2][0:R, R * i:R * (i + 1)], CT[:, 4 * j + i, 0:R], eye[0:R, 0:R])
                        last.then_inc(t_ps, 1)
                if inside(v):
                    pe.wait_ge(h_ok, v + 1)
                    nc.tensor.matmul(psK[0:R, 384:512], ones[0:1, 0:R], ffnb[:, :], start=True, stop=False)
                    nc.tensor.matmul(psK[0:R, 384:512], hT[:, :], ffnT[:, :], start=False, stop=True).then_inc(y_ps, 1)
                if inside(t - 4):
                    pe.wait_ge(eidx_ok, min(t, T) if is_int(t) else t)
                    if not is_int(t) or t >= 5:
                        pe.wait_ge(x_t_ok, t - 4)
                    pe.wait_ge(x_ok, t - 3)
                    nc.tensor.transpose(psS[:, 128:128 + R], xnew[par][:, :], eye[0:R, 0:R]).then_inc(x_ps, 1)
            pipeline_loop(pe, step, AFTER)

        @block.scalar
        def _(act):
            def step(t, par):
                v, u, up = t - 2, t - 1, 1 - par
                if inside(u):
                    if not is_int(u) or u >= 2:
                        act.wait_ge(agg, u - 1)
                    nc.scalar.copy(xt[up][:, :], xT[:, bass.ds(u * R, R)]).then_inc(xt_ok, 1)
                    for part in range(2):
                        act.wait_ge(g_in[up][part], (half(u, up) + 1) * (16 * PARTS[part]))
                        for j in range(PARTS[0] * part, PARTS[0] + PARTS[1] * part):
                            last = nc.scalar.mul(G[:, up, j, 0:D], G[:, up, j, 0:D], win[up][:, 3 * j + 2:3 * j + 3])
                        last.then_inc(scaled, 1)
                if inside(v):
                    if not is_int(v) or v >= 1:
                        act.wait_ge(t_ps, v * CH)
                    for j in range(CH):
                        act.wait_ge(c_ps, v * CH + j + 1)
                        k = pairs[j]
                        for q in range(2):
                            src = psC[(par + j) % 2][0:R, 0:2 * T * k].rearrange("p (i q c) -> p i q c", i=k, q=2)[:, :, q, :]
                            dst = CT[:, :, PAIRS * q + 10 * j:PAIRS * q + 10 * j + k].rearrange("p c i -> p i c")
                            last = nc.scalar.copy(dst, src)
                        last.then_inc(c_ok, 1)
                    act.wait_ge(h_ps, v + 1)
                    if not is_int(v) or v >= 1:
                        act.wait_ge(y_ps, v)
                    nc.scalar.copy(hT[:, :], psK[:, 256:256 + R]).then_inc(h_ok, 1)
                    for j in range(CH):
                        n = v * CH + j
                        act.wait_ge(t_ps, n + 1)
                        if not is_int(v) or n >= 2:
                            act.wait_ge(bias_ok, n - 1)
                        nc.scalar.activation(lns[(par + j) % 2][:, 0:cw[j]], psT[(par + j) % 2][0:R, 0:cw[j]], ACT.Ln,
                                             bias=tiny[0:R, :]).then_inc(ln_ok, 1)
                if inside(t - 4):
                    act.wait_ge(x_ps, t - 3)
                    nc.scalar.copy(xT[:, bass.ds((t - 4) * R, R)], psS[:, 128:128 + R]).then_inc(x_t_ok, 1)
            act.wait_ge(const, 2)
            pipeline_loop(act, step, AFTER)


def message_any(nc, a, m):
    ctx = ExitStack()
    with ctx:
        def sb(name, shape, dt):
            return ctx.enter_context(nc.sbuf_tensor(f"{name}_any", shape, dt))

        def sem(name):
            return ctx.enter_context(nc.semaphore(f"{name}_any"))

        h, xT, ones, iota, ps = (m[k] for k in ("h", "xT", "ones", "iota", "ps"))
        edges = sb("edges", [128, BLOCKS, 3], F32)
        lohi = sb("lohi", [128, BLOCKS, 2], F32)
        srcs = sb("srcs", [128, BLOCKS, 1], F32)
        cur = sb("edge_now", [128, 4], F32)
        at = sb("rel_at", [128, 1], U32)
        G = sb("gathered", [128, D], F32)
        A = sb("dst_onehot", [128, R], F32)
        Ab = sb("dst_onehot_b", [128, R], BF16)
        B = sb("src_onehot", [128, NODES], BF16)
        every = sb("all_nodes", [128, NODES], F32)
        nodes = sb("tile_nodes", [128, R], F32)
        xt = sb("xT_tile", [128, R], F32)
        zero = sb("zero", [1, CW], F32)
        loopw, lbias = m["loop_w"][:, 0:D], m["loop_bias"][:, 0:D]
        lns = sb("ln", [R, NODES], F32)
        rows = sb("bias_rows", [128, NODES], F32)
        tiny = sb("tiny", [128, 1], F32)
        spare = sb("spare", [128, 1], F32)
        names = ("e_in", "iota_ok", "dve", "at_ok", "settled", "g_in", "stored", "m_in", "summed", "xt_ok", "ln_ok", "bias_out")
        z = {n: sem(n) for n in names}
        cw = widths()
        SUMS = BLOCKS + 2
        CHAIN = 4 * BLOCKS + 3
        block = ctx.enter_context(nc.Block())

        @block.sync
        def _(sp):
            n = 128 * BLOCKS
            sp.dma_start(edges[:, :, :], m["records"][0:n, :].rearrange("(p n) c -> p n c", p=128)).then_inc(z["e_in"], 16)
            sp.dma_start(lohi[:, :, :], m["sources"][0:n, :].rearrange("(p n) c -> p n c", p=128)).then_inc(z["e_in"], 16)
            with sp.Fori(0, BLOCKS) as b:
                sp.wait_ge(z["g_in"], (b + 1) * 16)
                sp.dma_start(m["messages"][bass.ds(b, 1), :, :].rearrange("a p f -> (a p) f"), G[:, :]).then_inc(z["stored"], 16)
            sp.wait_ge(z["stored"], 16 * (BLOCKS + 1))
            with sp.Fori(0, T) as t:
                with sp.Fori(0, BLOCKS) as b:
                    sp.wait_ge(z["summed"], t * SUMS + b + 1)
                    sp.dma_start(G[:, :], m["messages"][bass.ds(b, 1), :, :].rearrange("a p f -> (a p) f")).then_inc(z["m_in"], 16)
                sp.wait_ge(z["dve"], 1 + (t + 1) * CHAIN)
                sp.dma_start(m["bias"][bass.ds(t, 1), :, :].rearrange("a p n -> (a p) n"), rows[:, :]).then_inc(z["bias_out"], 16)
            sp.wait_ge(z["bias_out"], 16 * (T + 1))

        @block.gpsimd
        def _(pool):
            nc.gpsimd.iota(every[:, :], pattern=[[1, NODES]], base=0, channel_multiplier=0,
                           allow_small_or_imprecise_dtypes=True).then_inc(z["iota_ok"], 1)
            nc.gpsimd.memset(spare[:, :], 0.0).then_inc(z["settled"], 1)
            with pool.Fori(0, BLOCKS) as b:
                pool.wait_ge(z["at_ok"], b + 1)
                pool.wait_ge(z["settled"], b + 1)
                nc.gpsimd.tensor_tensor(spare[:, :], spare[:, :], spare[:, :], ALU.add).then_inc(z["settled"], 1)
                nc.gpsimd.indirect_dma_start(out=G[:, :], out_offset=None, in_=m["rel_table"],
                                             in_offset=bass.IndirectOffsetOnAxis(ap=at[:, :], axis=0)).then_inc(z["g_in"], 16)

        @block.scalar
        def _(act):
            with act.Fori(0, T) as t:
                act.wait_ge(z["dve"], 1 + t * CHAIN)
                nc.scalar.copy(xt[:, :], xT[:, bass.ds(t * R, R)]).then_inc(z["xt_ok"], 1)
                act.wait_ge(z["summed"], (t + 1) * SUMS)
                for j in range(CH):
                    last = nc.scalar.activation(lns[:, CW * j:CW * j + cw[j]], ps[j][0:R, 0:cw[j]], ACT.Ln, bias=tiny[0:R, :])
                last.then_inc(z["ln_ok"], 1)

        @block.tensor
        def _(pe):
            pe.wait_ge(z["e_in"], 32)
            with pe.Fori(0, T) as t:
                pe.wait_ge(z["dve"], 1 + t * CHAIN)
                pe.wait_ge(z["xt_ok"], t + 1)
                nc.tensor.matmul(ps[CH][0:R, 0:D], xt[:, :], loopw[:, :], start=True, stop=False)
                nc.tensor.matmul(ps[CH][0:R, 0:D], ones[0:1, 0:R], lbias[:, :], start=False, stop=False)
                for j in range(CH):
                    last = nc.tensor.matmul(ps[j][0:R, 0:cw[j]], zero[:, 0:R], zero[:, 0:cw[j]], start=True, stop=False)
                last.then_inc(z["summed"], 1)
                with pe.Fori(0, BLOCKS) as b:
                    pe.wait_ge(z["dve"], 1 + t * CHAIN + (b + 1) * 4)
                    nc.tensor.matmul(ps[CH][0:R, 0:D], A[:, :], G[:, :], start=False, stop=False)
                    for j in range(CH):
                        last = nc.tensor.matmul(ps[j][0:R, 0:cw[j]], Ab[:, :], B[:, CW * j:CW * j + cw[j]], start=False, stop=False)
                    last.then_inc(z["summed"], 1)
                nc.tensor.matmul(ps[CH][0:R, 0:D], zero[:, 0:R], zero[:, 0:D], start=False, stop=True)
                for j in range(CH):
                    last = nc.tensor.matmul(ps[j][0:R, 0:cw[j]], zero[:, 0:R], zero[:, 0:cw[j]], start=False, stop=True)
                last.then_inc(z["summed"], 1)

        @block.vector
        def _(v):
            V = nc.vector
            V.memset(tiny[:, :], 1.0e-37)
            V.memset(zero[:, :], 0.0)
            V.memset(rows[96:128, :], 0.0)
            V.tensor_copy(nodes[:, :], iota[:, 0:R])
            v.wait_ge(z["e_in"], 32)
            v.wait_ge(z["iota_ok"], 1)
            V.scalar_tensor_tensor(srcs[:, :, 0], lohi[:, :, 1], float(R), lohi[:, :, 0], ALU.mult, ALU.add).then_inc(z["dve"], 1)
            v.wait_ge(z["dve"], 1)
            V.engine_nop().then_inc(z["bias_out"], 16)
            V.engine_nop().then_inc(z["stored"], 16)
            with v.Fori(0, BLOCKS) as b:
                v.wait_ge(z["stored"], (b + 1) * 16)
                V.tensor_copy(at[:, :], edges[:, bass.ds(b, 1), 0:1].rearrange("p a c -> p (a c)")).then_inc(z["at_ok"], 1)
            with v.Fori(0, T) as t:
                with v.Fori(0, BLOCKS) as b:
                    then = Steps(v, z["dve"], 1 + t * CHAIN + b * 4)
                    v.wait_ge(z["summed"], t * SUMS + b + 1)
                    V.tensor_copy(cur[:, 0:3], edges[:, bass.ds(b, 1), :].rearrange("p a c -> p (a c)"))
                    then(V.tensor_copy(cur[:, 3:4], srcs[:, bass.ds(b, 1), :].rearrange("p a c -> p (a c)")))
                    V.tensor_scalar(B[:, :], every[:, :], cur[:, 3:4], None, ALU.is_equal)
                    then(V.tensor_scalar(A[:, :], nodes[:, :], cur[:, 1:2], None, ALU.is_equal))
                    then(V.tensor_copy(Ab[:, :], A[:, :]))
                    v.wait_ge(z["m_in"], (t * BLOCKS + b + 1) * 16)
                    then(V.tensor_scalar(G[:, :], G[:, :], cur[:, 2:3], None, ALU.mult))
                then = Steps(v, z["dve"], 1 + t * CHAIN + 4 * BLOCKS)
                v.wait_ge(z["summed"], (t + 1) * SUMS)
                v.wait_ge(z["ln_ok"], t + 1)
                v.wait_ge(z["bias_out"], 16 * (t + 1))
                V.tensor_scalar_max(h[:, bass.ds(t, 1), :].rearrange("p a f -> p (a f)"), ps[CH][0:R, 0:D], 0.0)
                for j in range(CH):
                    last = V.tensor_scalar(rows[0:R, CW * j:CW * j + cw[j]], ps[j][0:R, 0:cw[j]], 0.0, NEG, ALU.is_equal, ALU.mult)
                then(last)
                then(V.tensor_tensor(rows[0:R, :], rows[0:R, :], lns[:, :], ALU.add))
                then(V.tensor_scalar_add(nodes[:, :], nodes[:, :], float(R)))


def pipeline_loop(eng, step, after=2):
    for t in range(FIRST):
        step(t, t % 2)
    with eng.Fori(0, (T - FIRST) // 2) as k:
        step(k * 2 + FIRST, FIRST % 2)
        step(k * 2 + FIRST + 1, (FIRST + 1) % 2)
    for t in range(T, T + after):
        step(t, t % 2)


def first_norms(nc, a, m):
    ctx = ExitStack()
    with ctx:
        def sb(name, shape, dt):
            return ctx.enter_context(nc.sbuf_tensor(name, shape, dt))

        def sem(name):
            return ctx.enter_context(nc.semaphore(name))

        x, xT, h, eye, ones, ps = m["x"], m["xT"], m["h"], m["eye"], m["ones"], m["ps"]
        ffnT, ffnb, gain, shift = m["ffnT"], m["ffn_b"], m["ln_g"], m["ln_b"]
        hT = [sb(f"hT{i}", [D, 4 * R], F32) for i in range(2)]
        y = sb("y_rows", [R, T, D], F32)
        shifted = sb("x_shifted", [R, T, D], F32)
        stats = [sb(f"stats{i}", [R, T, 6], F32) for i in range(2)]
        mean = [sb(f"mean{i}", [R, T, 2], F32) for i in range(2)]
        rstd = [sb(f"rstd{i}", [R, T, 1], F32) for i in range(2)]
        half_power = sb("minus_half", [R, 4, 1], F32)
        dve, h_ps, h_ok, y_ps, y_ok, x_ok, t_ps, t_ok, asked, rooted, half_ok, shift_ok, kept = (
            sem("f_" + n) for n in ("dve", "h_ps", "h_ok", "y_ps", "y_ok", "x_ok", "t_ps", "t_ok", "asked", "rooted",
                                    "half_ok", "shift_ok", "kept"))
        groups = [(g, min(4, T - g)) for g in range(0, T, 4)]
        N = len(groups)
        stages = [(i, n - i) for n in range(N + 2) for i in range(3) if 0 <= n - i < N]
        powers = [s for s in stages if s[0] < 2]
        block = ctx.enter_context(nc.Block())

        @block.sync
        def _(sp):
            for n, (g, k) in enumerate(groups):
                sp.wait_ge(x_ok, n + 1)
                sp.dma_start(m["x1"].rearrange("(t p) f -> p t f", p=R)[:, g:g + k, :], x[:, g:g + k, :]).then_inc(kept, 16)
            sp.wait_ge(kept, 16 * N)

        @block.gpsimd
        def _(pool):
            nc.gpsimd.memset(half_power[:, :, :], -0.5).then_inc(half_ok, 1)
            pool.wait_ge(half_ok, 1)
            for i, (which, n) in enumerate(powers):
                g, k = groups[n]
                if which == 0:
                    nc.gpsimd.tensor_tensor(shifted[:, g:g + k, :], x[:, g:g + k, :],
                                            shift[:, :].unsqueeze(1).to_broadcast([R, k, D]), ALU.add).then_inc(shift_ok, 1)
                pool.wait_ge(asked, i + 1)
                r = rstd[which][:, g:g + k, :]
                nc.gpsimd.tensor_tensor(r, r, half_power[:, 0:k, :], ALU.pow).then_inc(rooted, 1)

        @block.tensor
        def _(pe):
            def turn_h(n):
                g, k = groups[n]
                if n >= 2:
                    pe.wait_ge(h_ok, n - 1)
                for i in range(k):
                    last = nc.tensor.transpose(ps[n % 2][:, i * R:(i + 1) * R], h[:, g + i, :], eye[0:R, 0:R])
                last.then_inc(h_ps, 1)

            def turn_x(n):
                g, k = groups[n]
                pe.wait_ge(x_ok, n + 1)
                if n >= 2:
                    pe.wait_ge(t_ok, n - 1)
                for i in range(k):
                    last = nc.tensor.transpose(ps[4 + n % 2][:, i * R:(i + 1) * R], x[:, g + i, :], eye[0:R, 0:R])
                last.then_inc(t_ps, 1)

            turn_h(0)
            for n, (g, k) in enumerate(groups):
                if n + 1 < N:
                    turn_h(n + 1)
                pe.wait_ge(h_ok, n + 1)
                if n >= 2:
                    pe.wait_ge(y_ok, n - 1)
                for i in range(k):
                    to = ps[2 + n % 2][0:R, i * D:(i + 1) * D]
                    nc.tensor.matmul(to, ones[0:1, 0:R], ffnb[:, :], start=True, stop=False)
                    last = nc.tensor.matmul(to, hT[n % 2][:, i * R:(i + 1) * R], ffnT[:, :], start=False, stop=True)
                last.then_inc(y_ps, 1)
                if n >= 4:
                    turn_x(n - 4)
            for n in range(N - 4, N):
                turn_x(n)

        @block.scalar
        def _(act):
            def turn(n):
                g, k = groups[n]
                act.wait_ge(t_ps, n + 1)
                nc.scalar.copy(xT[:, g * R:(g + k) * R], ps[4 + n % 2][:, 0:k * R]).then_inc(t_ok, 1)

            for n, (g, k) in enumerate(groups):
                act.wait_ge(h_ps, n + 1)
                if n >= 2:
                    act.wait_ge(y_ps, n - 1)
                nc.scalar.copy(hT[n % 2][:, 0:k * R], ps[n % 2][:, 0:k * R]).then_inc(h_ok, 1)
                if n >= 5:
                    turn(n - 5)
            for n in range(N - 5, N):
                turn(n)

        @block.vector
        def _(v):
            then = Steps(v, dve)
            V = nc.vector

            def moments(rows, which, n, eps):
                g, k = groups[n]
                for i in range(k):
                    last = V.bn_stats(stats[which][:, g + i, :], rows[:, g + i, :])
                then(last)
                for i in range(k):
                    last = V.bn_aggr(mean[which][:, g + i, :], stats[which][:, g + i, :])
                then(last)
                V.tensor_scalar_add(rstd[which][:, g:g + k, :], mean[which][:, g:g + k, 1:2], eps).then_inc(asked, 1)

            for stage, n in stages:
                g, k = groups[n]
                if stage > 0:
                    v.wait_ge(rooted, powers.index((stage - 1, n)) + 1)
                if stage == 0:
                    v.wait_ge(y_ps, n + 1)
                    V.tensor_tensor(y[:, g:g + k, :], ps[2 + n % 2][0:R, 0:k * D].rearrange("p (t f) -> p t f", f=D),
                                    x[:, g:g + k, :], ALU.add).then_inc(y_ok, 1)
                    v.wait_ge(y_ok, n + 1)
                    moments(y, 0, n, 1.0e-8)
                elif stage == 1:
                    v.wait_ge(shift_ok, n + 1)
                    for i in range(g, g + k):
                        last = V.scalar_tensor_tensor(y[:, i, :], y[:, i, :], mean[0][:, i, 0:1], gain[:, :], ALU.subtract, ALU.mult)
                    then(last)
                    for i in range(g, g + k):
                        last = V.scalar_tensor_tensor(y[:, i, :], y[:, i, :], rstd[0][:, i, :], shifted[:, i, :], ALU.mult, ALU.add)
                    then(last)
                    moments(y, 1, n, 1.0e-5)
                else:
                    for i in range(g, g + k):
                        last = V.tensor_scalar(x[:, i, :], y[:, i, :], mean[1][:, i, 0:1], rstd[1][:, i, :], ALU.subtract, ALU.mult)
                    last.then_inc(x_ok, 1)


def conv(nc, a, m, layer, out):
    ctx = ExitStack()
    with ctx:
        def sb(name, shape, dt):
            return ctx.enter_context(nc.sbuf_tensor(f"{name}_l{layer}", shape, dt))

        def sem(name):
            return ctx.enter_context(nc.semaphore(f"{name}_l{layer}"))

        eye, ones, ps = m["eye"], m["ones"], m["ps"]
        inT = m["xT"] if layer == 1 else m["hT"]
        W = {c: m[f"W{c}{layer}"] for c in "qvs"}
        Wk = m[f"Wk{layer}"]
        bq, bk, bv, bs = (m[f"b{c}{layer}"] for c in "qkvs")
        qT = sb("qT", [128, NODES + R], F32)
        kparts = sb("k_parts", [128, HEADS, 3, NODES], BF16)
        qparts = [sb(f"q_parts{i}", [128, HEADS, 2, R], BF16) for i in range(2)]
        q_now = sb("q_tile", [128, R], F32)
        spare3 = sb("spare3", [R, 1], F32)
        qhi, qsmall, qrest = sb("q_hi", [128, 1, R], BF16), sb("q_mid_lo", [128, 2, R], BF16), sb("q_rest", [128, R], F32)
        bq_scaled = sb("bq_scaled", [D, 1], F32)
        SCALE = float(HD) ** -0.5
        krest = [sb(f"k_rest{i}", [128, CW], F32) for i in range(2)]
        vals = sb("values", [R, T, HEADS, HD + 1], F32)
        x_now = [sb(f"in_tile{i}", [128, R], F32) for i in range(2)]
        bias = [sb(f"bias_rows{i}", [128, NODES], F32) for i in range(2)]
        S = [sb(f"scores{i}", [R, HEADS, NODES], F32) for i in range(2)]
        PT = [sb(f"weightsT{i}", [R, CW], F32) for i in range(4)]
        mx = [sb(f"chunk_max{i}", [R, HEADS, CH], F32) for i in range(2)]
        top = sb("top", [R, HEADS], F32)
        neg = [sb(f"neg_max{i}", [R, HEADS], F32) for i in range(2)]
        den = sb("sum", [R, HEADS, 1], F32)
        rows = [sb(f"rows{i}", [R, 1, D], F32) for i in range(2)]
        x_old = [sb(f"x_rows{i}", [R, 1, D], F32) for i in range(2)]
        skip = sb("skip", [R, D], F32)
        OT = [sb(f"sumsT{i}", [HD + 1, HEADS, R], F32) for i in range(2)]
        stats, mean, rstd = sb("stats", [R, 1, 6], F32), sb("mean", [R, 1, 2], F32), sb("rstd", [R, 1, 1], F32)
        half_power = sb("minus_half", [R, 1, 1], F32)
        spare, spare2 = sb("spare", [R, 1], F32), sb("spare2", [R, 1], F32)

        names = ("dve", "q_ps", "q_ok", "k_ok", "v_ps", "v_ok", "qk", "masked", "neg_ok", "exp_ok", "t_ps", "pa_ok",
                 "pv_ok", "pt", "rows_ok", "r_ps", "r_ok", "one", "fin_ok", "dve2", "asked",
                 "rooted", "carried", "ot_ok", "o_ps", "x_cur", "q_laid", "kk_ps", "khi_ok", "bq_ok",
                 "krest_ok", "kmid_ok", "pool")
        z = {n: sem(n) for n in names}
        b_in = [sem("b_in0"), sem("b_in1")]
        x_in = [sem("x_rows_in0"), sem("x_rows_in1")]
        out_ok = [sem("rows_out0"), sem("rows_out1")]
        groups = [(g, min(4, T - g)) for g in range(0, T, 4)]
        cw = widths()
        psS, psT, psO = ps[0:4], ps[4:6], ps[6:8]
        ON_V = (1, 5, 8, 11, 13)
        NT = HEADS * CH
        TURN = [((), ()), ((0,), (1,)), ((2,), (3,)), ((4,), (5,)), ((6,), (7, 8)), ((9,), (10, 11)), ((12,), (13,))]
        KU = CH * HEADS
        Q_STEPS = 6
        EXP_BEFORE = {3: 2, 6: 3}
        EXP_AT = 3
        on_v = [sum(c < i for c in ON_V) for i in range(NT + 1)]
        block = ctx.enter_context(nc.Block())

        def chunk_out(eng, u, i):
            if i in ON_V:
                wait(eng, z["pt"], u * len(ON_V) + (on_v[i] + 1))
            else:
                wait(eng, z["pa_ok"], u * (NT - len(ON_V)) + (i - on_v[i] + 1))

        @block.sync
        def _(sp):
            def step(t, par):
                if inside(t):
                    if not is_int(t) or t >= 2:
                        sp.wait_ge(z["masked"], (t - 1) * NT)
                    sp.dma_start(bias[par][:, :], m["bias"][bass.ds(t, 1), :, :].rearrange("a p n -> (a p) n")).then_inc(b_in[par], 16)
                if layer == 2 and inside(t - 1):
                    if not is_int(t) or t >= 3:
                        sp.wait_ge(z["asked"], t - 2)
                    sp.dma_start(x_old[1 - par][:, 0, :], m["x1"][bass.ds((t - 1) * R, R), :]).then_inc(x_in[1 - par], 16)
                if layer == 2 and inside(t - 3):
                    sp.wait_ge(z["rows_ok"], t - 2)
                    sp.dma_start(out[bass.ds((t - 3) * R, R), :], rows[1 - par][:, 0, :]).then_inc(out_ok[1 - par], 16)
            pipeline_loop(sp, step, 3)
            if layer == 2:
                sp.wait_ge(out_ok[0], 16 * ((T + 1) // 2))
                sp.wait_ge(out_ok[1], 16 * (T // 2))

        @block.gpsimd
        def _(pool):
            nc.gpsimd.memset(half_power[:, :, :], -0.5)
            nc.gpsimd.memset(vals[:, :, :, HD:HD + 1], 1.0).then_inc(z["one"], 1)
            pool.wait_ge(z["one"], 1)
            pool.wait_ge(z["q_ok"], CH)

            def split_q(t):
                pq = Steps(pool, z["pool"], t * Q_STEPS)
                if not is_int(t) or t >= 1:
                    pool.wait_ge(z["pool"], t * Q_STEPS)
                    pool.wait_ge(z["q_laid"], t)
                nc.gpsimd.tensor_tensor(spare3[:, :], half_power[:, 0, :], half_power[:, 0, :], ALU.mult).then_inc(z["pool"], 1)
                pq.done = pq.done + 1
                pq(nc.gpsimd.tensor_copy(q_now[:, :], qT[:, bass.ds(t * R, R)]))
                pq(nc.gpsimd.tensor_tensor(qhi[:, 0, :], q_now[:, :], ones[:, 0:R], ALU.mult))
                pq(nc.gpsimd.tensor_tensor(qrest[:, :], q_now[:, :], qhi[:, 0, :], ALU.subtract))
                pq(nc.gpsimd.tensor_tensor(qsmall[:, 0, :], qrest[:, :], ones[:, 0:R], ALU.mult))
                nc.gpsimd.tensor_tensor(qsmall[:, 1, :], qrest[:, :], qsmall[:, 0, :], ALU.subtract).then_inc(z["pool"], 1)

            split_q(0)

            def step(t, par):
                if inside(t + 1):
                    split_q(t + 1)
                if inside(t - 2):
                    if not is_int(t) or t >= 4:
                        pool.wait_ge(z["o_ps"], t - 3)
                    nc.gpsimd.tensor_copy(x_now[par][:, :], inT[:, bass.ds((t - 2) * R, R)]).then_inc(z["x_cur"], 1)
                if layer == 2 and inside(t - 2):
                    pool.wait_ge(z["asked"], t - 1)
                    nc.gpsimd.tensor_tensor(rstd[:, :, :], rstd[:, :, :], half_power[:, :, :], ALU.pow).then_inc(z["rooted"], 1)
            pipeline_loop(pool, step)

        @block.tensor
        def _(pe):
            for j in range(CH):
                if j >= 2:
                    pe.wait_ge(z["q_ok"], j - 1)
                    pe.wait_ge(z["krest_ok"], 2 * j - 2)
                nc.tensor.matmul(ps[j % 2][:, 0:cw[j]], W["q"][:, :], inT[:, CW * j:CW * j + cw[j]], start=True, stop=True).then_inc(z["q_ps"], 1)
                for hd in range(HEADS):
                    nc.tensor.matmul(ps[(2, 3, 6, 7)[(2 * j + hd) % 4]][:, 0:cw[j]], Wk[:, hd, :, :].rearrange("f i c -> f (i c)"),
                                     inT[:, CW * j:CW * j + cw[j]], start=True, stop=True).then_inc(z["kk_ps"], 1)
                g, k = groups[j]
                if j >= 2:
                    pe.wait_ge(z["v_ok"], j - 1)
                for i in range(k):
                    to = ps[4 + j % 2][0:R, i * D:(i + 1) * D]
                    nc.tensor.matmul(to, ones[0:1, 0:R], bv[:, :], start=True, stop=False)
                    last = nc.tensor.matmul(to, inT[:, (g + i) * R:(g + i + 1) * R], W["v"][:, :], start=False, stop=True)
                last.then_inc(z["v_ps"], 1)
            pe.wait_ge(z["q_ok"], CH)
            pe.wait_ge(z["k_ok"], KU)
            pe.wait_ge(z["v_ok"], len(groups))
            pe.wait_ge(z["one"], 1)

            def product(u, up, i):
                hd, c = i // CH, i % CH
                chunk_out(pe, u, i)
                to = psO[up][0:HD + 1, R * hd:R * (hd + 1)]
                for b in range(cw[c] // R):
                    last = nc.tensor.matmul(to, vals[:, 4 * c + b, hd, :], PT[(2 * up + i) % 4][:, b * R:(b + 1) * R],
                                            start=(c == 0 and b == 0), stop=(c == CH - 1 and b == 0))
                last.then_inc(z["pv_ok"], 1)

            def scores(t, par, j, hd):
                if j == 0 and hd == 0:
                    pe.wait_ge(z["q_laid"], t + 1)
                if not is_int(t) or t * CH + j >= 2:
                    pe.wait_ge(z["masked"], (t * CH + (j - 2)) * 2 + (hd + 1))
                for i, (q, k) in enumerate(((0, 0), (0, 1), (1, 2))):
                    last = nc.tensor.matmul(psS[2 * ((par + j) % 2) + hd][0:R, 0:cw[j]], qparts[par][:, hd, q, :],
                                            kparts[:, hd, k, CW * j:CW * j + cw[j]], start=(i == 0), stop=(i == 2))
                last.then_inc(z["qk"], 1)

            def step(t, par):
                u, up, w = t - 1, 1 - par, t - 2
                for j in range(CH):
                    for hd_s in range(HEADS):
                        if inside(t):
                            scores(t, par, j, hd_s)
                        if j == 0 and inside(w):
                            product(w, par, NT - 2 + hd_s)
                        if not inside(u):
                            continue
                        for i in TURN[j][hd_s]:
                            hd, c = i // CH, i % CH
                            if c in (0, EXP_AT):
                                pe.wait_ge(z["exp_ok"], u * 4 + (2 * hd + 1 + (c > 0)))
                            if i >= 2:
                                chunk_out(pe, u, i - 2)
                            elif not is_int(u) or u >= 1:
                                chunk_out(pe, u - 1, i - 2 + NT)
                            for b in range(cw[c] // R):
                                n = 4 * c + b
                                last = nc.tensor.transpose(psT[i % 2][0:R, b * R:(b + 1) * R], S[up][:, hd, n * R:(n + 1) * R],
                                                           eye[0:R, 0:R])
                            last.then_inc(z["t_ps"], 1)
                            if i == 2 and (not is_int(u) or u >= 2):
                                pe.wait_ge(z["fin_ok"], u - 1)
                            if i >= 2:
                                product(u, up, i - 2)
                    if j == 2 and inside(w):
                        pe.wait_ge(z["ot_ok"], w + 1)
                        pe.wait_ge(z["x_cur"], w + 1)
                        for hd in range(HEADS):
                            nc.tensor.transpose(psO[par][0:R, 256 + 128 * hd:256 + 128 * hd + HD + 1], OT[par][:, hd, :],
                                                       eye[0:HD + 1, 0:HD + 1])
                        nc.tensor.matmul(psO[par][0:R, 0:D], x_now[par][:, :], W["s"][:, :], start=True, stop=True).then_inc(z["o_ps"], 1)
                    if layer == 1 and j == 5 and inside(w):
                        pe.wait_ge(z["rows_ok"], w + 1)
                        nc.tensor.transpose(psO[par][:, 128:128 + R], rows[par][:, 0, :], eye[0:R, 0:R]).then_inc(z["r_ps"], 1)
            pipeline_loop(pe, step)

        @block.scalar
        def _(act):
            def k_mid(n):
                j, hd = n // 2, n % 2
                act.wait_ge(z["krest_ok"], n + 1)
                nc.scalar.copy(kparts[:, hd, 1, CW * j:CW * j + cw[j]], krest[n % 2][:, 0:cw[j]]).then_inc(z["kmid_ok"], 1)

            act.wait_ge(z["bq_ok"], 1)
            for n in range(KU):
                j, hd = n // 2, n % 2
                act.wait_ge(z["kk_ps"], n + 1)
                nc.scalar.activation(kparts[:, hd, 0, CW * j:CW * j + cw[j]], ps[(2, 3, 6, 7)[n % 4]][:, 0:cw[j]], ACT.Identity,
                                     bias=bk[:, hd:hd + 1]).then_inc(z["khi_ok"], 1)
                if n >= 1:
                    k_mid(n - 1)
                if hd == 1:
                    g, k = groups[j]
                    act.wait_ge(z["q_ps"], j + 1)
                    nc.scalar.activation(qT[:, CW * j:CW * j + cw[j]], ps[j % 2][:, 0:cw[j]], ACT.Identity, scale=SCALE,
                                         bias=bq_scaled[:, :]).then_inc(z["q_ok"], 1)
                    act.wait_ge(z["v_ps"], j + 1)
                    nc.scalar.copy(vals[:, g:g + k, :, 0:HD], ps[4 + j % 2][0:R, 0:k * D].rearrange("p (t h f) -> p t h f", h=HEADS, f=HD)).then_inc(z["v_ok"], 1)
            k_mid(KU - 1)

            def lay_q(t, par):
                act.wait_ge(z["pool"], (t + 1) * Q_STEPS)
                if not is_int(t) or t >= 2:
                    act.wait_ge(z["qk"], (t - 1) * NT)
                for hd in range(HEADS):
                    own, other = slice(HD * hd, HD * (hd + 1)), slice(HD * (1 - hd), HD * (2 - hd))
                    nc.scalar.copy(qparts[par][own, hd, :, :], qhi[own, :, :].to_broadcast([HD, 2, R]))
                    last = nc.scalar.copy(qparts[par][other, hd, :, :], qsmall[own, :, :])
                last.then_inc(z["q_laid"], 1)

            def sums_out(w, par):
                act.wait_ge(z["pv_ok"], (w + 1) * NT)
                if not is_int(w) or w >= 2:
                    act.wait_ge(z["o_ps"], w - 1)
                nc.scalar.copy(OT[par][:, :, :], psO[par][0:HD + 1, 0:2 * R].rearrange("p (h n) -> p h n", h=HEADS)).then_inc(z["ot_ok"], 1)

            def step(t, par):
                u, up, w = t - 1, 1 - par, t - 2
                def exps(n):
                    hd, (lo, hi) = n // 2, ((0, CW * EXP_AT), (CW * EXP_AT, NODES))[n % 2]
                    part = S[up][:, hd, lo:hi]
                    nc.scalar.activation(part, part, ACT.Exp, bias=neg[up][:, hd:hd + 1]).then_inc(z["exp_ok"], 1)

                if inside(u):
                    act.wait_ge(z["neg_ok"], u + 1)
                    exps(0)
                    exps(1)
                if inside(w):
                    sums_out(w, par)
                if inside(u):
                    for i in range(NT):
                        if i in EXP_BEFORE:
                            exps(EXP_BEFORE[i])
                        if i in ON_V:
                            continue
                        c = i % CH
                        act.wait_ge(z["t_ps"], u * NT + (i + 1))
                        if i >= 4 or not is_int(u) or u >= 1:
                            act.wait_ge(z["pv_ok"], u * NT + (i - 3))
                        nc.scalar.copy(PT[(2 * up + i) % 4][:, 0:cw[c]], psT[i % 2][0:R, 0:cw[c]]).then_inc(z["pa_ok"], 1)
                        if i == 9:
                            if inside(t + 1):
                                lay_q(t + 1, 1 - par)
                        if layer == 1 and i == 12 and inside(w):
                            turned(w, par)
                elif layer == 1 and inside(w):
                    turned(w, par)
                if is_int(t) and t == 0:
                    lay_q(1, 1)

            def turned(w, par):
                act.wait_ge(z["r_ps"], w + 1)
                nc.scalar.copy(m["hT"][:, bass.ds(w * R, R)], psO[par][:, 128:128 + R]).then_inc(z["r_ok"], 1)
            lay_q(0, 0)
            pipeline_loop(act, step)

        @block.vector
        def _(v):
            V = nc.vector
            V.memset(qT[:, NODES:NODES + R], 0.0)
            V.tensor_scalar_mul(bq_scaled[:, :], bq[:, :], SCALE).then_inc(z["bq_ok"], 1)
            def k_low(n):
                j, hd = n // 2, n % 2
                own, other = slice(HD * hd, HD * (hd + 1)), slice(HD * (1 - hd), HD * (2 - hd))
                at = slice(CW * j, CW * j + cw[j])
                V.tensor_copy(kparts[other, hd, 2, at], kparts[other, hd, 0, at])
                v.wait_ge(z["kmid_ok"], n + 1)
                V.tensor_tensor(kparts[own, hd, 2, at], krest[n % 2][own, 0:cw[j]], kparts[own, hd, 1, at], ALU.subtract).then_inc(z["k_ok"], 1)

            for n in range(KU):
                j, hd = n // 2, n % 2
                v.wait_ge(z["khi_ok"], n + 1)
                if n >= 2:
                    v.wait_ge(z["k_ok"], n - 1)
                V.scalar_tensor_tensor(krest[n % 2][:, 0:cw[j]], ps[(2, 3, 6, 7)[n % 4]][:, 0:cw[j]], bk[:, hd:hd + 1],
                                       kparts[:, hd, 0, CW * j:CW * j + cw[j]], ALU.add, ALU.subtract).then_inc(z["krest_ok"], 1)
                if n >= 1:
                    k_low(n - 1)
            k_low(KU - 1)

            def finish(w, par, then):
                v.wait_ge(z["o_ps"], w + 1)
                O = psO[par][0:R, 256:512].rearrange("p (h f) -> p h f", h=HEADS)
                then(V.tensor_scalar_max(den[:, :, :], O[:, :, HD:HD + 1], 1.0e-30))
                V.tensor_tensor(skip[:, :], psO[par][0:R, 0:D], bs[:, :], ALU.add)
                then(V.reciprocal(den[:, :, :], den[:, :, :]))
                if layer == 2 and (not is_int(w) or w >= 2):
                    v.wait_ge(out_ok[par], half(w, par) * 16)
                for hd in range(HEADS):
                    last = V.scalar_tensor_tensor(rows[par][:, 0, HD * hd:HD * (hd + 1)], O[:, hd, 0:HD], den[:, hd, :],
                                                  skip[:, HD * hd:HD * (hd + 1)], ALU.mult, ALU.add)
                last.then_inc(z["fin_ok"], 1)
                v.wait_ge(z["fin_ok"], w + 1)
                r = rows[par]
                if layer == 1:
                    V.tensor_scalar_max(r[:, :, :], r[:, :, :], 0.0).then_inc(z["rows_ok"], 1)
                else:
                    v.wait_ge(x_in[par], (half(w, par) + 1) * 16)
                    then(V.tensor_tensor(r[:, :, :], r[:, :, :], x_old[par][:, :, :], ALU.add))
                    then(V.bn_stats(stats[:, 0, :], r[:, 0, :]))
                    V.memset(spare2[:, :], 0.0).then_inc(then.sem, 1)
                    then.done = then.done + 1
                    then(V.bn_aggr(mean[:, 0, :], stats[:, 0, :]))
                    V.tensor_scalar_add(rstd[:, :, :], mean[:, :, 1:2], 1.0e-5).then_inc(z["asked"], 1)

            def normalize(w, par):
                v.wait_ge(z["rooted"], w + 1)
                r = rows[par][:, 0, :]
                V.tensor_scalar(r, r, mean[:, 0, 0:1], rstd[:, 0, :], ALU.subtract, ALU.mult).then_inc(z["rows_ok"], 1)

            CHAIN = 2 if layer == 1 else 6

            def step(t, par):
                u, up, w = t - 1, 1 - par, t - 2
                then = Steps(v, z["dve"], w * CHAIN if not is_int(w) else CHAIN * max(0, w))
                if inside(t):
                    v.wait_ge(b_in[par], (half(t, par) + 1) * 16)
                    if not is_int(t) or t >= 2:
                        v.wait_ge(z["t_ps"], (t - 1) * NT)
                        v.wait_ge(z["neg_ok"], t - 1)
                for j in range(CH):
                    if inside(t):
                        v.wait_ge(z["carried"], t * CH + j) if not is_int(t) or t * CH + j > 0 else None
                        v.wait_ge(z["qk"], (t * CH + (j + 1)) * 2)
                        V.memset(spare[:, :], 0.0).then_inc(z["carried"], 1)
                        for hd in range(HEADS):
                            lo, hi = CW * j, CW * j + cw[j]
                            V.tensor_tensor_reduce(S[par][:, hd, lo:hi], psS[2 * ((par + j) % 2) + hd][0:R, 0:cw[j]],
                                                   bias[par][0:R, lo:hi], 1.0, FLOOR, ALU.add, ALU.max,
                                                   mx[par][:, hd, j:j + 1]).then_inc(z["masked"], 1)
                    if inside(u):
                        for i in TURN[j][0] + TURN[j][1]:
                            if i in ON_V:
                                c = i % CH
                                v.wait_ge(z["t_ps"], u * NT + (i + 1))
                                if i >= 4 or not is_int(u) or u >= 1:
                                    v.wait_ge(z["pv_ok"], u * NT + (i - 3))
                                V.tensor_copy(PT[(2 * up + i) % 4][:, 0:cw[c]], psT[i % 2][0:R, 0:cw[c]]).then_inc(z["pt"], 1)
                    if j == 3 and inside(w):
                        finish(w, par, then)
                    if layer == 2 and j == 5 and inside(w):
                        normalize(w, par)
                if inside(t):
                    v.wait_ge(z["masked"], (t + 1) * NT)
                    wait(v, z["neg_ok"], t)
                    V.tensor_reduce(top[:, :], mx[par][:, :, :], AX.X, ALU.max).then_inc(z["dve2"], 1)
                    v.wait_ge(z["dve2"], t + 1)
                    if not is_int(t) or t >= 2:
                        v.wait_ge(z["exp_ok"], (t - 1) * 4)
                    V.tensor_scalar_mul(neg[par][:, :], top[:, :], -1.0).then_inc(z["neg_ok"], 1)
            pipeline_loop(v, step)


INPUTS = ['x', 'src', 'dst', 'edge_type_8', 'edge_weight', 'L0_gnn_V', 'L0_gnn_w_comp', 'L0_gnn_loop_w', 'L0_gnn_bias',
          'L0_gnn_ffn_w', 'L0_gnn_ffn_b', 'L0_gnn_ln_g', 'L0_gnn_ln_b'] + [
              f'L1_gnn_{w}{k}{l}' for l in (1, 2) for k in 'qkvs' for w in 'Wb']


def kernel(**inputs):
    import numpy as np
    import concourse.bacc as bacc
    from concourse.bass_utils import run_bass_kernel_spmd

    nc = bacc.Bacc("TRN2", target_bir_lowering=False, num_devices=1)
    arrays, args = {}, {}
    for name in INPUTS:
        value = np.ascontiguousarray(inputs[name])
        arrays[f"in_{name}"] = value
        args[name] = nc.dram_tensor(f"in_{name}", value.shape, mybir.dt.from_np(value.dtype), kind="ExternalInput").ap()
    out = nc.dram_tensor("out", (NODES, D), F32, kind="ExternalOutput").ap()
    build(nc, args, out)
    return run_bass_kernel_spmd(nc, [arrays], core_ids=[0]).results[0]["out"]
```
